# Optimizing a Trainium2 kernel written in Bass

```python
import numpy as np
import jax
import jax.numpy as jnp

def _softmax(x, axis=-1):
    return jax.nn.softmax(x, axis=axis)

def _gelu(x):
    return jax.nn.gelu(x, approximate=True)

def _silu(x):
    return jax.nn.silu(x)

def _sigmoid(x):
    return jax.nn.sigmoid(x)

def _layernorm(x, axis=-1, eps=1e-05):
    m = jnp.mean(x, axis=axis, keepdims=True)
    v = jnp.var(x, axis=axis, keepdims=True)
    return (x - m) / jnp.sqrt(v + eps)

def _scatter_add(tgt, idx, src, axis=0):
    return tgt.at[idx].add(src)

def _segment_sum(src, seg, n):
    return jax.ops.segment_sum(src, seg, n)
kernel_name = 'mk_xattn_ffn_d2_seqx_r8_ca864a'

def setup_inputs(seed: int=0):
    np.random.seed(seed)
    _w = jnp.asarray

    def _rec_inputs():
        import jax
        import jax.numpy as jnp
        _rk = jax.random.key(seed)
        x = -0.0005207 + 1.001 * jax.random.normal(jax.random.fold_in(_rk, 1), (64, 64, 128), jnp.float32)
        _lenS = 64 - jax.random.randint(jax.random.fold_in(_rk, 7), (64,), 0, max(1, 64 // 4) + 1, jnp.int32)
        _lenS2 = 64 - jax.random.randint(jax.random.fold_in(_rk, 8), (64,), 0, max(1, 64 // 4) + 1, jnp.int32)
        _ctx_1024P = jax.random.normal(jax.random.fold_in(_rk, 11), (64, 16, 128), jnp.float32)
        _ctx_1024c = jax.random.dirichlet(jax.random.fold_in(_rk, 511), 0.3 * jnp.ones((16,), jnp.float32), (64, 64))
        _ctx_1024t = jnp.einsum('bsk,bkd->bsd', _ctx_1024c, _ctx_1024P)
        _ctx_1024t = _ctx_1024t * jax.lax.rsqrt(jnp.mean(jnp.square(_ctx_1024t)) + 1e-12) * 0.953939
        ctx_1024 = -0.000514642 + 1.00011 * (_ctx_1024t + 0.3 * jax.random.normal(jax.random.fold_in(_rk, 611), (64, 64, 128), jnp.float32))
        return (x, ctx_1024)
    x, ctx_1024 = _rec_inputs()

    def _L0_xattn_setup():
        import jax, jax.numpy as jnp
        import numpy as np
        B, S, E, NH = (1, 256, 128, 8)
        DH = E // NH
        EPS = 1e-06
        LN_EPS = 1e-05
        key = jax.random.key(seed)
        ks = jax.random.split(key, 8)
        q = jax.random.normal(ks[0], (B, S, E), dtype=jnp.float32)
        k = jax.random.normal(ks[1], (B, S, E), dtype=jnp.float32)
        v = jax.random.normal(ks[2], (B, S, E), dtype=jnp.float32)
        scale = 1.0 / np.sqrt(3 * E)
        igate_w = jax.random.normal(ks[3], (NH, 3 * E), dtype=jnp.float32) * scale
        igate_b = jax.random.normal(ks[4], (NH,), dtype=jnp.float32) * 0.1
        fgate_w = jax.random.normal(ks[5], (NH, 3 * E), dtype=jnp.float32) * scale
        fgate_b = jnp.linspace(3.0, 6.0, NH, dtype=jnp.float32)
        out_w = 1.0 + 0.1 * jax.random.normal(ks[6], (E,), dtype=jnp.float32)
        return {'q': q, 'k': k, 'v': v, 'igate_w': igate_w, 'igate_b': igate_b, 'fgate_w': fgate_w, 'fgate_b': fgate_b, 'out_w': out_w}
    _L0_xattn_all = _L0_xattn_setup()
    _L0_xattn_in = {k: v for k, v in _L0_xattn_all.items() if k in ('igate_w', 'igate_b', 'fgate_w', 'fgate_b', 'out_w')}
    del _L0_xattn_all

    def _L0_ffn_setup():
        import jax, jax.numpy as jnp
        import numpy as np
        B, S, H = (2, 256, 128)
        N, F, SF, K = (16, 128, 512, 1)
        key = jax.random.key(seed)
        ks = jax.random.split(key, 7)
        std = 0.02
        return {'hidden_states': jax.random.normal(ks[0], (B, S, H), dtype=jnp.float32), 'router_w': jax.random.normal(ks[1], (N, H), dtype=jnp.float32) * std, 'gate_up_proj': jax.random.normal(ks[2], (N, H, 2 * F), dtype=jnp.float32) * std, 'down_proj': jax.random.normal(ks[3], (N, F, H), dtype=jnp.float32) * std, 'shared_gate_w': jax.random.normal(ks[4], (SF, H), dtype=jnp.float32) * std, 'shared_up_w': jax.random.normal(ks[5], (SF, H), dtype=jnp.float32) * std, 'shared_down_w': jax.random.normal(ks[6], (H, SF), dtype=jnp.float32) * std}
    _L0_ffn_all = _L0_ffn_setup()
    _L0_ffn_in = {k: v for k, v in _L0_ffn_all.items() if k in ('router_w', 'gate_up_proj', 'down_proj', 'shared_gate_w', 'shared_up_w', 'shared_down_w')}
    del _L0_ffn_all

    def _L1_xattn_setup():
        import jax, jax.numpy as jnp
        import numpy as np
        B, T, N = (128, 32, 196)
        E = 128
        FD = 128
        H = 128
        A = 128
        SCALE = 0.02

        def _lstm_cell(x, h, c, W_ih, W_hh, b_ih, b_hh):
            gates = x @ W_ih.T + h @ W_hh.T + (b_ih + b_hh)
            i, f, g, o = jnp.split(gates, 4, axis=-1)
            c_new = jax.nn.sigmoid(f) * c + jax.nn.sigmoid(i) * jnp.tanh(g)
            h_new = jax.nn.sigmoid(o) * jnp.tanh(c_new)
            return (h_new, c_new)
        key = jax.random.key(seed)
        ks = jax.random.split(key, 16)
        g = lambda k, shape: jax.random.normal(k, shape, dtype=jnp.float32) * SCALE
        return {'feats': jax.random.normal(ks[0], (B, N, FD), dtype=jnp.float32), 'embeddings': jax.random.normal(ks[1], (B, T, E), dtype=jnp.float32), 'Wf': g(ks[2], (FD, A)), 'Wh': g(ks[3], (H, A)), 'b_att': jnp.zeros((A,), dtype=jnp.float32), 'v': g(ks[4], (A,)), 'W_ih0': g(ks[5], (4 * H, E + FD)), 'W_hh0': g(ks[6], (4 * H, H)), 'b_ih0': jnp.zeros((4 * H,), dtype=jnp.float32), 'b_hh0': jnp.zeros((4 * H,), dtype=jnp.float32), 'W_ih1': g(ks[7], (4 * H, H)), 'W_hh1': g(ks[8], (4 * H, H)), 'b_ih1': jnp.zeros((4 * H,), dtype=jnp.float32), 'b_hh1': jnp.zeros((4 * H,), dtype=jnp.float32)}
    _L1_xattn_all = _L1_xattn_setup()
    _L1_xattn_in = {k: v for k, v in _L1_xattn_all.items() if k in ('Wf', 'Wh', 'b_att', 'v', 'W_ih0', 'W_hh0', 'b_ih0', 'b_hh0', 'W_ih1', 'W_hh1', 'b_ih1', 'b_hh1')}
    del _L1_xattn_all

    def _L1_ffn_setup():
        import jax, jax.numpy as jnp
        import numpy as np
        D_MODEL = 128
        N_HEADS = 16
        HEAD_DIM = D_MODEL // N_HEADS
        FFN_DIM = 512
        N_EXPERTS = 8
        TOP_K = 2
        BATCH = 4
        SEQ = 128

        def _layernorm(x, w, b, eps=1e-05):
            mu = jnp.mean(x, axis=-1, keepdims=True)
            var = jnp.mean(jnp.square(x - mu), axis=-1, keepdims=True)
            return (x - mu) * jax.lax.rsqrt(var + eps) * w + b

        def _causal_attention(nx, Wqkv, bqkv, Wo, bo):
            B, S, D = nx.shape
            qkv = nx @ Wqkv + bqkv
            q, k, v = jnp.split(qkv, 3, axis=-1)
            q = q.reshape(B, S, N_HEADS, HEAD_DIM)
            k = k.reshape(B, S, N_HEADS, HEAD_DIM)
            v = v.reshape(B, S, N_HEADS, HEAD_DIM)
            scores = jnp.einsum('bqhd,bkhd->bhqk', q, k) / jnp.sqrt(jnp.float32(HEAD_DIM))
            causal = jnp.tril(jnp.ones((S, S), bool))
            scores = jnp.where(causal, scores, jnp.finfo(scores.dtype).min)
            attn = jax.nn.softmax(scores, axis=-1)
            out = jnp.einsum('bhqk,bkhd->bqhd', attn, v).reshape(B, S, D)
            return out @ Wo + bo

        def _moe_ffn(nx, gate_W, fc1_w, fc1_b, fc2_w, fc2_b):
            gate_logits = nx @ gate_W
            topk_vals, topk_idx = jax.lax.top_k(gate_logits, TOP_K)
            gate_w = jax.nn.softmax(topk_vals, axis=-1)
            dense_gates = jnp.sum(jax.nn.one_hot(topk_idx, N_EXPERTS, dtype=nx.dtype) * gate_w[..., None], axis=-2)
            moe_out = jnp.zeros_like(nx)
            for e in range(N_EXPERTS):
                h = jax.nn.gelu(jnp.einsum('bsd,fd->bsf', nx, fc1_w[e]) + fc1_b[e], approximate=False)
                y = jnp.einsum('bsf,df->bsd', h, fc2_w[e]) + fc2_b[e]
                moe_out = moe_out + y * dense_gates[..., e:e + 1]
            return moe_out
        key = jax.random.key(seed)
        ks = jax.random.split(key, 12)
        s = lambda k, shape, scale: jax.random.normal(k, shape, dtype=jnp.float32) * scale
        inp = {'x': s(ks[0], (BATCH, SEQ, D_MODEL), 1.0), 'ln1_w': jnp.ones((D_MODEL,), jnp.float32), 'ln1_b': jnp.zeros((D_MODEL,), jnp.float32), 'ln2_w': jnp.ones((D_MODEL,), jnp.float32), 'ln2_b': jnp.zeros((D_MODEL,), jnp.float32), 'Wqkv': s(ks[1], (D_MODEL, 3 * D_MODEL), 0.02), 'bqkv': jnp.zeros((3 * D_MODEL,), jnp.float32), 'Wo': s(ks[2], (D_MODEL, D_MODEL), 0.02), 'bo': jnp.zeros((D_MODEL,), jnp.float32), 'gate_W': s(ks[3], (D_MODEL, N_EXPERTS), 0.02), 'fc1_w': s(ks[4], (N_EXPERTS, FFN_DIM, D_MODEL), (2.0 / D_MODEL) ** 0.5), 'fc1_b': jnp.zeros((N_EXPERTS, FFN_DIM), jnp.float32), 'fc2_w': s(ks[5], (N_EXPERTS, D_MODEL, FFN_DIM), (1.0 / FFN_DIM) ** 0.5), 'fc2_b': jnp.zeros((N_EXPERTS, D_MODEL), jnp.float32)}
        return inp
    _L1_ffn_all = _L1_ffn_setup()
    _L1_ffn_in = {k: v for k, v in _L1_ffn_all.items() if k in ('ln1_w', 'ln1_b', 'ln2_w', 'ln2_b', 'Wqkv', 'bqkv', 'Wo', 'bo', 'gate_W', 'fc1_w', 'fc1_b', 'fc2_w', 'fc2_b')}
    del _L1_ffn_all
    return {'x': x, 'ctx_1024': ctx_1024, 'L0_xattn_igate_w': _L0_xattn_in['igate_w'], 'L0_xattn_igate_b': _L0_xattn_in['igate_b'], 'L0_xattn_fgate_w': _L0_xattn_in['fgate_w'], 'L0_xattn_fgate_b': _L0_xattn_in['fgate_b'], 'L0_xattn_out_w': _L0_xattn_in['out_w'], 'L0_ffn_router_w': _L0_ffn_in['router_w'], 'L0_ffn_gate_up_proj': _L0_ffn_in['gate_up_proj'], 'L0_ffn_down_proj': _L0_ffn_in['down_proj'], 'L0_ffn_shared_gate_w': _L0_ffn_in['shared_gate_w'], 'L0_ffn_shared_up_w': _L0_ffn_in['shared_up_w'], 'L0_ffn_shared_down_w': _L0_ffn_in['shared_down_w'], 'L1_xattn_Wf': _L1_xattn_in['Wf'], 'L1_xattn_Wh': _L1_xattn_in['Wh'], 'L1_xattn_b_att': _L1_xattn_in['b_att'], 'L1_xattn_v': _L1_xattn_in['v'], 'L1_xattn_W_ih0': _L1_xattn_in['W_ih0'], 'L1_xattn_W_hh0': _L1_xattn_in['W_hh0'], 'L1_xattn_b_ih0': _L1_xattn_in['b_ih0'], 'L1_xattn_b_hh0': _L1_xattn_in['b_hh0'], 'L1_xattn_W_ih1': _L1_xattn_in['W_ih1'], 'L1_xattn_W_hh1': _L1_xattn_in['W_hh1'], 'L1_xattn_b_ih1': _L1_xattn_in['b_ih1'], 'L1_xattn_b_hh1': _L1_xattn_in['b_hh1'], 'L1_ffn_ln1_w': _L1_ffn_in['ln1_w'], 'L1_ffn_ln1_b': _L1_ffn_in['ln1_b'], 'L1_ffn_ln2_w': _L1_ffn_in['ln2_w'], 'L1_ffn_ln2_b': _L1_ffn_in['ln2_b'], 'L1_ffn_Wqkv': _L1_ffn_in['Wqkv'], 'L1_ffn_bqkv': _L1_ffn_in['bqkv'], 'L1_ffn_Wo': _L1_ffn_in['Wo'], 'L1_ffn_bo': _L1_ffn_in['bo'], 'L1_ffn_gate_W': _L1_ffn_in['gate_W'], 'L1_ffn_fc1_w': _L1_ffn_in['fc1_w'], 'L1_ffn_fc1_b': _L1_ffn_in['fc1_b'], 'L1_ffn_fc2_w': _L1_ffn_in['fc2_w'], 'L1_ffn_fc2_b': _L1_ffn_in['fc2_b']}

def reference(x, ctx_1024, L0_xattn_igate_w, L0_xattn_igate_b, L0_xattn_fgate_w, L0_xattn_fgate_b, L0_xattn_out_w, L0_ffn_router_w, L0_ffn_gate_up_proj, L0_ffn_down_proj, L0_ffn_shared_gate_w, L0_ffn_shared_up_w, L0_ffn_shared_down_w, L1_xattn_Wf, L1_xattn_Wh, L1_xattn_b_att, L1_xattn_v, L1_xattn_W_ih0, L1_xattn_W_hh0, L1_xattn_b_ih0, L1_xattn_b_hh0, L1_xattn_W_ih1, L1_xattn_W_hh1, L1_xattn_b_ih1, L1_xattn_b_hh1, L1_ffn_ln1_w, L1_ffn_ln1_b, L1_ffn_ln2_w, L1_ffn_ln2_b, L1_ffn_Wqkv, L1_ffn_bqkv, L1_ffn_Wo, L1_ffn_bo, L1_ffn_gate_W, L1_ffn_fc1_w, L1_ffn_fc1_b, L1_ffn_fc2_w, L1_ffn_fc2_b):
    import jax
    import jax.numpy as jnp

    def _L0_xattn_ref(q, k, v, igate_w, igate_b, fgate_w, fgate_b, out_w):
        import jax, jax.numpy as jnp
        import numpy as np
        B, S, E, NH = (1, 256, 128, 8)
        DH = E // NH
        EPS = 1e-06
        LN_EPS = 1e-05
        Bq, Sq, Eq = q.shape
        nh = igate_b.shape[0]
        dh = Eq // nh
        gi = jnp.concatenate([q, k, v], axis=-1)
        ig = (gi @ igate_w.T + igate_b).transpose(0, 2, 1)
        fg = (gi @ fgate_w.T + fgate_b).transpose(0, 2, 1)
        qh = q.reshape(Bq, Sq, nh, dh).transpose(0, 2, 1, 3)
        kh = k.reshape(Bq, Sq, nh, dh).transpose(0, 2, 1, 3)
        vh = v.reshape(Bq, Sq, nh, dh).transpose(0, 2, 1, 3)
        log_f = jax.nn.log_sigmoid(fg)
        cs = jnp.cumsum(log_f, axis=-1)
        diff = cs[..., :, None] - cs[..., None, :]
        mask = jnp.tril(jnp.ones((Sq, Sq), dtype=bool))
        log_fg_mat = jnp.where(mask, diff, -jnp.inf)
        log_D = log_fg_mat + ig[..., None, :]
        max_log_D = jnp.max(log_D, axis=-1, keepdims=True)
        D = jnp.exp(log_D - max_log_D)
        qk = jnp.einsum('bhsd,bhtd->bhst', qh, kh) / jnp.sqrt(jnp.float32(dh))
        C = qk * D
        normalizer = jnp.maximum(jnp.abs(C.sum(-1, keepdims=True)), jnp.exp(-max_log_D))
        h = jnp.einsum('bhst,bhtd->bhsd', C / (normalizer + EPS), vh)
        mean = h.mean(-1, keepdims=True)
        var = ((h - mean) ** 2).mean(-1, keepdims=True)
        hn = (h - mean) / jnp.sqrt(var + LN_EPS)
        hn = hn * out_w.reshape(nh, dh)[None, :, None, :]
        return hn.transpose(0, 2, 1, 3).reshape(Bq, Sq, Eq)

    def _L0_ffn_ref(hidden_states, router_w, gate_up_proj, down_proj, shared_gate_w, shared_up_w, shared_down_w):
        import jax, jax.numpy as jnp
        import numpy as np
        B, S, H = (2, 256, 128)
        N, F, SF, K = (16, 128, 512, 1)
        b, s, h = hidden_states.shape
        hidden = hidden_states.reshape(-1, h)
        t = hidden.shape[0]
        logits = hidden @ router_w.T
        top_vals, top_idx = jax.lax.top_k(logits, K)
        scores = jnp.full_like(logits, -jnp.inf)
        scores = scores.at[jnp.arange(t)[:, None], top_idx].set(top_vals)
        scores = jax.nn.sigmoid(scores.astype(jnp.float32)).astype(hidden.dtype)
        routed_in = hidden[None, :, :] * scores.T[:, :, None]
        gate_up = jnp.einsum('nth,nhf->ntf', routed_in, gate_up_proj)
        gate, up = jnp.split(gate_up, 2, axis=-1)
        routed_out = jnp.einsum('ntf,nfh->nth', up * jax.nn.silu(gate), down_proj)
        expert_sum = routed_out.sum(axis=0)
        shared = jax.nn.silu(hidden @ shared_gate_w.T) * (hidden @ shared_up_w.T) @ shared_down_w.T
        return (shared + expert_sum).reshape(b, s, h)

    def _L1_xattn_ref(feats, embeddings, Wf, Wh, b_att, v, W_ih0, W_hh0, b_ih0, b_hh0, W_ih1, W_hh1, b_ih1, b_hh1):
        import jax, jax.numpy as jnp
        import numpy as np
        B, T, N = (128, 32, 196)
        E = 128
        FD = 128
        H = 128
        A = 128
        SCALE = 0.02

        def _lstm_cell(x, h, c, W_ih, W_hh, b_ih, b_hh):
            gates = x @ W_ih.T + h @ W_hh.T + (b_ih + b_hh)
            i, f, g, o = jnp.split(gates, 4, axis=-1)
            c_new = jax.nn.sigmoid(f) * c + jax.nn.sigmoid(i) * jnp.tanh(g)
            h_new = jax.nn.sigmoid(o) * jnp.tanh(c_new)
            return (h_new, c_new)
        Bb = embeddings.shape[0]
        f_proj = jnp.einsum('bnf,fa->bna', feats, Wf) + b_att
        h0 = jnp.zeros((Bb, H), dtype=feats.dtype)
        c0 = jnp.zeros((Bb, H), dtype=feats.dtype)

        def step(carry, embed_t):
            h0, c0 = carry
            e = jnp.tanh(f_proj + (h0 @ Wh)[:, None, :])
            scores = jnp.einsum('bna,a->bn', e, v)
            alpha = jax.nn.softmax(scores, axis=-1)
            attn = jnp.einsum('bn,bnf->bf', alpha, feats)
            x = jnp.concatenate([embed_t, attn], axis=1)
            h0n, c0n = _lstm_cell(x, h0, c0, W_ih0, W_hh0, b_ih0, b_hh0)
            h1, c1 = _lstm_cell(h0n, h0n, c0n, W_ih1, W_hh1, b_ih1, b_hh1)
            return ((h0n, c0n), h1)
        (_, _), outs = jax.lax.scan(step, (h0, c0), jnp.swapaxes(embeddings, 0, 1))
        return jnp.swapaxes(outs, 0, 1)

    def _L1_ffn_ref(x, ln1_w, ln1_b, ln2_w, ln2_b, Wqkv, bqkv, Wo, bo, gate_W, fc1_w, fc1_b, fc2_w, fc2_b):
        import jax, jax.numpy as jnp
        import numpy as np
        D_MODEL = 128
        N_HEADS = 16
        HEAD_DIM = D_MODEL // N_HEADS
        FFN_DIM = 512
        N_EXPERTS = 8
        TOP_K = 2
        BATCH = 4
        SEQ = 128

        def _layernorm(x, w, b, eps=1e-05):
            mu = jnp.mean(x, axis=-1, keepdims=True)
            var = jnp.mean(jnp.square(x - mu), axis=-1, keepdims=True)
            return (x - mu) * jax.lax.rsqrt(var + eps) * w + b

        def _causal_attention(nx, Wqkv, bqkv, Wo, bo):
            B, S, D = nx.shape
            qkv = nx @ Wqkv + bqkv
            q, k, v = jnp.split(qkv, 3, axis=-1)
            q = q.reshape(B, S, N_HEADS, HEAD_DIM)
            k = k.reshape(B, S, N_HEADS, HEAD_DIM)
            v = v.reshape(B, S, N_HEADS, HEAD_DIM)
            scores = jnp.einsum('bqhd,bkhd->bhqk', q, k) / jnp.sqrt(jnp.float32(HEAD_DIM))
            causal = jnp.tril(jnp.ones((S, S), bool))
            scores = jnp.where(causal, scores, jnp.finfo(scores.dtype).min)
            attn = jax.nn.softmax(scores, axis=-1)
            out = jnp.einsum('bhqk,bkhd->bqhd', attn, v).reshape(B, S, D)
            return out @ Wo + bo

        def _moe_ffn(nx, gate_W, fc1_w, fc1_b, fc2_w, fc2_b):
            gate_logits = nx @ gate_W
            topk_vals, topk_idx = jax.lax.top_k(gate_logits, TOP_K)
            gate_w = jax.nn.softmax(topk_vals, axis=-1)
            dense_gates = jnp.sum(jax.nn.one_hot(topk_idx, N_EXPERTS, dtype=nx.dtype) * gate_w[..., None], axis=-2)
            moe_out = jnp.zeros_like(nx)
            for e in range(N_EXPERTS):
                h = jax.nn.gelu(jnp.einsum('bsd,fd->bsf', nx, fc1_w[e]) + fc1_b[e], approximate=False)
                y = jnp.einsum('bsf,df->bsd', h, fc2_w[e]) + fc2_b[e]
                moe_out = moe_out + y * dense_gates[..., e:e + 1]
            return moe_out
        nx = _layernorm(x, ln1_w, ln1_b)
        attn_out = _causal_attention(nx, Wqkv, bqkv, Wo, bo)
        x = x + attn_out
        nx2 = _layernorm(x, ln2_w, ln2_b)
        moe_out = _moe_ffn(nx2, gate_W, fc1_w, fc1_b, fc2_w, fc2_b)
        return x + moe_out
    x = x + _L0_xattn_ref(_layernorm(x, axis=-1), ctx_1024, ctx_1024, L0_xattn_igate_w, L0_xattn_igate_b, L0_xattn_fgate_w, L0_xattn_fgate_b, L0_xattn_out_w)
    x = x + _L0_ffn_ref(_layernorm(x, axis=-1), L0_ffn_router_w, L0_ffn_gate_up_proj, L0_ffn_down_proj, L0_ffn_shared_gate_w, L0_ffn_shared_up_w, L0_ffn_shared_down_w)
    x = x + _L1_xattn_ref(ctx_1024, _layernorm(x, axis=-1), L1_xattn_Wf, L1_xattn_Wh, L1_xattn_b_att, L1_xattn_v, L1_xattn_W_ih0, L1_xattn_W_hh0, L1_xattn_b_ih0, L1_xattn_b_hh0, L1_xattn_W_ih1, L1_xattn_W_hh1, L1_xattn_b_ih1, L1_xattn_b_hh1)
    x = x + _L1_ffn_ref(_layernorm(x, axis=-1), L1_ffn_ln1_w, L1_ffn_ln1_b, L1_ffn_ln2_w, L1_ffn_ln2_b, L1_ffn_Wqkv, L1_ffn_bqkv, L1_ffn_Wo, L1_ffn_bo, L1_ffn_gate_W, L1_ffn_fc1_w, L1_ffn_fc1_b, L1_ffn_fc2_w, L1_ffn_fc2_b)
    return x

_drawn_inputs = setup_inputs


def setup_inputs(seed=0):
    import zlib

    import numpy as np

    out = dict(_drawn_inputs(seed))
    spreads = {'L1_xattn_b_att': (0.0, 2.0),
     'L1_xattn_b_ih0': (0.0, 0.29),
     'L1_xattn_b_hh0': (0.0, 0.325),
     'L1_xattn_b_ih1': (0.0, 0.781),
     'L1_xattn_b_hh1': (0.0, 0.433),
     'L1_ffn_ln1_w': (1.0, 0.6),
     'L1_ffn_ln1_b': (0.0, 0.97),
     'L1_ffn_ln2_w': (1.0, 0.2),
     'L1_ffn_ln2_b': (0.0, 0.1),
     'L1_ffn_bqkv': (0.0, 0.1),
     'L1_ffn_bo': (0.0, 0.1),
     'L1_ffn_fc1_b': (0.0, 0.457),
     'L1_ffn_fc2_b': (0.0, 0.311)}
    factors = {'L0_xattn_igate_b': 64.0,
     'L0_ffn_router_w': 7.585,
     'L0_ffn_gate_up_proj': 8.0,
     'L0_ffn_down_proj': 7.105,
     'L0_ffn_shared_gate_w': 2.963,
     'L0_ffn_shared_down_w': 2.779,
     'L1_xattn_Wf': 34.469,
     'L1_xattn_Wh': 64.0,
     'L1_xattn_v': 32.062,
     'L1_xattn_W_hh0': 11.99,
     'L1_xattn_W_ih1': 11.916,
     'L1_xattn_W_hh1': 14.567}
    for name, (base, spread) in spreads.items():
        noise = np.random.default_rng([zlib.crc32(name.encode()), seed]).standard_normal(out[name].shape)
        drawn = base * np.exp(spread * noise) if base else spread * noise
        out[name] = jnp.asarray(drawn.astype(out[name].dtype))
    for name, factor in factors.items():
        out[name] = (out[name] * factor).astype(out[name].dtype)
    return out
```

```python
from contextlib import ExitStack

import concourse.bass as bass
from concourse import mybir

ALU = mybir.AluOpType
ACT = mybir.ActivationFunctionType
AX = mybir.AxisListType
F32 = mybir.dt.float32
BF16 = mybir.dt.bfloat16

P = 128
B, S, D = 64, 64, 128
T = B * S
NT = T // P
W = 512
NW = T // W
TW = W // P
H0, DH0 = 8, 16
E0, SF = 16, 512
H1, DH1 = 16, 8
E1, F1 = 8, 512
LN_EPS = 1e-5
NEVER = -1e30
GRP = T // 4
STAGES = 9
START = 1


class Chain:

    def __init__(self, engine, semaphore, per_turn=0):
        self.engine, self.semaphore, self.per_turn = engine, semaphore, per_turn
        self.base, self.n = 0, 0

    def turn(self, i):
        self.base, self.n = i * self.per_turn, 0

    def mark(self, instruction):
        instruction.then_inc(self.semaphore, 1)
        self.n += 1

    def wait(self):
        self.engine.wait_ge(self.semaphore, START + self.base + self.n)

    def step(self, instruction):
        self.mark(instruction)
        self.wait()

    def ended(self):
        assert self.n == self.per_turn, (self.n, self.per_turn)


def reached(n):
    return START + (max(0, n) if isinstance(n, int) else n)


def build(nc, A, out, stages=STAGES):
    ctx = ExitStack()
    with ctx:
        def sb(name, shape, dt=F32):
            return ctx.enter_context(nc.sbuf_tensor(name, shape, dt))

        semaphores = []

        def sem(name):
            semaphores.append(ctx.enter_context(nc.semaphore(name)))
            return semaphores[-1]

        bank = [ctx.enter_context(nc.psum_tensor(f"bank{n}", [P, W], F32)) for n in range(8)]

        x = sb("x", [P, T])
        ctxT = sb("ctxT", [P, T])
        hT = sb("hT", [P, T])
        ident = sb("ident", [P, P])
        ident_bf = sb("ident_bf", [P, P], BF16)
        minus_half = sb("minus_half", [P, NT])
        minus_half64 = sb("minus_half64", [P, NT // 4 * H0])
        ln_stat = sb("ln_stat", [P, NT, 6])
        ln_mean = sb("ln_mean", [P, NT])
        ln_var = sb("ln_var", [P, NT])
        ln_tmp = sb("ln_tmp", [P, 3, NT])
        ln_rstd = sb("ln_rstd", [P, NT])
        ln_out = sb("ln_out", [P, 2, W])

        s_x = sem("s_x")
        s_const = sem("s_const")
        s_half = sem("s_half")
        s_lnchain = sem("s_lnchain")
        s_lnvar = sem("s_lnvar")
        s_lnrstd = sem("s_lnrstd")
        s_lnout = sem("s_lnout")
        s_lntp = sem("s_lntp")
        s_hT = sem("s_hT")
        s_out = sem("s_out")

        w0 = ExitStack()
        ctx.enter_context(w0)

        def sbw0(name, shape, dt=F32):
            return w0.enter_context(nc.sbuf_tensor(name, shape, dt))

        wr = sbw0("wr", [P, E0])
        wg = sbw0("wg", [P, E0, D])
        wu = sbw0("wu", [P, E0, D])
        wd = sbw0("wd", [P, E0, D])
        vg = sbw0("vg", [P, SF])
        vu = sbw0("vu", [P, SF])
        vd = sbw0("vd", [P, SF // P, D])
        prio = sbw0("prio", [P, E0])
        sel0 = sbw0("sel0", [P, E0 + 1, P], BF16)
        l0 = ExitStack()
        ctx.enter_context(l0)

        def sb0(name, shape, dt=F32):
            return l0.enter_context(nc.sbuf_tensor(name, shape, dt))

        gw = sb0("gw", [P, 3, 2, 32])
        gkv = sb0("gkv", [P, 2, 32])
        gb = sb0("gb", [P, 2])
        outw = sb0("outw", [P, D])
        headmask = sb0("headmask", [P, H0])
        causalT = sb0("causalT", [P, W], BF16)
        causal = sb0("causal", [P, W], BF16)
        ig = sb0("ig", [P, GRP])
        zf = sb0("zf", [P, GRP])
        nz = sb0("nz", [P, GRP])
        lf = sb0("lf", [P, GRP])
        cs = sb0("cs", [P, GRP])
        cmax = sb0("cmax", [P, GRP])
        keep = sb0("keep", [P, GRP])
        drop = sb0("drop", [P, GRP])
        gparts = sb0("gparts", [P, 3, GRP], BF16)
        cparts = sb0("cparts", [P, 3, GRP], BF16)
        rest = sb0("rest", [P, 2, GRP])
        enT = sb0("enT", [P, NT, H0])
        lhs9 = sb0("lhs9", [9, 2, 2, W], BF16)
        rhs9 = sb0("rhs9", [9, 2, 2, W // 2], BF16)
        kblk = sb0("kblk", [P, 2, 2, H0, S])
        vraw = sb0("vraw", [P, 2, 2, D])
        vblk = sb0("vblk", [P, 2, 2, H0 // 2, 2, DH0 + 1])
        dmat = sb0("dmat", [P, 2, W])
        cmat = sb0("cmat", [P, 2, W])
        num = sb0("num", [P, NT, H0, DH0 + 1])
        hsum = sb0("hsum", [P, 3, NT * H0])
        hcen = sb0("hcen", [P, 2, NT // 4 * D])

        s_g0 = sem("s_g0")
        s_gsum = sem("s_gsum")
        s_gates = sem("s_gates")
        s_gact = sem("s_gact")
        s_gdve = sem("s_gdve")
        s_gpool = sem("s_gpool")
        s_gout = sem("s_gout")
        s_entp = sem("s_entp")
        s_enT = sem("s_enT")
        s_vinit = sem("s_vinit")
        s_nine = [sem(f"s_nine{u}") for u in range(2)]
        s_vraw = [sem(f"s_vraw{u}") for u in range(2)]
        s_kblk = sem("s_kblk")
        s_vblk = sem("s_vblk")
        s_qk = sem("s_qk")
        s_dlog = sem("s_dlog")
        s_dmat = sem("s_dmat")
        s_cmat = sem("s_cmat")
        s_pv = sem("s_pv")
        s_num = sem("s_num")
        s_ctxT = sem("s_ctxT")
        s_gparts = sem("s_gparts")
        s_cparts = sem("s_cparts")
        s_mld = sem("s_mld")
        s_cmax = sem("s_cmax")
        s_en = sem("s_en")
        s_hchain = sem("s_hchain")
        s_hvar = sem("s_hvar")
        s_hrstd = sem("s_hrstd")
        s_x1 = sem("s_x1")

        gd = nc.dram_tensor("scratch_g", [3, B, H0, S], BF16).ap()
        cd = nc.dram_tensor("scratch_c", [3, B, H0, S], BF16).ap()

        l0.close()
        f0 = ExitStack()
        ctx.enter_context(f0)

        def sbf0(name, shape, dt=F32):
            return f0.enter_context(nc.sbuf_tensor(name, shape, dt))

        lgT = sbf0("lgT", [E0, 2, W])
        lg = sbf0("lg", [P, NT, E0])
        eq = sbf0("eq", [P, NT, E0])
        top = sbf0("top", [P, 4, NT])
        route = sbf0("route", [P, NT, P], BF16)
        routeT = sbf0("routeT", [P, T], BF16)
        hs = sbf0("hs", [P, W])
        mb = sbf0("mb", [P, E0, W], BF16)
        xe = sbf0("xe", [P, 2, W])
        th = sbf0("th", [P, W])
        sg = sbf0("sg", [P, W])
        prs = sbf0("prs", [P, 2, W])
        pp = sbf0("pp", [P, W])
        pe_in = sbf0("pe_in", [P, 4, W])
        yT = sbf0("yT", [P, W])

        s_w0 = sem("s_w0")
        s_lgT = sem("s_lgT")
        s_lgc = sem("s_lgc")
        s_lg = sem("s_lg")
        s_route = sem("s_route")
        s_score = sem("s_score")
        s_parts = sem("s_parts")
        s_rtp = sem("s_rtp")
        s_routeT = sem("s_routeT")
        s_sbc = sem("s_sbc")
        s_hs = sem("s_hs")
        s_mb = sem("s_mb")
        s_mbs = sem("s_mbs")
        s_xe = sem("s_xe")
        s_gu = sem("s_gu")
        s_sgu = sem("s_sgu")
        s_th = sem("s_th")
        s_sg = sem("s_sg")
        s_pr = sem("s_pr")
        s_peD = sem("s_peD")
        s_peP = sem("s_peP")
        s_sdown = sem("s_sdown")
        s_down = sem("s_down")
        s_yT = sem("s_yT")
        s_ytp = sem("s_ytp")
        s_x2 = sem("s_x2")

        f0.close()
        w0.close()
        w1 = ExitStack()
        ctx.enter_context(w1)

        def sbw1(name, shape, dt=F32):
            return w1.enter_context(nc.sbuf_tensor(name, shape, dt))

        wqkv = sbw1("wqkv", [P, 3 * D])
        wo = sbw1("wo", [P, D])
        gw1 = sbw1("gw1", [P, E1])
        fc1 = sbw1("fc1", [P, E1, F1])
        fc2 = sbw1("fc2", [P, E1, F1 // P, D])
        fc1b = sbw1("fc1b", [P, E1, F1 // P])
        fc2b = sbw1("fc2b", [P, E1])
        cols1 = sbw1("cols1", [P, 8])
        bo1 = sbw1("bo1", [1, D])
        headmask1 = sbw1("headmask1", [P, H1])
        causal1 = sbw1("causal1", [P, W], BF16)
        prio1 = sbw1("prio1", [P, E1])
        sel1 = sbw1("sel1", [P, E1, P], BF16)
        r1 = ExitStack()
        ctx.enter_context(r1)

        def sbr1(name, shape, dt=F32):
            return r1.enter_context(nc.sbuf_tensor(name, shape, dt))

        ctx3 = sbr1("ctx3", [P, 3, NT, D], BF16)
        e3 = sbr1("e3", [P, 3, T], BF16)
        wx = sbr1("wx", [P, 3, 4 * D])
        wx3 = sbr1("wx3", [P, 3, 3, 4 * D], BF16)
        Wf = sbr1("Wf", [P, D])
        Wh = sbr1("Wh", [P, D])
        vrow = sbr1("vrow", [P, 2 * B - 2])
        b_att = sbr1("b_att", [P, 1])
        W2 = sbr1("W2", [P, 2, 4 * D])
        b1c = sbr1("b1c", [4, 2, D])
        b1r = sbr1("b1r", [4, D])
        b1p = sbr1("b1p", [P, D], BF16)
        b2c = sbr1("b2c", [P, 2, 4])
        gsel = sbr1("gsel", [P, 4, B], BF16)
        own = sbr1("own", [2, B + P], BF16)
        ones = sbr1("ones", [P, P], BF16)
        fT = sbr1("fT", [P, B, S])
        ex = ctxT[:, :].rearrange("p (b t) -> p b t", b=B)
        Hall = hT
        Call = sbr1("Call", [P, T + B])
        ctx_tok = Call[:, B:B + T].rearrange("p (n f) -> p n f", n=NT)
        state = sbr1("state", [P, B])
        st3 = sbr1("st3", [P, 3, B], BF16)
        strest = sbr1("strest", [P, B])
        unit = sbr1("unit", [P, B])
        nmx = sbr1("nmx", [B, 1])
        al = sbr1("al", [P, P])
        alpha3 = sbr1("alpha3", [P, 3, B], BF16)
        alrest = sbr1("alrest", [P, B])
        rs = sbr1("rs", [P, B])
        at = sbr1("at", [P, 3, B])
        at3 = sbr1("at3", [P, 3, B], BF16)
        tz = sbr1("tz", [P, 4, B])
        ca = sbr1("ca", [P, 2, B])
        tc = sbr1("tc", [P, B])
        t2 = e3[:, 0, :].bitcast(F32).rearrange("p (g w) -> p g w", g=4)
        c2 = e3[:, 1, :].bitcast(F32).rearrange("p (g w) -> p g w", g=4)

        s_w1 = sem("s_w1")
        s_wsc = sem("s_wsc")
        s_fps = sem("s_fps")
        s_fT = sem("s_fT")
        s_bsplit = sem("s_bsplit")
        s_split = sem("s_split")
        s_splitA = sem("s_splitA")
        s_hw = sem("s_hw")
        s_pre = sem("s_pre")
        s_ex = sem("s_ex")
        s_sc = sem("s_sc")
        s_mx = sem("s_mx")
        s_al = sem("s_al")
        s_alT = sem("s_alT")
        s_alc = sem("s_alc")
        s_asum = sem("s_asum")
        s_rs = sem("s_rs")
        s_attn = sem("s_attn")
        s_atc = sem("s_atc")
        s_z = sem("s_z")
        s_tz = sem("s_tz")
        s_cell = sem("s_cell")
        s_c = sem("s_c")
        s_tc = sem("s_tc")
        s_h = sem("s_h")
        s_st = sem("s_st")
        s_unit = sem("s_unit")
        s_2z = sem("s_2z")
        s_2t = sem("s_2t")
        s_2d = sem("s_2d")
        s_2c = sem("s_2c")
        s_2tc = sem("s_2tc")
        s_h1 = sem("s_h1")
        s_h1T = sem("s_h1T")
        s_x3 = sem("s_x3")

        r1.close()
        a1 = ExitStack()
        ctx.enter_context(a1)

        def sba1(name, shape, dt=F32):
            return a1.enter_context(nc.sbuf_tensor(name, shape, dt))

        qT = sba1("qT", [P, T])
        kT = sba1("kT", [P, T])
        bob = sba1("bob", [P, D])
        bvx = sba1("bvx", [P, P])
        ones1 = sba1("ones1", [1, P])
        kblk1 = sba1("kblk1", [P, 2, 2, H1, S])
        qst = sba1("qst", [P, 2, 2, S])
        nst = sba1("nst", [P, 2, 2, 2, S])
        vh = sba1("vh", [P, 2, 2, H1 // 2, 2, DH1 + 1])
        smax = sba1("smax", [P, 2, H1])
        prb = sba1("prb", [P, 2, H1, S])
        prT = sba1("prT", [P, 2, H1 // 2, P])
        asum = sba1("asum", [P, 2, H1])
        att = sba1("att", [P, 2, H1, DH1])
        attT = sba1("attT", [P, 2, P])

        a1.close()
        f1 = ExitStack()
        ctx.enter_context(f1)

        def sbf1(name, shape, dt=F32):
            return f1.enter_context(nc.sbuf_tensor(name, shape, dt))

        lgT1 = sbf1("lgT1", [E1, 2, W])
        lg1 = sbf1("lg1", [P, NT, E1])
        sc1 = sbf1("sc1", [P, 3, NT, E1])
        top1 = sbf1("top1", [P, 6, NT])
        route1 = sbf1("route1", [P, NT, P], BF16)
        routeT1 = sbf1("routeT1", [P, T], BF16)
        hid = sbf1("hid", [P, 4, W])
        gbs = sbf1("gbs", [P, 2, W])
        yg = sbf1("yg", [P, 2, W])
        acc = sbf1("acc", [P, W])

        x3 = ctxT
        s_x3c = sem("s_x3c")
        s_y = sem("s_y")
        s_x3a = sem("s_x3a")
        s_wl1 = sem("s_wl1")
        s_bo = sem("s_bo")
        s_bop = sem("s_bop")
        s_bob = sem("s_bob")
        s_qkp = sem("s_qkp")
        s_qkT = sem("s_qkT")
        s_a1init = sem("s_a1init")
        s_kbD = sem("s_kbD")
        s_kbP = sem("s_kbP")
        s_kq = sem("s_kq")
        s_qst = sem("s_qst")
        s_nst = sem("s_nst")
        s_vps = sem("s_vps")
        s_vh = sem("s_vh")
        s_scr = sem("s_scr")
        s_smax = sem("s_smax")
        s_ssub = sem("s_ssub")
        s_prb = sem("s_prb")
        s_prTp = sem("s_prTp")
        s_prT = sem("s_prT")
        s_pv1 = sem("s_pv1")
        s_asum1 = sem("s_asum1")
        s_att = sem("s_att")
        s_attTp = sem("s_attTp")
        s_attT = sem("s_attT")
        s_wop = sem("s_wop")
        s_x4 = sem("s_x4")
        s_lgT1 = sem("s_lgT1")
        s_lgc1 = sem("s_lgc1")
        s_lg1 = sem("s_lg1")
        s_route1 = sem("s_route1")
        s_top1 = sem("s_top1")
        s_exp1 = sem("s_exp1")
        s_rt1 = sem("s_rt1")
        s_rtp1 = sem("s_rtp1")
        s_routeT1 = sem("s_routeT1")
        s_gb = sem("s_gb")
        s_gbs = sem("s_gbs")
        s_hps = sem("s_hps")
        s_hid = sem("s_hid")
        s_yps = sem("s_yps")
        s_yg = sem("s_yg")
        s_acc = sem("s_acc")
        s_accT = sem("s_accT")
        s_x5 = sem("s_x5")

        block = ctx.enter_context(nc.Block())

        def tile4(buffer, i):
            return buffer[:, bass.ds(i * W, W)]

        LN_STEPS = 6

        def dve_statistics(dve, m):
            c = Chain(dve, s_lnchain)
            c.n = m * (NW + LN_STEPS) + NW
            with dve.Fori(0, NW) as i:
                for j in range(TW):
                    last = nc.vector.bn_stats(ln_stat[:, bass.ds(i * TW + j, 1), :],
                                              x[:, bass.ds(i * W + j * P, P)])
                last.then_inc(s_lnchain, 1)
            c.wait()
            mean_e, mean_o = ln_stat[:, :, 1], ln_stat[:, :, 4]
            c.mark(nc.vector.tensor_tensor(ln_tmp[:, 0, :], mean_e, mean_o, ALU.add))
            c.mark(nc.vector.tensor_tensor(ln_tmp[:, 1, :], mean_e, mean_o, ALU.subtract))
            c.step(nc.vector.tensor_tensor(ln_tmp[:, 2, :], ln_stat[:, :, 2], ln_stat[:, :, 5], ALU.add))
            c.step(nc.vector.tensor_scalar(ln_mean[:, :], ln_tmp[:, 0, :], 0.5, None, ALU.mult))
            c.step(nc.vector.tensor_tensor(ln_tmp[:, 0, :], ln_tmp[:, 1, :], ln_tmp[:, 1, :], ALU.mult))
            c.step(nc.vector.scalar_tensor_tensor(out=ln_tmp[:, 1, :], in0=ln_tmp[:, 0, :], scalar=D / 4.0,
                                                  in1=ln_tmp[:, 2, :], op0=ALU.mult, op1=ALU.add))
            nc.vector.tensor_scalar(ln_var[:, :], ln_tmp[:, 1, :], 1.0 / D, LN_EPS, ALU.mult, ALU.add)\
                .then_inc(s_lnvar, 1)
            dve.wait_ge(s_lnrstd, START + m + 1)

        def dve_layernorm(dve, k, m):
            dve_statistics(dve, m)
            with dve.Fori(0, NW // 2) as turn:
                i = 2 * turn
                dve.wait_ge(s_lntp, START + i + k * NW)
                for u in range(2):
                    for j in range(TW):
                        last = nc.vector.tensor_scalar(
                            ln_out[:, u, j * P:(j + 1) * P], x[:, bass.ds(i * W + (u * TW + j) * P, P)],
                            ln_mean[:, bass.ds(i * TW + u * TW + j, 1)],
                            ln_rstd[:, bass.ds(i * TW + u * TW + j, 1)], ALU.subtract, ALU.mult)
                    last.then_inc(s_lnout, 1)

        def pool_layernorm(pool, k):
            if k == 0:
                nc.gpsimd.memset(minus_half[:, :], -0.5)
                nc.gpsimd.memset(minus_half64[:, :], -0.5).then_inc(s_half, 1)
                pool.wait_ge(s_half, START + 1)
            pool.wait_ge(s_lnvar, START + k + 1)
            nc.gpsimd.tensor_tensor(ln_rstd[:, :], ln_var[:, :], minus_half[:, :], ALU.pow).then_inc(s_lnrstd, 1)

        def pe_layernorm(pe, k):
            with pe.Fori(0, NW // 2) as turn:
                i = 2 * turn
                pe.wait_ge(s_hT, START + i + k * NW)
                for u in range(2):
                    pe.wait_ge(s_lnout, START + i + (k * NW + u + 1))
                    for j in range(TW):
                        last = nc.tensor.transpose(bank[u][:, j * P:(j + 1) * P],
                                                   ln_out[:, u, j * P:(j + 1) * P], ident[:, :])
                    last.then_inc(s_lntp, 1)

        def act_layernorm(act, k, scale=1.0, bias=0.0, by_position=False):
            with act.Fori(0, NW // 2) as turn:
                i = 2 * turn
                for u in range(2):
                    act.wait_ge(s_lntp, START + i + (k * NW + u + 1))
                    if by_position:
                        bs = W // S
                        dst = hT[:, :].rearrange("p (t b) -> p b t", b=B)[:, bass.ds((i + u) * bs, bs), :]
                        src = bank[u][:, :].rearrange("p (b t) -> p b t", t=S)
                    else:
                        dst, src = hT[:, bass.ds((i + u) * W, W)], bank[u][:, :]
                    nc.scalar.activation(dst, src, ACT.Identity, bias=bias, scale=scale).then_inc(s_hT, 1)

        GROUPS = 4
        TAILS = 4
        TT = NT // TAILS

        def sp_mixer(sp):
            for n in range(4):
                cols = slice(n * GRP, (n + 1) * GRP)
                sp.dma_start(x[:, cols], A["x"][:, cols]).then_inc(s_x, 16)
            for dst, src in ((ident, "ident"), (ident_bf, "ident_bf")):
                sp.dma_start(dst[:, :], A[src]).then_inc(s_const, 16)
            for n in range(4):
                cols = slice(n * GRP, (n + 1) * GRP)
                sp.dma_start(ctxT[:, cols], A["ctxT"][:, cols]).then_inc(s_ctxT, 16)
            sp.dma_start(gw[:, :, :, :].rearrange("p a b c -> p (a b c)"), A["gw"]).then_inc(s_g0, 16)
            sp.dma_start(gb[:, :], A["gb"]).then_inc(s_g0, 16)
            sp.dma_start(outw[:, :], A["outw"].to_broadcast([P, D])).then_inc(s_g0, 16)
            sp.dma_start(headmask[:, :], A["headmask0"]).then_inc(s_g0, 16)
            sp.dma_start(causalT[:, :], A["causalT"]).then_inc(s_g0, 16)
            sp.dma_start(causal[:, :], A["causal"]).then_inc(s_g0, 16)
            sp.dma_start(lhs9[:, :, :, :].rearrange("p a b c -> p (a b c)"), A["lhs9"]).then_inc(s_g0, 16)
            sp.dma_start(rhs9[:, :, :, :].rearrange("p a b c -> p (a b c)"), A["rhs9"]).then_inc(s_g0, 16)
            if stages >= 2:
                sp_experts0(sp)
            sp.wait_ge(s_gparts, START + 1)
            for part in range(3):
                for j in range(GROUPS):
                    sp.dma_start(gd[part, 16 * j:16 * j + 16].rearrange("b h t -> h b t"),
                                 gparts[32 * j:32 * j + H0, part, :].rearrange("h (b t) -> h b t", t=S))\
                        .then_inc(s_gout, 16)
            sp.wait_ge(s_cparts, START + 1)
            for part in range(3):
                for j in range(GROUPS):
                    sp.dma_start(cd[part, 16 * j:16 * j + 16].rearrange("b h t -> h b t"),
                                 cparts[32 * j:32 * j + H0, part, :].rearrange("h (b t) -> h b t", t=S))\
                        .then_inc(s_gout, 16)
            sp.wait_ge(s_gout, START + 2 * 3 * GROUPS * 16)
            with sp.Fori(0, NT // 2) as turn:
                i = 2 * turn
                for u in range(2):
                    b0 = 2 * (i + u)
                    sp.wait_ge(s_dlog, START + i)
                    sp.dma_start(lhs9[0:3, u].rearrange("r b n -> r (b n)"),
                                 gd[:, bass.ds(b0, 2)].rearrange("r b h t -> r (b h t)"))\
                        .then_inc(s_nine[u], 16)
                    for h2 in range(2):
                        for b in range(2):
                            sp.dma_start(
                                rhs9[3 + 3 * h2:6 + 3 * h2, u, b, :].rearrange("r (h s) -> r h s", s=S),
                                cd[:, bass.ds(b0 + b, 1)].rearrange("r o (h two) s -> r (o h) two s", two=2)[:, :, h2, :])\
                                .then_inc(s_nine[u], 16)
                    sp.wait_ge(s_vblk, START + i)
                    for dup in range(2):
                        sp.dma_start(vraw[S * dup:S * dup + S, u, :, :],
                                     A["ctx"][bass.ds(b0, 2)].rearrange("b t f -> t b f"))\
                            .then_inc(s_vraw[u], 16)

        def pe_mixer(pe):
            pe.wait_ge(s_const, START + 32)
            pe_layernorm(pe, 0)
            pe.wait_ge(s_gsum, START + 1)
            pe.wait_ge(s_ctxT, START + 64)
            for n in range(NW):
                j, half = n // 2, n % 2
                pe.wait_ge(s_hT, START + n + 1)
                cols = slice(n * W, (n + 1) * W)
                for g in range(2):
                    dst = bank[2 + 2 * g + half][32 * j:32 * j + 32, :]
                    nc.tensor.matmul(dst, gw[:, 0, g, :], hT[:, cols], start=True, stop=False)
                    last = nc.tensor.matmul(dst, gkv[:, g, :], ctxT[:, cols], start=False, stop=True)
            last.then_inc(s_gates, 1)
            pe.wait_ge(s_en, START + 1)
            for c in range(GRP // P):
                last = nc.tensor.transpose(bank[6 + c // 4][:, (c % 4) * P:(c % 4 + 1) * P],
                                           cs[:, c * P:(c + 1) * P], ident[:, :])
            last.then_inc(s_entp, 1)
            pe.wait_ge(s_enT, START + 1)

            with pe.Fori(0, NT // 2) as turn:
                i = 2 * turn
                for u in range(2):
                    pe.wait_ge(s_kblk, START + i + (u + 1))
                    pe.wait_ge(s_cmat, START + i)
                    for b in range(2):
                        for hp in range(H0 // 2):
                            at = b * (W // 2) + hp * S
                            last = nc.tensor.matmul(
                                bank[u][:, at:at + S],
                                kblk[:, u, b, 2 * hp:2 * hp + 2, :].rearrange("p h t -> p (h t)"),
                                hT[:, bass.ds((i + u) * P + b * S, S)], start=True, stop=True)
                    last.then_inc(s_qk, 1)
                    pe.wait_ge(s_nine[u], START + i * (16 * 5 // 2) + 16 * 5)
                    pe.wait_ge(s_dmat, START + i)
                    for b in range(2):
                        for hp in range(H0 // 2):
                            at = b * (W // 2) + hp * S
                            last = nc.tensor.matmul(bank[2 + u][:, at:at + S], lhs9[:, u, b, hp * P:(hp + 1) * P],
                                                    rhs9[:, u, b, hp * S:(hp + 1) * S], start=at == 0,
                                                    stop=False, skip_group_check=True)
                    last = nc.tensor.matmul(bank[2 + u][:, :], ident_bf[:, :], causalT[:, :], start=False,
                                            stop=True, skip_group_check=True)
                    last.then_inc(s_dlog, 1)
                for u in range(2):
                    pe.wait_ge(s_cmat, START + i + (u + 1))
                    pe.wait_ge(s_vblk, START + i + (u + 1))
                    pe.wait_ge(s_num, START + i)
                    for b in range(2):
                        for hp in range(H0 // 2):
                            at = b * (W // 2) + hp * S
                            w = 2 * (DH0 + 1)
                            last = nc.tensor.matmul(
                                bank[4 + u][S * b:S * b + S, hp * w:(hp + 1) * w], cmat[:, u, at:at + S],
                                vblk[:, u, b, hp, :, :].rearrange("p h d -> p (h d)"), start=True, stop=True)
                    last.then_inc(s_pv, 1)

        def act_mixer(act):
            act_layernorm(act, 0)
            a = Chain(act, s_gact)
            act.wait_ge(s_g0, START + 8 * 16)
            act.wait_ge(s_gates, START + 1)
            for half in range(2):
                cols = slice(half * W, (half + 1) * W)
                a.mark(nc.scalar.activation(zf[:, cols], bank[4 + half][:, :], ACT.Identity, bias=gb[:, 1:2]))
            for half in range(2):
                cols = slice(half * W, (half + 1) * W)
                a.mark(nc.scalar.activation(ig[:, cols], bank[2 + half][:, :], ACT.Identity, bias=gb[:, 0:1]))
            act.wait_ge(s_gdve, START + 1)
            a.step(nc.scalar.activation(nz[:, :], nz[:, :], ACT.Exp))
            a.mark(nc.scalar.activation(nz[:, :], nz[:, :], ACT.Ln, bias=1.0))
            act.wait_ge(s_mld, START + 1)
            nc.scalar.activation(cs[:, :], cs[:, :], ACT.Exp, scale=-1.0).then_inc(s_en, 1)
            act.wait_ge(s_entp, START + 1)
            for c4 in range(2):
                src = bank[6 + c4][:, :].rearrange("p (c j h) -> p c j h", c=4, j=GROUPS)[:, :, :, 0:H0]
                dst = enT[:, :, :].rearrange("p (j c) h -> p c j h", j=GROUPS)[:, 4 * c4:4 * c4 + 4]
                last = nc.scalar.activation(dst, src, ACT.Identity)
            last.then_inc(s_enT, 1)
            with act.Fori(0, NT // 2) as turn:
                i = 2 * turn
                for u in range(2):
                    act.wait_ge(s_dlog, START + i + (u + 1))
                    act.wait_ge(s_cmat, START + i)
                    nc.scalar.activation(dmat[:, u, :], bank[2 + u][:, :], ACT.Exp).then_inc(s_dmat, 1)
                for u in range(2):
                    act.wait_ge(s_pv, START + i + (u + 1))
                    nc.scalar.activation(
                        num[:, bass.ds(i + u, 1), :, :].rearrange("p o h d -> p (o h d)"),
                        bank[4 + u][:, 0:H0 * (DH0 + 1)], ACT.Identity).then_inc(s_num, 1)

        def pool_mixer(pool):
            pool_layernorm(pool, 0)
            p = Chain(pool, s_gpool)
            pool.wait_ge(s_cmax, START + 1)
            split(nc.gpsimd, p, cmax, cparts, rest[:, 1, :], s_cparts)
            pool.wait_ge(s_g0, START + 8 * 16)
            pool.wait_ge(s_ctxT, START + 64)
            with pool.Fori(0, NT // 2) as turn:
                i = 2 * turn
                for u in range(2):
                    pool.wait_ge(s_qk, START + i)
                    for b in range(2):
                        k1 = ctxT[:, bass.ds((i + u) * P + b * S, S)]
                        last = nc.gpsimd.tensor_tensor(
                            kblk[:, u, b, :, :], k1.unsqueeze(1).to_broadcast([P, H0, S]),
                            headmask[:, :].unsqueeze(2).to_broadcast([P, H0, S]), ALU.mult)
                    last.then_inc(s_kblk, 1)
            with pool.Fori(0, TAILS) as i:
                pool.wait_ge(s_hvar, START + i + 1)
                nc.gpsimd.tensor_tensor(hsum[:, 1, 0:TT * H0], hsum[:, 2, 0:TT * H0],
                                        minus_half64[:, :], ALU.pow).then_inc(s_hrstd, 1)

        def split(engine, chain, src, parts, spare, ready):
            chain.step(engine.tensor_copy(parts[:, 0, :], src[:, :]))
            chain.step(engine.tensor_tensor(spare, src[:, :], parts[:, 0, :], ALU.subtract))
            chain.step(engine.tensor_copy(parts[:, 1, :], spare))
            engine.tensor_tensor(parts[:, 2, :], spare, parts[:, 1, :], ALU.subtract).then_inc(ready, 1)

        def dve_mixer(dve):
            d = Chain(dve, s_gdve)
            dve.wait_ge(s_g0, START + 8 * 16)
            nc.vector.tensor_tensor(gkv[:, :, :], gw[:, 1, :, :], gw[:, 2, :, :], ALU.add).then_inc(s_gsum, 1)
            dve.wait_ge(s_x, START + 64)
            dve_layernorm(dve, 0, 0)
            dve.wait_ge(s_gact, START + 2)
            d.mark(nc.vector.scalar_tensor_tensor(out=nz[:, :], in0=zf[:, :], scalar=-1.0, in1=zf[:, :],
                                                  op0=ALU.mult, op1=ALU.min))
            d.mark(nc.vector.memset(keep[:, :], 1.0))
            d.step(nc.vector.memset(drop[:, :], 0.0))
            first = lambda buffer: buffer[:, :].rearrange("p (b t) -> p b t", t=S)[:, :, 0:1]
            d.mark(nc.vector.memset(first(keep), 0.0))
            d.mark(nc.vector.memset(first(drop), NEVER))
            dve.wait_ge(s_gact, START + 6)
            d.step(nc.vector.scalar_tensor_tensor(out=lf[:, :], in0=zf[:, :], scalar=0.0, in1=nz[:, :],
                                                  op0=ALU.min, op1=ALU.subtract))
            d.step(nc.vector.tensor_tensor_scan(cs[:, :], keep[:, :], lf[:, :], 0.0, ALU.mult, ALU.add))
            d.step(nc.vector.tensor_tensor(lf[:, :], ig[:, :], cs[:, :], ALU.subtract))
            d.step(nc.vector.tensor_tensor_scan(cmax[:, :], drop[:, :], lf[:, :], 0.0, ALU.add, ALU.max))
            nc.vector.tensor_tensor(cs[:, :], cs[:, :], cmax[:, :], ALU.add).then_inc(s_mld, 1)
            dve.wait_ge(s_mld, START + 1)
            nc.vector.tensor_scalar(cmax[:, :], cmax[:, :], -1.0, None, ALU.mult).then_inc(s_cmax, 1)
            split(nc.vector, d, lf, gparts, rest[:, 0, :], s_gparts)
            nc.vector.memset(vblk[:, :, :, :, :, :].rearrange("p a b c d e -> p (a b c d e)"), 0.0)\
                .then_inc(s_vinit, 1)
            dve.wait_ge(s_vinit, START + 1)
            for h2 in range(2):
                for u in range(2):
                    last = nc.vector.memset(vblk[S * h2:S * h2 + S, u, :, :, h2, DH0:DH0 + 1], 1.0)
            last.then_inc(s_vinit, 1)
            dve.wait_ge(s_vinit, START + 2)
            with dve.Fori(0, NT // 2) as turn:
                i = 2 * turn
                for u in range(2):
                    dve.wait_ge(s_vraw[u], START + i * 16 + 32)
                    dve.wait_ge(s_pv, START + i)
                    for h2 in range(2):
                        rows = slice(S * h2, S * h2 + S)
                        src = vraw[rows, u, :, :].rearrange("p b (h two d) -> p b h two d", two=2, d=DH0)
                        last = nc.vector.tensor_copy(vblk[rows, u, :, :, h2, 0:DH0], src[:, :, :, h2, :])
                    last.then_inc(s_vblk, 1)
                for u in range(2):
                    dve.wait_ge(s_qk, START + i + (u + 1))
                    dve.wait_ge(s_dmat, START + i + (u + 1))
                    dve.wait_ge(s_pv, START + i)
                    nc.vector.tensor_tensor(cmat[:, u, :], bank[u][:, :], dmat[:, u, :], ALU.mult)\
                        .then_inc(s_cmat, 1)
            h = Chain(dve, s_hchain, per_turn=14)
            with dve.Fori(0, TAILS) as i:
                h.turn(i)
                tiles = bass.ds(i * TT, TT)
                dve.wait_ge(s_num, START + i * TT + TT)
                v = num[:, tiles, :, 0:DH0].rearrange("p n h d -> p (n h) d")
                total = num[:, tiles, :, DH0].rearrange("p n h -> p (n h)")
                en = enT[:, tiles, :].rearrange("p n h -> p (n h)")
                r, mean, var = (hsum[:, n, 0:TT * H0] for n in range(3))
                cen, sq = (hcen[:, n, :].rearrange("p (g d) -> p g d", d=DH0) for n in range(2))
                h.mark(nc.vector.tensor_reduce(mean, v, AX.X, ALU.add))
                h.step(nc.vector.scalar_tensor_tensor(out=r, in0=total, scalar=-1.0, in1=total,
                                                      op0=ALU.mult, op1=ALU.max))
                h.step(nc.vector.tensor_tensor(r, r, en, ALU.max))
                h.mark(nc.vector.tensor_scalar(mean, mean, 1.0 / DH0, None, ALU.mult))
                h.step(nc.vector.tensor_scalar(r, r, 1e-6, None, ALU.add))
                h.mark(nc.vector.tensor_tensor(cen, v, mean.unsqueeze(2).to_broadcast([P, TT * H0, DH0]), ALU.subtract))
                h.step(nc.vector.reciprocal(r, r))
                h.step(nc.vector.tensor_tensor(sq, cen, cen, ALU.mult))
                h.step(nc.vector.tensor_reduce(var, sq, AX.X, ALU.add))
                h.step(nc.vector.tensor_tensor(var, var, r, ALU.mult))
                h.step(nc.vector.tensor_tensor(var, var, r, ALU.mult))
                nc.vector.tensor_scalar(var, var, 1.0 / DH0, LN_EPS, ALU.mult, ALU.add).then_inc(s_hvar, 1)
                dve.wait_ge(s_hrstd, START + i + 1)
                h.step(nc.vector.tensor_tensor(r, r, mean, ALU.mult))
                h.step(nc.vector.tensor_tensor(cen, cen, r.unsqueeze(2).to_broadcast([P, TT * H0, DH0]), ALU.mult))
                cen = hcen[:, 0, :].rearrange("p (n f) -> p n f", f=D)
                h.step(nc.vector.tensor_tensor(cen, cen, outw[:, :].unsqueeze(1).to_broadcast([P, TT, D]), ALU.mult))
                xt = x[:, bass.ds(i * (TT * D), TT * D)]
                nc.vector.tensor_tensor(xt, xt, hcen[:, 0, :], ALU.add).then_inc(s_x1, 1)
                dve.wait_ge(s_x1, START + i + 1)
                h.ended()

        SC = SF // P
        SH_AFTER = {5: 1, 10: 2, 15: 3}
        GLUS = SC + 1
        GLU_ROUTED = 3

        def sp_experts0(sp):
            for dst, src in ((wr, "wr"), (prio, "prio")):
                sp.dma_start(dst[:, :], A[src]).then_inc(s_w0, 16)
            sp.dma_start(sel0[:, :, :], A["sel0"]).then_inc(s_w0, 16)
            for dst, src in ((wg, "wg"), (wu, "wu"), (wd, "wd")):
                sp.dma_start(dst[:, :, :], A[src]).then_inc(s_w0, 16)
            for dst, src in ((vg, "vg"), (vu, "vu")):
                sp.dma_start(dst[:, :], A[src]).then_inc(s_w0, 16)
            sp.dma_start(vd[:, :, :], A["vd"]).then_inc(s_w0, 16)

        def pe_experts0(pe):
            pe_layernorm(pe, 1)
            pe.wait_ge(s_w0, START + 9 * 16)
            for n in range(NW):
                pe.wait_ge(s_hT, START + NW + n + 1)
                if n >= 2:
                    pe.wait_ge(s_lgc, START + n - 1)
                nc.tensor.matmul(bank[2 + n % 2][0:E0, :], wr[:, :], hT[:, n * W:(n + 1) * W], start=True,
                                 stop=True).then_inc(s_lgT, 1)
                if n >= 1:
                    logits_by_token(pe, n - 1)
            logits_by_token(pe, NW - 1)
            pe.wait_ge(s_parts, START + 1)
            for n in range(NT):
                per = NT // 4
                last = nc.tensor.transpose(
                    bank[4 + n // per][:, :].bitcast(BF16)[:, (n % per) * P:(n % per + 1) * P],
                    route[:, n, :], ident_bf[:, :])
                if n % per == per - 1:
                    last.then_inc(s_rtp, 1)
            pe.wait_ge(s_routeT, START + 4)
            with pe.Fori(0, NW) as i:
                rcols = routeT[:, bass.ds(i * W, W)]
                hcols = hT[:, bass.ds(i * W, W)]

                def mask(e):
                    if e >= 2:
                        pe.wait_ge(s_mbs, START + i * E0 + (e - 1))
                    else:
                        pe.wait_ge(s_mbs, START + i * E0)
                    nc.tensor.matmul(bank[e % 2][:, :], sel0[:, e, :], rcols, start=True, stop=True)\
                        .then_inc(s_mb, 1)

                def shared(c):
                    if c == 0:
                        pe.wait_ge(s_pr, START + i * GLUS)
                    else:
                        pe.wait_ge(s_pr, START + i * GLUS + (c if c < SC else c + 1))
                    nc.tensor.matmul(bank[4][:, :], vg[:, c * P:(c + 1) * P], hcols, start=True, stop=True)
                    nc.tensor.matmul(bank[5][:, :], vu[:, c * P:(c + 1) * P], hcols, start=True, stop=True)\
                        .then_inc(s_sgu, 1)

                def shared_down(c):
                    pe.wait_ge(s_pr, START + i * GLUS + (c + 1 if c < 3 else GLUS))
                    nc.tensor.matmul(bank[6][:, :], vd[:, c, :], prs[:, c % 2, :], start=c == 0, stop=False)\
                        .then_inc(s_sdown, 1)

                pe.wait_ge(s_x2, START + i)
                nc.tensor.matmul(bank[7][:, :], sel0[:, E0, :], rcols, start=True, stop=True).then_inc(s_sbc, 1)
                mask(0)
                mask(1)
                shared(0)
                for e in range(E0):
                    pe.wait_ge(s_xe, START + i * E0 + (e + 1))
                    nc.tensor.matmul(bank[2][:, :], wg[:, e, :], xe[:, e % 2, :], start=e == 0, stop=e == E0 - 1)
                    nc.tensor.matmul(bank[3][:, :], wu[:, e, :], xe[:, e % 2, :], start=e == 0, stop=e == E0 - 1)\
                        .then_inc(s_gu, 1)
                    if e + 2 < E0:
                        mask(e + 2)
                    if e in SH_AFTER:
                        c = SH_AFTER[e]
                        if c == 1:
                            pe.wait_ge(s_yT, START + i)
                        if c < 3:
                            shared_down(c - 1)
                        shared(c)
                shared_down(2)
                for e in range(E0):
                    if e % 2 == 0:
                        pe.wait_ge(s_peD, START + i * (E0 // 2) + (e // 2 + 1))
                    else:
                        pe.wait_ge(s_peP, START + i * (E0 // 2) + (e // 2 + 1))
                    nc.tensor.matmul(bank[6][:, :], wd[:, e, :], pe_in[:, e % 4, :], start=False,
                                     stop=e == E0 - 1).then_inc(s_down, 1)
                    if e == 3:
                        shared_down(3)
                pe.wait_ge(s_yT, START + i + 1)
                for j in range(TW):
                    last = nc.tensor.transpose(bank[7][:, j * P:(j + 1) * P], yT[:, j * P:(j + 1) * P], ident[:, :])
                last.then_inc(s_ytp, 1)

        def logits_by_token(pe, n):
            pe.wait_ge(s_lgc, START + n + 1)
            for j in range(TW):
                at = (n * TW + j) * E0
                last = nc.tensor.transpose(bank[0][:, at:at + E0], lgT[:, n % 2, j * P:(j + 1) * P],
                                           ident[0:E0, 0:E0])
            last.then_inc(s_lg, 1)

        def act_experts0(act):
            act_layernorm(act, 1)
            for n in range(NW):
                act.wait_ge(s_lgT, START + n + 1)
                if n >= 2:
                    act.wait_ge(s_lg, START + n - 1)
                nc.scalar.activation(lgT[:, n % 2, :], bank[2 + n % 2][0:E0, :], ACT.Identity).then_inc(s_lgc, 1)
            act.wait_ge(s_route, START + 3)
            nc.scalar.activation(top[:, 1, :], top[:, 0, :], ACT.Tanh, scale=0.5).then_inc(s_score, 1)
            for n in range(4):
                act.wait_ge(s_rtp, START + n + 1)
                nc.scalar.activation(routeT[:, n * 2 * W:(n + 1) * 2 * W],
                                     bank[4 + n][:, :].bitcast(BF16), ACT.Identity)\
                    .then_inc(s_routeT, 1)
            with act.Fori(0, NW) as i:
                def mask(e):
                    act.wait_ge(s_mb, START + i * E0 + (e + 1))
                    if e == 0:
                        act.wait_ge(s_peD, START + i * (E0 // 2))
                        act.wait_ge(s_peP, START + i * (E0 // 2))
                    nc.scalar.activation(mb[:, e, :], bank[e % 2][:, :], ACT.Identity).then_inc(s_mbs, 1)

                def tanh(k):
                    if k == GLU_ROUTED:
                        act.wait_ge(s_gu, START + i * E0 + E0)
                    else:
                        act.wait_ge(s_sgu, START + i * SC + (k + 1 if k < GLU_ROUTED else SC))
                    act.wait_ge(s_sg, START + i * GLUS + k)
                    nc.scalar.activation(th[:, :], bank[2 if k == GLU_ROUTED else 4][:, :], ACT.Tanh, scale=0.5)\
                        .then_inc(s_th, 1)

                mask(0)
                mask(1)
                tanh(0)
                for e in range(2, E0):
                    mask(e)
                    if e - 2 in SH_AFTER:
                        tanh(SH_AFTER[e - 2])
                tanh(GLU_ROUTED)
                tanh(GLU_ROUTED + 1)
                act.wait_ge(s_down, START + i * E0 + E0)
                act.wait_ge(s_ytp, START + i)
                nc.scalar.activation(yT[:, :], bank[6][:, :], ACT.Identity).then_inc(s_yT, 1)

        def dve_experts0(dve):
            dve.wait_ge(s_x1, START + TAILS)
            dve_layernorm(dve, 1, 1)
            r = Chain(dve, s_route)
            dve.wait_ge(s_w0, START + 9 * 16)
            dve.wait_ge(s_lg, START + NW)
            bc = lambda a: a.unsqueeze(2).to_broadcast([P, NT, E0])
            r.mark(nc.vector.memset(route[:, :, :].rearrange("p n e -> p (n e)").bitcast(F32), 0.0))
            r.step(nc.vector.tensor_copy(lg[:, :, :].rearrange("p n e -> p (n e)"), bank[0][:, :]))
            r.step(nc.vector.tensor_reduce(top[:, 0, :], lg[:, :, :], AX.X, ALU.max))
            r.step(nc.vector.tensor_tensor(eq[:, :, :], lg[:, :, :], bc(top[:, 0, :]), ALU.is_equal))
            r.step(nc.vector.tensor_tensor(eq[:, :, :], eq[:, :, :],
                                           prio[:, :].unsqueeze(1).to_broadcast([P, NT, E0]), ALU.mult))
            r.step(nc.vector.tensor_reduce(top[:, 2, :], eq[:, :, :], AX.X, ALU.max))
            r.mark(nc.vector.tensor_tensor(route[:, :, 0:E0], eq[:, :, :], bc(top[:, 2, :]), ALU.is_equal))
            dve.wait_ge(s_score, START + 1)
            r.step(nc.vector.tensor_scalar(top[:, 1, :], top[:, 1, :], 0.5, 0.5, ALU.mult, ALU.add))
            r.step(nc.vector.tensor_copy(route[:, :, E0], top[:, 1, :]))
            r.step(nc.vector.tensor_tensor(top[:, 3, :], top[:, 1, :], route[:, :, E0], ALU.subtract))
            r.step(nc.vector.tensor_copy(route[:, :, E0 + 1], top[:, 3, :]))
            nc.vector.tensor_tensor(route[:, :, E0 + 2], top[:, 3, :], route[:, :, E0 + 1], ALU.subtract)\
                .then_inc(s_parts, 1)
            with dve.Fori(0, NW) as i:
                def expert_input(e):
                    dve.wait_ge(s_mbs, START + i * E0 + (e + 1))
                    dve.wait_ge(s_gu, START + i * E0 + max(0, e - 1))
                    nc.vector.tensor_tensor(xe[:, e % 2, :], hs[:, :], mb[:, e, :], ALU.mult).then_inc(s_xe, 1)

                def gated(k):
                    g, dst = (bank[2], pp[:, :]) if k == GLU_ROUTED else (bank[4], prs[:, (k if k < 3 else 3) % 2, :])
                    u = bank[3] if k == GLU_ROUTED else bank[5]
                    dve.wait_ge(s_th, START + i * GLUS + (k + 1))
                    dve.wait_ge(s_pr, START + i * GLUS + k)
                    nc.vector.scalar_tensor_tensor(out=sg[:, :], in0=th[:, :], scalar=1.0, in1=g[:, :],
                                                   op0=ALU.add, op1=ALU.mult).then_inc(s_sg, 1)
                    dve.wait_ge(s_sg, START + i * GLUS + (k + 1))
                    if k == GLU_ROUTED + 1:
                        dve.wait_ge(s_sdown, START + i * SC + 2)
                    elif k == 2:
                        dve.wait_ge(s_sdown, START + i * SC + 1)
                    elif k < 2:
                        dve.wait_ge(s_sdown, START + i * SC)
                    nc.vector.scalar_tensor_tensor(out=dst, in0=sg[:, :], scalar=0.5, in1=u[:, :],
                                                   op0=ALU.mult, op1=ALU.mult).then_inc(s_pr, 1)

                dve.wait_ge(s_sbc, START + i + 1)
                dve.wait_ge(s_gu, START + i * E0)
                nc.vector.tensor_tensor(hs[:, :], tile4(hT, i), bank[7][:, :], ALU.mult).then_inc(s_hs, 1)
                dve.wait_ge(s_hs, START + i + 1)
                expert_input(0)
                expert_input(1)
                gated(0)
                for e in range(2, E0):
                    expert_input(e)
                    if e - 2 in SH_AFTER:
                        gated(SH_AFTER[e - 2])
                gated(GLU_ROUTED)
                gated(GLU_ROUTED + 1)
                dve.wait_ge(s_pr, START + i * GLUS + GLUS)
                for e in range(0, E0, 2):
                    dve.wait_ge(s_down, START + i * E0 + max(0, e - 3))
                    nc.vector.tensor_tensor(pe_in[:, e % 4, :], pp[:, :], mb[:, e, :], ALU.mult).then_inc(s_peD, 1)
                dve.wait_ge(s_ytp, START + i + 1)
                nc.vector.tensor_tensor(tile4(x, i), tile4(x, i), bank[7][:, :], ALU.add).then_inc(s_x2, 1)

        def pool_experts0(pool):
            pool_layernorm(pool, 1)
            with pool.Fori(0, NW) as i:
                for e in range(1, E0, 2):
                    pool.wait_ge(s_pr, START + i * GLUS + (GLU_ROUTED + 1))
                    pool.wait_ge(s_down, START + i * E0 + max(0, e - 3))
                    nc.gpsimd.tensor_tensor(pe_in[:, e % 4, :], pp[:, :], mb[:, e, :], ALU.mult).then_inc(s_peP, 1)

        BC = W // S
        SUMS = ((0, 2), (2, 3), (5, 4), (9, 5), (14, 6), (20, 6), (26, 6))
        PRODUCTS = ((0, 0), (0, 1), (1, 0), (1, 1), (0, 2), (2, 0))
        EMB, ATT, STA = range(3)

        def sp_recurrence(sp):
            sp.wait_ge(s_x2, START + NW)
            for name, dst in (("ctx_tok", ctx_tok[:, :, :]), ("Wf", Wf[:, :]), ("b_att", b_att[:, :]),
                              ("wx", wx[:, :, :]), ("Wh", Wh[:, :]), ("vrow", vrow[:, :]),
                              ("W2", W2[:, :, :]), ("b1c", b1c[:, :, :]), ("b2c", b2c[:, :, :]),
                              ("gsel", gsel[:, :, :]), ("own", own[:, :]), ("ones", ones[:, :])):
                sp.dma_start(dst, A[name]).then_inc(s_w1, 16)

        def pe_recurrence(pe):
            pe_layernorm(pe, 2)
            pe.wait_ge(s_w1, START + 12 * 16)
            for n in range(NW):
                pe.wait_ge(s_fT, START + max(0, n - 3))
                nc.tensor.matmul(bank[2 + n % 4][:, :], Wf[:, :], ctxT[:, n * W:(n + 1) * W], start=True,
                                 stop=True).then_inc(s_fps, 1)
            pe.wait_ge(s_wsc, START + WSC)
            pe.wait_ge(s_split, START + SPLITS * 2 + 3)
            pe.wait_ge(s_fT, START + NW)

            def keep_warm(count):
                for _ in range(count):
                    nc.tensor.matmul(bank[4][:, 0:W // 2], b1p[:, :], gsel[:, :, :].rearrange("p g b -> p (g b)"),
                                     start=True, stop=True, skip_group_check=True)

            def gates(which, parts, last_group, chosen=range(4)):
                for g in chosen:
                    for a, b in PRODUCTS:
                        last = nc.tensor.matmul(bank[3][:, g * B:(g + 1) * B],
                                                wx3[:, which, a, g * D:(g + 1) * D], parts(b), start=False,
                                                stop=last_group and (a, b) == PRODUCTS[-1], skip_group_check=True)
                return last

            with pe.Fori(0, S) as t:
                pe.wait_ge(s_tz, START + t)
                nc.tensor.matmul(bank[3][:, 0:4 * B], b1p[:, :], gsel[:, :, :].rearrange("p g b -> p (g b)"),
                                 start=True, stop=False, skip_group_check=True)
                gates(EMB, lambda b: e3[:, b, bass.ds(t * B, B)], False)
                keep_warm(4)
                nc.tensor.matmul(bank[1][0:B, 0:P], own[:, 0:B], own[:, B:B + P], start=True, stop=False)
                pe.wait_ge(s_h, START + t + 1)
                nc.tensor.matmul(bank[0][:, 0:B], Wh[:, :], state[:, :], start=True, stop=True).then_inc(s_hw, 1)
                keep_warm(8)
                for k, (n0, count) in enumerate(SUMS):
                    pe.wait_ge(s_ex, START + t * len(SUMS) + (k + 1))
                    for p in range(n0, n0 + count):
                        last = nc.tensor.matmul(bank[1][0:B, 0:P], vrow[:, B - 2 - 2 * p:2 * B - 2 - 2 * p],
                                                ex[:, 2 * p:2 * p + 2, :].rearrange("p b t -> p (b t)"),
                                                start=False, stop=p == NT - 1)
                last.then_inc(s_sc, 1)
                pe.wait_ge(s_st, START + 5 * t + 5)
                gates(STA, lambda b: st3[:, b, :], False, (0, 1))
                pe.wait_ge(s_al, START + t + 1)
                nc.tensor.transpose(bank[2][:, 0:P], al[:, :], ident[:, :]).then_inc(s_alT, 1)
                keep_warm(4)
                pe.wait_ge(s_alc, START + 4 * t + 4)
                for part in range(3):
                    last = nc.tensor.matmul(bank[7][:, 0:B], ones[:, :], alpha3[:, part, :], start=part == 0,
                                            stop=part == 2)
                last.then_inc(s_asum, 1)
                for p in range(NT):
                    for part in range(3):
                        last = nc.tensor.matmul(
                            bank[6][:, 0:3 * B].rearrange("p (c b) -> p c b", c=3)[:, 0:3 - part, 2 * p:2 * p + 2],
                            ctx3[:, part, p, :], alpha3[:, 0:3 - part, 2 * p:2 * p + 2], start=part == 0, stop=True,
                            skip_group_check=True)
                last.then_inc(s_attn, 1)
                gates(STA, lambda b: st3[:, b, :], False, (2, 3))
                keep_warm(8)
                pe.wait_ge(s_atc, START + 6 * t + 6)
                gates(ATT, lambda b: at3[:, b, :], True).then_inc(s_z, 1)
            pe.wait_ge(s_tz, START + S)
            pe.wait_ge(s_st, START + 5 * S + 1)
            pe.wait_ge(s_rs, START + S)
            pe.wait_ge(s_atc, START + 6 * S)
            with pe.Fori(0, NW) as i:
                pe.wait_ge(s_2t, START + i * 4)
                for g in range(4):
                    nc.tensor.matmul(bank[g][:, :], W2[:, 0, g * D:(g + 1) * D], Hall[:, bass.ds(i * W, W)],
                                     start=True, stop=True).then_inc(s_2z, 1)
            pe.wait_ge(s_h1, START + NW)
            for n in range(NW):
                if n >= 2:
                    pe.wait_ge(s_x3, START + n - 1)
                for j in range(TW):
                    p = n * TW + j
                    last = nc.tensor.transpose(bank[4 + n % 2][:, j * P:(j + 1) * P],
                                               fT[:, 2 * p:2 * p + 2, :].rearrange("p b t -> p (b t)"), ident[:, :])
                last.then_inc(s_h1T, 1)

        SPLITS = 2 * 4
        PIECE = T // 4
        WSC = 9

        def pieces():
            for n in range(4):
                cols = slice(n * PIECE, (n + 1) * PIECE)
                yield (Call[:, B:B + T][:, cols],
                       lambda k, cols=cols: ctx3[:, k, :, :].rearrange("p n f -> p (n f)")[:, cols])
            for n in range(4):
                cols = slice(n * PIECE, (n + 1) * PIECE)
                yield hT[:, cols], lambda k, cols=cols: e3[:, k, cols]

        def act_recurrence(act):
            act_layernorm(act, 2, by_position=True)
            act.wait_ge(s_w1, START + 12 * 16)
            for n in range(NW):
                act.wait_ge(s_fps, START + n + 1)
                nc.scalar.activation(fT[:, n * BC:(n + 1) * BC, :].rearrange("p b t -> p (b t)"),
                                     bank[2 + n % 4][:, :], ACT.Identity, bias=b_att[:, 0:1]).then_inc(s_fT, 1)
            act.wait_ge(s_hT, START + 3 * NW)
            todo = list(pieces())
            for n in range(SPLITS + 1):
                if n < SPLITS:
                    source, parts = todo[n]
                    nc.scalar.activation(parts(0), source, ACT.Identity).then_inc(s_splitA, 1)
                if n >= 1:
                    source, parts = todo[n - 1]
                    act.wait_ge(s_split, START + 2 * (n - 1) + 1)
                    nc.scalar.activation(parts(1), source, ACT.Identity).then_inc(s_splitA, 1)
            with act.Fori(0, S) as t:
                for k, (n0, count) in enumerate(SUMS):
                    act.wait_ge(s_pre, START + t * len(SUMS) + (k + 1))
                    e = ex[:, 2 * n0:2 * (n0 + count), :].rearrange("p b t -> p (b t)")
                    nc.scalar.activation(e, e, ACT.Tanh).then_inc(s_ex, 1)
                act.wait_ge(s_mx, START + t + 1)
                nc.scalar.activation(al[0:B, :], bank[1][0:B, 0:P], ACT.Exp, bias=nmx[:, 0:1]).then_inc(s_al, 1)
                act.wait_ge(s_z, START + t + 1)
                nc.scalar.activation(tz[:, :, :].rearrange("p g b -> p (g b)"), bank[3][:, 0:4 * B], ACT.Tanh)\
                    .then_inc(s_tz, 1)
                act.wait_ge(s_c, START + t + 1)
                nc.scalar.activation(tc[:, :], Call[:, bass.ds(t * B + B, B)], ACT.Tanh, scale=0.5)\
                    .then_inc(s_tc, 1)
            with act.Fori(0, NW) as i:
                act.wait_ge(s_h1, START + i)
                for g in range(4):
                    act.wait_ge(s_2z, START + i * 4 + (g + 1))
                    nc.scalar.activation(t2[:, g, :], bank[g][:, :], ACT.Tanh, bias=b2c[:, 0, g:g + 1],
                                         scale=0.25 if g < 3 else 0.5).then_inc(s_2t, 1)
                act.wait_ge(s_2c, START + i + 1)
                nc.scalar.activation(c2[:, 2, :], c2[:, 2, :], ACT.Tanh, scale=0.5).then_inc(s_2tc, 1)

        def dve_recurrence(dve):
            dve.wait_ge(s_x2, START + NW)
            dve_layernorm(dve, 2, 2)
            dve.wait_ge(s_w1, START + 12 * 16)
            sc = Chain(dve, s_wsc)
            sc.mark(nc.vector.tensor_tensor(b1r[:, :], b1c[:, 0, :], b1c[:, 1, :], ALU.add))
            sc.mark(nc.vector.tensor_tensor(b2c[:, 0, :], b2c[:, 0, :], b2c[:, 1, :], ALU.add))
            sc.mark(nc.vector.tensor_tensor(W2[:, 0, :], W2[:, 0, :], W2[:, 1, :], ALU.add))
            sc.mark(nc.vector.tensor_scalar(Wh[:, :], Wh[:, :], 0.5, None, ALU.mult))
            sc.step(nc.vector.tensor_scalar(wx[:, STA, :], wx[:, STA, :], 0.5, None, ALU.mult))
            sc.mark(nc.vector.tensor_scalar(b1r[0:3, :], b1r[0:3, :], 0.5, None, ALU.mult))
            sc.mark(nc.vector.tensor_scalar(b2c[:, 0, 0:3], b2c[:, 0, 0:3], 0.5, None, ALU.mult))
            nc.vector.memset(al[:, :], 0.0)
            nc.vector.memset(b1p[:, :].bitcast(F32), 0.0)
            nc.vector.memset(Call[:, 0:B], 0.0)
            sc.step(nc.vector.tensor_scalar(wx[:, :, 0:3 * D], wx[:, :, 0:3 * D], 0.5, None, ALU.mult))
            d = Chain(dve, s_bsplit)
            d.step(nc.vector.tensor_copy(b1p[0:4, :], b1r[:, :]))
            d.step(nc.vector.tensor_tensor(b1r[:, :], b1r[:, :], b1p[0:4, :], ALU.subtract))
            d.step(nc.vector.tensor_copy(b1p[32:36, :], b1r[:, :]))
            d.step(nc.vector.tensor_tensor(b1r[:, :], b1r[:, :], b1p[32:36, :], ALU.subtract))
            sc.mark(nc.vector.tensor_copy(b1p[64:68, :], b1r[:, :]))
            assert sc.n == WSC
            sp_ = Chain(dve, s_split)
            for n, (source, parts) in enumerate(pieces()):
                dve.wait_ge(s_splitA, START + max(1, 2 * n))
                sp_.mark(nc.vector.tensor_tensor(source, source, parts(0), ALU.subtract))
                dve.wait_ge(s_splitA, START + min(2 * n + 3, 2 * SPLITS))
                sp_.mark(nc.vector.tensor_tensor(parts(2), source, parts(1), ALU.subtract))
            sp_.step(nc.vector.tensor_copy(wx3[:, :, 0, :], wx[:, :, :]))
            sp_.step(nc.vector.tensor_tensor(wx[:, :, :], wx[:, :, :], wx3[:, :, 0, :], ALU.subtract))
            nc.vector.tensor_copy(wx3[:, :, 1, :], wx[:, :, :]).then_inc(s_bsplit, 1)
            dve.wait_ge(s_bsplit, START + 5)
            sp_.mark(nc.vector.tensor_tensor(wx3[:, :, 2, :], wx[:, :, :], wx3[:, :, 1, :], ALU.subtract))
            dve.wait_ge(s_split, START + 2 * SPLITS + 3)
            nc.vector.memset(state[:, :], 0.0).then_inc(s_h, 1)
            dve.wait_ge(s_fT, START + NW)
            cell = Chain(dve, s_cell, per_turn=2)
            alc = Chain(dve, s_alc, per_turn=4)
            atc = Chain(dve, s_atc, per_turn=6)
            with dve.Fori(0, S) as t:
                for chain in (cell, alc, atc):
                    chain.turn(t)
                dve.wait_ge(s_hw, START + t + 1)
                dve.wait_ge(s_sc, START + t)
                for n0, count in SUMS:
                    bs = slice(2 * n0, 2 * (n0 + count))
                    nc.vector.tensor_tensor(ex[:, bs, :], fT[:, bs, :],
                                            bank[0][:, bs].unsqueeze(2).to_broadcast([P, 2 * count, S]), ALU.add)\
                        .then_inc(s_pre, 1)
                dve.wait_ge(s_sc, START + t + 1)
                nc.vector.tensor_reduce(nmx[:, :], bank[1][0:B, 0:P], AX.X, ALU.max, negate=True).then_inc(s_mx, 1)
                dve.wait_ge(s_alT, START + t + 1)
                dve.wait_ge(s_attn, START + t)
                alc.step(nc.vector.tensor_copy(alpha3[:, 0, :], bank[2][:, 0:B]))
                alc.step(nc.vector.tensor_tensor(alrest[:, :], bank[2][:, 0:B], alpha3[:, 0, :], ALU.subtract))
                alc.step(nc.vector.tensor_copy(alpha3[:, 1, :], alrest[:, :]))
                alc.mark(nc.vector.tensor_tensor(alpha3[:, 2, :], alrest[:, :], alpha3[:, 1, :], ALU.subtract))
                alc.ended()
                dve.wait_ge(s_asum, START + t + 1)
                nc.vector.reciprocal(rs[:, :], bank[7][:, 0:B]).then_inc(s_rs, 1)
                dve.wait_ge(s_rs, START + t + 1)
                dve.wait_ge(s_attn, START + t + 1)
                atc.step(nc.vector.tensor_reduce(at[:, 0, :], bank[6][:, 0:3 * B].rearrange("p (c b) -> p b c", c=3),
                                                 AX.X, ALU.add))
                atc.step(nc.vector.tensor_tensor(at[:, 1, :], at[:, 0, :], rs[:, :], ALU.mult))
                atc.step(nc.vector.tensor_copy(at3[:, 0, :], at[:, 1, :]))
                atc.step(nc.vector.tensor_tensor(at[:, 2, :], at[:, 1, :], at3[:, 0, :], ALU.subtract))
                atc.step(nc.vector.tensor_copy(at3[:, 1, :], at[:, 2, :]))
                atc.mark(nc.vector.tensor_tensor(at3[:, 2, :], at[:, 2, :], at3[:, 1, :], ALU.subtract))
                atc.ended()
                dve.wait_ge(s_tz, START + t + 1)
                cell.mark(nc.vector.scalar_tensor_tensor(out=ca[:, 0, :], in0=tz[:, 1, :], scalar=1.0,
                                                         in1=Call[:, bass.ds(t * B, B)], op0=ALU.add, op1=ALU.mult))
                cell.step(nc.vector.scalar_tensor_tensor(out=ca[:, 1, :], in0=tz[:, 0, :], scalar=1.0,
                                                         in1=tz[:, 3, :], op0=ALU.add, op1=ALU.mult))
                cell.ended()
                nc.vector.scalar_tensor_tensor(out=Call[:, bass.ds(t * B + B, B)], in0=ca[:, 0, :], scalar=0.5,
                                               in1=ca[:, 1, :], op0=ALU.mult, op1=ALU.add).then_inc(s_c, 1)
                dve.wait_ge(s_tc, START + t + 1)
                dve.wait_ge(s_st, START + 5 * t + 5)
                nc.vector.scalar_tensor_tensor(out=state[:, :], in0=tz[:, 2, :], scalar=1.0,
                                               in1=tc[:, :], op0=ALU.add, op1=ALU.mult).then_inc(s_h, 1)
            d2 = Chain(dve, s_2d, per_turn=2)
            h1 = fT[:, :, :].rearrange("p b t -> p t b")
            with dve.Fori(0, NW) as i:
                d2.turn(i)
                dve.wait_ge(s_2t, START + i * 4 + 4)
                dve.wait_ge(s_h1, START + i)
                d2.mark(nc.vector.scalar_tensor_tensor(out=c2[:, 0, :], in0=t2[:, 1, :], scalar=1.0,
                                                       in1=Call[:, bass.ds(i * W + B, W)], op0=ALU.add, op1=ALU.mult))
                d2.step(nc.vector.scalar_tensor_tensor(out=c2[:, 1, :], in0=t2[:, 0, :], scalar=1.0,
                                                       in1=t2[:, 3, :], op0=ALU.add, op1=ALU.mult))
                nc.vector.scalar_tensor_tensor(out=c2[:, 2, :], in0=c2[:, 0, :], scalar=0.5,
                                               in1=c2[:, 1, :], op0=ALU.mult, op1=ALU.add).then_inc(s_2c, 1)
                dve.wait_ge(s_2tc, START + i + 1)
                tb = lambda a: a.rearrange("p (t b) -> p t b", b=B)
                nc.vector.scalar_tensor_tensor(out=h1[:, bass.ds(i * BC, BC), :], in0=tb(t2[:, 2, :]), scalar=1.0,
                                               in1=tb(c2[:, 2, :]), op0=ALU.add, op1=ALU.mult).then_inc(s_h1, 1)
            for n in range(NW):
                dve.wait_ge(s_h1T, START + n + 1)
                xt = x[:, n * W:(n + 1) * W]
                nc.vector.scalar_tensor_tensor(out=xt, in0=bank[4 + n % 2][:, :], scalar=0.5, in1=xt,
                                               op0=ALU.mult, op1=ALU.add).then_inc(s_x3, 1)

        def pool_recurrence(pool):
            pool_layernorm(pool, 2)
            st = Chain(pool, s_st, per_turn=5)

            def split_state():
                st.step(nc.gpsimd.tensor_tensor(st3[:, 0, :], state[:, :], unit[:, :], ALU.mult))
                st.step(nc.gpsimd.tensor_tensor(strest[:, :], state[:, :], st3[:, 0, :], ALU.subtract))
                st.step(nc.gpsimd.tensor_tensor(st3[:, 1, :], strest[:, :], unit[:, :], ALU.mult))
                st.step(nc.gpsimd.tensor_tensor(st3[:, 2, :], strest[:, :], st3[:, 1, :], ALU.subtract))

            pool.wait_ge(s_x2, START + NW)
            nc.gpsimd.memset(unit[:, :], 1.0).then_inc(s_unit, 1)
            pool.wait_ge(s_unit, START + 1)
            pool.wait_ge(s_h, START + 1)
            split_state()
            st.step(nc.gpsimd.tensor_tensor(strest[:, :], state[:, :], unit[:, :], ALU.mult))
            with pool.Fori(0, S) as t:
                st.turn(t + 1)
                pool.wait_ge(s_h, START + t + 2)
                st.step(nc.gpsimd.tensor_tensor(Hall[:, bass.ds(t * B, B)], state[:, :], unit[:, :], ALU.mult))
                pool.wait_ge(s_z, START + t + 1)
                split_state()
                st.ended()

        HP1 = H1 // 2
        VW = 2 * (DH1 + 1)

        def sp_attention1(sp):
            for name, dst in (("wqkv", wqkv[:, :]), ("wo", wo[:, :]), ("gw1", gw1[:, :]), ("fc1", fc1[:, :, :]),
                              ("fc2", fc2[:, :, :, :]), ("fc1b", fc1b[:, :, :]), ("fc2b", fc2b[:, :]),
                              ("cols1", cols1[:, :]), ("bo1", bo1[:, :]), ("headmask1", headmask1[:, :]),
                              ("causal", causal1[:, :]), ("prio1", prio1[:, :]), ("sel1", sel1[:, :, :])):
                sp.dma_start(dst, A[name]).then_inc(s_wl1, 16)

        def pe_attention1(pe):
            pe_layernorm(pe, 3)
            for n in range(NW):
                pe.wait_ge(s_hT, START + 3 * NW + n + 1)
                for g in range(2):
                    if n >= 1:
                        pe.wait_ge(s_qkT, START + 2 * n + g - 1)
                    nc.tensor.matmul(bank[2 + g][:, :], wqkv[:, g * D:(g + 1) * D], hT[:, n * W:(n + 1) * W],
                                     start=True, stop=True).then_inc(s_qkp, 1)
            pe.wait_ge(s_bo, START + 2)
            nc.tensor.matmul(bank[4][:, 0:D], bvx[:, :], wo[:, :], start=True, stop=False)
            nc.tensor.matmul(bank[4][:, 0:D], ones1[:, :], bo1[:, :], start=False, stop=True).then_inc(s_bop, 1)
            pe.wait_ge(s_bob, START + 1)

            def values(i, u):
                pe.wait_ge(s_nst, START + i + 1)
                pe.wait_ge(s_vh, reached(i))
                pe.wait_ge(s_x4, reached(i - 2))
                for b in range(2):
                    last = nc.tensor.matmul(bank[6][:, b * D:(b + 1) * D],
                                            nst[:, u, b, :, :].rearrange("p a t -> p (a t)"), wqkv[:, 2 * D:3 * D],
                                            start=True, stop=True)
                last.then_inc(s_vps, 1)

            def score_half(i, u, b, n):
                return nc.tensor.matmul(
                    bank[2 * u + n][b * S:b * S + S, :], qst[:, u, b, :],
                    kblk1[:, u, b, n * (H1 // 2):(n + 1) * (H1 // 2), :].rearrange("p h t -> p (h t)"),
                    start=True, stop=False, skip_group_check=True)

            def scores_first(i, u):
                pe.wait_ge(s_qst, START + i + 1)
                pe.wait_ge(s_kbD, START + i + 1)
                pe.wait_ge(s_ssub, reached(2 * (i - 2) + 2))
                for n in range(2):
                    score_half(i, u, 0, n)

            def scores_second(i, u, between):
                pe.wait_ge(s_kbP, START + i + 1)
                score_half(i, u, 1, 0)
                between()
                score_half(i, u, 1, 1).then_inc(s_kq, 1)
                for n in range(2):
                    last = nc.tensor.matmul(bank[2 * u + n][:, :], ident_bf[:, :], causal1[:, :], start=False,
                                            stop=True, skip_group_check=True)
                last.then_inc(s_scr, 1)

            def transposed(i, u):
                pe.wait_ge(s_prb, START + i + 1)
                pe.wait_ge(s_prT, reached(2 * i))
                for hp in range(HP1):
                    last = nc.tensor.transpose(bank[4 + hp // 4][:, (hp % 4) * P:(hp % 4 + 1) * P],
                                               prb[:, u, 2 * hp:2 * hp + 2, :].rearrange("p h t -> p (h t)"),
                                               ident[:, :])
                last.then_inc(s_prTp, 1)

            def attended(i, u):
                pe.wait_ge(s_prT, START + 2 * i + 2)
                pe.wait_ge(s_vh, START + i + 1)
                pe.wait_ge(s_att, reached(i))
                for b in range(2):
                    for hp in range(HP1):
                        last = nc.tensor.matmul(bank[7][b * S:b * S + S, hp * VW:(hp + 1) * VW],
                                                prT[:, u, hp, b * S:b * S + S],
                                                vh[:, u, b, hp, :, :].rearrange("p h d -> p (h d)"),
                                                start=True, stop=True)
                last.then_inc(s_pv1, 1)

            def heads_turned(i, u, values_read):
                pe.wait_ge(s_att, START + i + 1)
                pe.wait_ge(s_vh, START + values_read)
                nc.tensor.transpose(bank[6][:, 2 * D:2 * D + P], att[:, u, :, :].rearrange("p h d -> p (h d)"),
                                    ident[:, :]).then_inc(s_attTp, 1)

            def out_product(i, u):
                pe.wait_ge(s_attT, START + i + 1)
                nc.tensor.matmul(bank[6][:, 3 * D:4 * D], attT[:, u, :], wo[:, :], start=True, stop=True)\
                    .then_inc(s_wop, 1)

            def turn(i, u, first=False):
                values(i + 1, 1 - u)
                scores_first(i + 1, 1 - u)
                transposed(i, u)
                if not first:
                    heads_turned(i - 1, 1 - u, i + 2)
                scores_second(i + 1, 1 - u, lambda: None if first else out_product(i - 1, 1 - u))
                attended(i, u)

            values(0, 0)
            scores_first(0, 0)
            scores_second(0, 0, lambda: None)
            turn(0, 0, first=True)
            with pe.Fori(0, NT // 2 - 1) as j:
                for v in range(2):
                    turn(2 * j + (1 + v), 1 - v)
            transposed(NT - 1, 1)
            heads_turned(NT - 2, 0, NT)
            out_product(NT - 2, 0)
            attended(NT - 1, 1)
            pe.wait_ge(s_x4, START + NT - 1)
            heads_turned(NT - 1, 1, NT)
            out_product(NT - 1, 1)

        def act_attention1(act):
            act.wait_ge(s_wl1, START + 13 * 16)
            act_layernorm(act, 3, scale=cols1[:, 0:1], bias=cols1[:, 1:2])
            act.wait_ge(s_bo, START + 2)
            for n in range(NW):
                for g, dst in enumerate((qT, kT)):
                    act.wait_ge(s_qkp, START + 2 * n + g + 1)
                    nc.scalar.activation(dst[:, n * W:(n + 1) * W], bank[2 + g][:, :], ACT.Identity,
                                         bias=cols1[:, 4 + g:5 + g], scale=DH1 ** -0.5 if g == 0 else 1.0)\
                        .then_inc(s_qkT, 1)
            act.wait_ge(s_bop, START + 1)
            nc.scalar.activation(bob[:, :], bank[4][:, 0:D], ACT.Identity).then_inc(s_bob, 1)

            def operands(i, u):
                act.wait_ge(s_vps, reached(i - 1))
                act.wait_ge(s_kq, reached(i - 1))
                src = hT[:, bass.ds(i * P, P)].rearrange("p (b t) -> p b t", b=2)
                nc.scalar.activation(nst[:, u, :, :, :], src.unsqueeze(2).to_broadcast([P, 2, 2, S]), ACT.Identity)\
                    .then_inc(s_nst, 1)
                nc.scalar.activation(qst[:, u, :, :].rearrange("p b s -> p (b s)"), qT[:, bass.ds(i * P, P)],
                                     ACT.Identity).then_inc(s_qst, 1)

            def exponentials(i, u):
                act.wait_ge(s_ssub, START + 2 * i + 2)
                pr = prb[:, u, :, :].rearrange("p h t -> p (h t)")
                nc.scalar.activation(pr, pr, ACT.Exp).then_inc(s_prb, 1)

            def transposed(i, u):
                act.wait_ge(s_prTp, START + i + 1)
                act.wait_ge(s_pv1, reached(i - 1))
                for n in range(2):
                    nc.scalar.activation(prT[:, u, 4 * n:4 * n + 4, :].rearrange("p h s -> p (h s)"),
                                         bank[4 + n][:, :], ACT.Identity).then_inc(s_prT, 1)

            def heads_turned(i, u):
                act.wait_ge(s_attTp, START + i + 1)
                act.wait_ge(s_wop, reached(i - 1))
                nc.scalar.activation(attT[:, u, :], bank[6][:, 2 * D:2 * D + P], ACT.Identity).then_inc(s_attT, 1)

            operands(0, 0)
            operands(1, 1)
            exponentials(0, 0)
            operands(2, 0)
            transposed(0, 0)
            exponentials(1, 1)

            def turn(i, u, prepare=True):
                if prepare:
                    operands(i + 2, u)
                transposed(i, u)
                heads_turned(i - 1, 1 - u)
                exponentials(i + 1, 1 - u)

            with act.Fori(0, NT // 2 - 2) as j:
                for v in range(2):
                    turn(2 * j + (1 + v), 1 - v)
            turn(NT - 3, 1)
            turn(NT - 2, 0, prepare=False)
            transposed(NT - 1, 1)
            heads_turned(NT - 2, 0)
            heads_turned(NT - 1, 1)

        def dve_attention1(dve):
            dve.wait_ge(s_x3, START + NW)
            dve_statistics(dve, 3)
            dve.wait_ge(s_x3c, START + 1)
            with dve.Fori(0, NW) as i:
                for j in range(TW):
                    xt = x[:, bass.ds(i * W + j * P, P)]
                    last = nc.vector.tensor_scalar(xt, xt, ln_mean[:, bass.ds(i * TW + j, 1)],
                                                   ln_rstd[:, bass.ds(i * TW + j, 1)], ALU.subtract, ALU.mult)
                last.then_inc(s_y, 1)
            dve.wait_ge(s_y, START + NW)
            dve_layernorm(dve, 3, 4)
            dve.wait_ge(s_wl1, START + 13 * 16)
            dve.wait_ge(s_x3, START + NW)
            nc.vector.memset(ones1[:, :], 1.0)
            nc.vector.tensor_copy(bvx[:, :], cols1[:, 6:7].to_broadcast([P, P])).then_inc(s_bo, 1)
            nc.vector.tensor_scalar(cols1[:, 4:5], cols1[:, 4:5], DH1 ** -0.5, None, ALU.mult).then_inc(s_bo, 1)
            nc.vector.memset(vh[:, :, :, :, :, :].rearrange("p a b c d e -> p (a b c d e)"), 0.0)\
                .then_inc(s_a1init, 1)
            dve.wait_ge(s_a1init, START + 1)
            for h2 in range(2):
                last = nc.vector.memset(vh[S * h2:S * h2 + S, :, :, :, h2, DH1:DH1 + 1], 1.0)
            last.then_inc(s_a1init, 1)
            dve.wait_ge(s_a1init, START + 2)
            dve.wait_ge(s_bob, START + 1)
            nc.vector.tensor_tensor(x[:, :].rearrange("p (n f) -> p n f", f=D),
                                    x[:, :].rearrange("p (n f) -> p n f", f=D),
                                    bob[:, :].unsqueeze(1).to_broadcast([P, NT, D]), ALU.add).then_inc(s_a1init, 1)
            dve.wait_ge(s_a1init, START + 3)
            dve.wait_ge(s_qkT, START + 2 * NW)

            def keys(i, u):
                dve.wait_ge(s_kq, reached(i - 1))
                nc.vector.tensor_tensor(kblk1[:, u, 0, :, :],
                                        kT[:, bass.ds(i * P, S)].unsqueeze(1).to_broadcast([P, H1, S]),
                                        headmask1[:, :].unsqueeze(2).to_broadcast([P, H1, S]), ALU.mult)\
                    .then_inc(s_kbD, 1)

            def values(i, u):
                dve.wait_ge(s_vps, START + i + 1)
                dve.wait_ge(s_pv1, reached(i - 1))
                for h2 in range(2):
                    rows = slice(S * h2, S * h2 + S)
                    src = bank[6][rows, 0:2 * D].rearrange("p (b h two d) -> p b h two d", b=2, two=2, d=DH1)
                    last = nc.vector.tensor_copy(vh[rows, u, :, :, h2, 0:DH1], src[:, :, :, h2, :])
                last.then_inc(s_vh, 1)

            def scores(i, u):
                dve.wait_ge(s_scr, START + i + 1)
                dve.wait_ge(s_prTp, reached(i - 1))
                for n in range(2):
                    nc.vector.tensor_reduce(smax[:, u, n * 8:n * 8 + 8],
                                            bank[2 * u + n][:, :].rearrange("p (h t) -> p h t", t=S), AX.X, ALU.max)\
                        .then_inc(s_smax, 1)
                for n in range(2):
                    dve.wait_ge(s_smax, START + 2 * i + (n + 1))
                    nc.vector.tensor_tensor(prb[:, u, n * 8:n * 8 + 8, :],
                                            bank[2 * u + n][:, :].rearrange("p (h t) -> p h t", t=S),
                                            smax[:, u, n * 8:n * 8 + 8].unsqueeze(2).to_broadcast([P, 8, S]),
                                            ALU.subtract).then_inc(s_ssub, 1)

            def attended(i, u):
                dve.wait_ge(s_pv1, START + i + 1)
                dve.wait_ge(s_attTp, reached(i - 1))
                o = bank[7][:, 0:HP1 * VW].rearrange("p (h d) -> p h d", d=DH1 + 1)
                nc.vector.reciprocal(asum[:, u, :], o[:, :, DH1]).then_inc(s_asum1, 1)
                dve.wait_ge(s_asum1, START + i + 1)
                nc.vector.tensor_tensor(att[:, u, :, :], o[:, :, 0:DH1],
                                        asum[:, u, :].unsqueeze(2).to_broadcast([P, H1, DH1]), ALU.mult)\
                    .then_inc(s_att, 1)

            def onto_stream(i):
                dve.wait_ge(s_wop, START + i + 1)
                xt = x[:, bass.ds(i * D, D)]
                nc.vector.tensor_tensor(xt, xt, bank[6][:, 3 * D:4 * D], ALU.add).then_inc(s_x4, 1)

            keys(0, 0)
            values(0, 0)
            keys(1, 1)
            scores(0, 0)
            values(1, 1)
            keys(2, 0)
            scores(1, 1)
            attended(0, 0)

            def turn(i, u, prepare=True):
                values(i + 1, 1 - u)
                if prepare:
                    keys(i + 2, u)
                onto_stream(i - 1)
                scores(i + 1, 1 - u)
                attended(i, u)

            with dve.Fori(0, NT // 2 - 2) as j:
                for v in range(2):
                    turn(2 * j + (1 + v), 1 - v)
            turn(NT - 3, 1)
            turn(NT - 2, 0, prepare=False)
            onto_stream(NT - 2)
            attended(NT - 1, 1)
            onto_stream(NT - 1)

        def pool_attention1(pool):
            pool.wait_ge(s_x3, START + NW)
            nc.gpsimd.tensor_copy(x3[:, :], x[:, :]).then_inc(s_x3c, 1)
            pool_layernorm(pool, 3)
            pool_layernorm(pool, 4)
            pool.wait_ge(s_qkT, START + 2 * NW)

            def keys(i, u):
                pool.wait_ge(s_kq, reached(i - 1))
                nc.gpsimd.tensor_tensor(kblk1[:, u, 1, :, :],
                                        kT[:, bass.ds(i * P + S, S)].unsqueeze(1).to_broadcast([P, H1, S]),
                                        headmask1[:, :].unsqueeze(2).to_broadcast([P, H1, S]), ALU.mult)\
                    .then_inc(s_kbP, 1)

            keys(0, 0)
            keys(1, 1)
            with pool.Fori(1, NT // 2) as j:
                for u in range(2):
                    keys(2 * j + u, u)

        C1 = F1 // P
        UNITS = E1 * C1

        def pe_experts1(pe):
            pe_layernorm(pe, 4)

            def by_token(n):
                pe.wait_ge(s_lgc1, START + n + 1)
                for j in range(TW):
                    at_ = (n * TW + j) * E1
                    last = nc.tensor.transpose(bank[0][:, at_:at_ + E1], lgT1[:, n % 2, j * P:(j + 1) * P],
                                               ident[0:E1, 0:E1])
                last.then_inc(s_lg1, 1)

            for n in range(NW):
                pe.wait_ge(s_hT, START + 4 * NW + n + 1)
                if n >= 2:
                    pe.wait_ge(s_lgc1, START + n - 1)
                nc.tensor.matmul(bank[2 + n % 2][0:E1, :], gw1[:, :], hT[:, n * W:(n + 1) * W], start=True,
                                 stop=True).then_inc(s_lgT1, 1)
                if n >= 1:
                    by_token(n - 1)
            by_token(NW - 1)
            pe.wait_ge(s_rt1, START + 1)
            per = NT // 4
            for n in range(NT):
                last = nc.tensor.transpose(bank[4 + n // per][:, :].bitcast(BF16)[:, (n % per) * P:(n % per + 1) * P],
                                           route1[:, n, :], ident_bf[:, :])
                if n % per == per - 1:
                    last.then_inc(s_rtp1, 1)
            pe.wait_ge(s_routeT1, START + 4)
            with pe.Fori(0, NW) as i:
                hcols = hT[:, bass.ds(i * W, W)]
                rcols = routeT1[:, bass.ds(i * W, W)]

                def first(u):
                    e, c = u // C1, u % C1
                    pe.wait_ge(s_hid, START + i * UNITS + max(0, u - 3))
                    nc.tensor.matmul(bank[u % 4][:, :], fc1[:, e, c * P:(c + 1) * P], hcols, start=True, stop=True)\
                        .then_inc(s_hps, 1)

                def second(u):
                    e, c = u // C1, u % C1
                    if c == 0:
                        pe.wait_ge(s_gbs, START + i * E1 + e)
                        nc.tensor.matmul(bank[6][:, :], sel1[:, e, :], rcols, start=True, stop=True)\
                            .then_inc(s_gb, 1)
                        pe.wait_ge(s_yg, START + i * E1 + max(0, e - 1))
                    pe.wait_ge(s_hid, START + i * UNITS + (u + 1))
                    last = nc.tensor.matmul(bank[4 + e % 2][:, :], fc2[:, e, c, :], hid[:, u % 4, :], start=c == 0,
                                            stop=c == C1 - 1)
                    last.then_inc(s_yps, 1)

                for u in range(UNITS + 2):
                    if u < UNITS:
                        first(u)
                    if u >= 2:
                        second(u - 2)
                pe.wait_ge(s_acc, START + i * (E1 - 1) + (E1 - 1))
                pe.wait_ge(s_x5, START + i)
                for j in range(TW):
                    last = nc.tensor.transpose(bank[7][:, j * P:(j + 1) * P], acc[:, j * P:(j + 1) * P], ident[:, :])
                last.then_inc(s_accT, 1)

        def act_experts1(act):
            act_layernorm(act, 4, scale=cols1[:, 2:3], bias=cols1[:, 3:4])
            for n in range(NW):
                act.wait_ge(s_lgT1, START + n + 1)
                if n >= 2:
                    act.wait_ge(s_lg1, START + n - 1)
                nc.scalar.activation(lgT1[:, n % 2, :], bank[2 + n % 2][0:E1, :], ACT.Identity).then_inc(s_lgc1, 1)
            act.wait_ge(s_top1, START + 1)
            nc.scalar.activation(top1[:, 4, :], top1[:, 4, :], ACT.Exp).then_inc(s_exp1, 1)
            for n in range(4):
                act.wait_ge(s_rtp1, START + n + 1)
                nc.scalar.activation(routeT1[:, n * 2 * W:(n + 1) * 2 * W], bank[4 + n][:, :].bitcast(BF16),
                                     ACT.Identity).then_inc(s_routeT1, 1)
            with act.Fori(0, NW) as i:
                def gate(e):
                    act.wait_ge(s_gb, START + i * E1 + (e + 1))
                    act.wait_ge(s_yg, START + i * E1 + max(0, e - 1))
                    nc.scalar.activation(gbs[:, e % 2, :], bank[6][:, :], ACT.Identity).then_inc(s_gbs, 1)

                for u in range(UNITS):
                    act.wait_ge(s_hps, START + i * UNITS + (u + 1))
                    act.wait_ge(s_yps, START + i * UNITS + max(0, u - 3))
                    nc.scalar.activation(hid[:, u % 4, :], bank[u % 4][:, :], ACT.Gelu,
                                         bias=fc1b[:, u // C1, u % C1:u % C1 + 1]).then_inc(s_hid, 1)
                    if u % C1 == 2:
                        gate(u // C1)

        def dve_experts1(dve):
            dve.wait_ge(s_x4, START + NT)
            dve_layernorm(dve, 4, 5)
            r = Chain(dve, s_route1)
            dve.wait_ge(s_lg1, START + NW)
            flat = lambda a: a.rearrange("p n e -> p (n e)")
            bc = lambda a: a.unsqueeze(2).to_broadcast([P, NT, E1])
            pr = prio1[:, :].unsqueeze(1).to_broadcast([P, NT, E1])
            r.mark(nc.vector.memset(flat(route1[:, :, :]).bitcast(F32), 0.0))
            r.step(nc.vector.tensor_copy(flat(lg1[:, :, :]), bank[0][:, 0:NT * E1]))
            for k in range(2):
                chosen = sc1[:, k, :, :]
                r.step(nc.vector.tensor_reduce(top1[:, k, :], lg1[:, :, :], AX.X, ALU.max))
                r.step(nc.vector.tensor_tensor(chosen, lg1[:, :, :], bc(top1[:, k, :]), ALU.is_equal))
                r.step(nc.vector.tensor_tensor(chosen, chosen, pr, ALU.mult))
                r.step(nc.vector.tensor_reduce(top1[:, 2, :], chosen, AX.X, ALU.max))
                r.step(nc.vector.tensor_tensor(chosen, chosen, bc(top1[:, 2, :]), ALU.is_equal))
                if k == 0:
                    r.step(nc.vector.scalar_tensor_tensor(out=flat(lg1[:, :, :]), in0=flat(chosen), scalar=NEVER,
                                                          in1=flat(lg1[:, :, :]), op0=ALU.mult, op1=ALU.add))
            nc.vector.tensor_tensor(top1[:, 4, :], top1[:, 1, :], top1[:, 0, :], ALU.subtract).then_inc(s_top1, 1)
            dve.wait_ge(s_exp1, START + 1)
            r.step(nc.vector.tensor_scalar(top1[:, 3, :], top1[:, 4, :], 1.0, None, ALU.add))
            r.step(nc.vector.reciprocal(top1[:, 3, :], top1[:, 3, :]))
            r.step(nc.vector.tensor_tensor(top1[:, 5, :], top1[:, 3, :], top1[:, 4, :], ALU.mult))
            r.step(nc.vector.tensor_tensor(sc1[:, 0, :, :], sc1[:, 0, :, :], bc(top1[:, 3, :]), ALU.mult))
            r.step(nc.vector.tensor_tensor(sc1[:, 1, :, :], sc1[:, 1, :, :], bc(top1[:, 5, :]), ALU.mult))
            r.step(nc.vector.tensor_tensor(sc1[:, 0, :, :], sc1[:, 0, :, :], sc1[:, 1, :, :], ALU.add))
            part = lambda n: route1[:, :, n * E1:(n + 1) * E1]
            r.step(nc.vector.tensor_copy(part(0), sc1[:, 0, :, :]))
            r.step(nc.vector.tensor_tensor(sc1[:, 2, :, :], sc1[:, 0, :, :], part(0), ALU.subtract))
            r.step(nc.vector.tensor_copy(part(1), sc1[:, 2, :, :]))
            nc.vector.tensor_tensor(part(2), sc1[:, 2, :, :], part(1), ALU.subtract).then_inc(s_rt1, 1)
            dve.wait_ge(s_x3a, START + 1)
            with dve.Fori(0, NW) as i:
                for e in range(E1):
                    dve.wait_ge(s_yps, START + i * UNITS + C1 * (e + 1))
                    dve.wait_ge(s_gbs, START + i * E1 + (e + 1))
                    if e == 0:
                        dve.wait_ge(s_accT, START + i)
                    dst = acc[:, :] if e == 0 else yg[:, e % 2, :]
                    nc.vector.scalar_tensor_tensor(out=dst, in0=bank[4 + e % 2][:, :], scalar=fc2b[:, e:e + 1],
                                                   in1=gbs[:, e % 2, :], op0=ALU.add, op1=ALU.mult)\
                        .then_inc(s_yg, 1)
                    dve.wait_ge(s_yg, START + i * E1 + (e + 1))
                    if e == 0:
                        continue
                    dve.wait_ge(s_acc, START + i * (E1 - 1) + (e - 1))
                    nc.vector.tensor_tensor(acc[:, :], acc[:, :], yg[:, e % 2, :], ALU.add).then_inc(s_acc, 1)
                dve.wait_ge(s_accT, START + i + 1)
                nc.vector.tensor_tensor(tile4(x, i), tile4(x, i), bank[7][:, :], ALU.add).then_inc(s_x5, 1)

        def pool_experts1(pool):
            pool_layernorm(pool, 5)
            pool.wait_ge(s_lnout, START + 5 * NW)
            nc.gpsimd.tensor_tensor(x[:, :], x[:, :], x3[:, :], ALU.add).then_inc(s_x3a, 1)

        last_stage = [(s_x1, TAILS), (s_x2, NW), (s_x3, NW), (s_x5, NW)][:stages]
        @block.sync
        def _(sp):
            sp_mixer(sp)
            if stages >= 3:
                sp_recurrence(sp)
            if stages >= 4:
                sp_attention1(sp)
            sp.wait_ge(last_stage[-1][0], START + last_stage[-1][1])
            sp.dma_start(out, x[:, :]).then_inc(s_out, 16)
            sp.wait_ge(s_out, START + 16)

        @block.tensor
        def _(pe):
            pe_mixer(pe)
            if stages >= 2:
                pe_experts0(pe)
            if stages >= 3:
                pe_recurrence(pe)
            if stages >= 4:
                pe_attention1(pe)
                pe_experts1(pe)

        @block.scalar
        def _(act):
            act_mixer(act)
            if stages >= 2:
                act_experts0(act)
            if stages >= 3:
                act_recurrence(act)
            if stages >= 4:
                act_attention1(act)
                act_experts1(act)

        @block.vector
        def _(dve):
            dve_mixer(dve)
            if stages >= 2:
                dve_experts0(dve)
            if stages >= 3:
                dve_recurrence(dve)
            if stages >= 4:
                dve_attention1(dve)
                dve_experts1(dve)

        @block.gpsimd
        def _(pool):
            for semaphore in semaphores:
                pool.sem_inc(semaphore, START)
            pool_mixer(pool)
            if stages >= 2:
                pool_experts0(pool)
            if stages >= 3:
                pool_recurrence(pool)
            if stages >= 4:
                pool_attention1(pool)
                pool_experts1(pool)


def layout(I):

    import numpy as np

    bf = mybir.dt.np(BF16)

    def tokens(a):
        return np.ascontiguousarray(a.reshape(NT, P, D).transpose(1, 0, 2).reshape(P, T))

    L = {"x": tokens(I["x"]), "ctx": I["ctx_1024"]}
    L["ctxT"] = np.ascontiguousarray(I["ctx_1024"].reshape(T, D).T)
    L["ident"] = np.eye(P, dtype=np.float32)
    L["ident_bf"] = np.eye(P, dtype=bf)
    gates = [I["L0_xattn_igate_w"], I["L0_xattn_fgate_w"]]
    gw = np.zeros((P, 3, 2, 32), np.float32)
    for n, w in enumerate(gates):
        gw[:, :, n, :H0] = w.reshape(H0, 3, D).transpose(2, 1, 0)
    L["gw"] = gw.reshape(P, 192)
    gb = np.zeros((4, 32, 2), np.float32)
    gb[:, :H0, 0] = I["L0_xattn_igate_b"]
    gb[:, :H0, 1] = I["L0_xattn_fgate_b"]
    L["gb"] = gb.reshape(P, 2)
    L["outw"] = I["L0_xattn_out_w"].reshape(1, D)
    L["headmask0"] = (np.repeat(np.eye(H0), DH0, axis=0) * DH0 ** -0.5).astype(np.float32)
    later = np.where(np.arange(S)[:, None] > np.arange(S)[None, :], NEVER, 0.0)
    L["causalT"] = np.tile(later, (2, W // S)).astype(bf)
    L["causal"] = np.tile(later.T, (2, W // S)).astype(bf)
    lhs9 = np.ones((9, 2, 2, H0 // 2, 2, S))
    lhs9[3:6, :, :, :, 1] = 0
    lhs9[6:9, :, :, :, 0] = 0
    L["lhs9"] = lhs9.reshape(9, -1).astype(bf)
    L["rhs9"] = np.ones((9, 2 * W), bf)
    L["wr"] = I["L0_ffn_router_w"].T
    gate_up = I["L0_ffn_gate_up_proj"].transpose(1, 0, 2)
    L["wg"], L["wu"] = gate_up[:, :, :D], gate_up[:, :, D:]
    L["wd"] = I["L0_ffn_down_proj"].transpose(1, 0, 2)
    L["vg"], L["vu"] = I["L0_ffn_shared_gate_w"].T, I["L0_ffn_shared_up_w"].T
    L["vd"] = I["L0_ffn_shared_down_w"].T.reshape(SF // P, P, D).transpose(1, 0, 2)
    L["prio"] = np.tile(np.arange(E0, 0, -1, dtype=np.float32), (P, 1))
    sel0 = np.zeros((P, E0 + 1, P))
    sel0[np.arange(E0), np.arange(E0)] = 1
    sel0[E0:E0 + 3, E0] = 1
    L["sel0"] = sel0.astype(bf)
    order = lambda w: np.concatenate([w[0:2 * D], w[3 * D:], w[2 * D:3 * D]])
    L["ctx_tok"] = I["ctx_1024"].reshape(NT, P, D).transpose(1, 0, 2)
    L["Wf"], L["Wh"] = I["L1_xattn_Wf"], I["L1_xattn_Wh"]
    L["b_att"] = I["L1_xattn_b_att"].reshape(D, 1)
    L["vrow"] = np.zeros((P, 2 * B - 2), np.float32)
    L["vrow"][:, B - 2:B] = I["L1_xattn_v"][:, None]
    w_in = order(I["L1_xattn_W_ih0"]).T
    L["wx"] = np.stack([w_in[:D], w_in[D:], order(I["L1_xattn_W_hh0"]).T], axis=1)
    L["W2"] = np.stack([order(I["L1_xattn_W_ih1"]).T, order(I["L1_xattn_W_hh1"]).T], axis=1)
    L["b1c"] = np.stack([order(I[f"L1_xattn_b_{k}0"]).reshape(4, D) for k in ("ih", "hh")], axis=1)
    L["b2c"] = np.stack([order(I[f"L1_xattn_b_{k}1"]).reshape(4, D).T for k in ("ih", "hh")], axis=1)
    gsel = np.zeros((P, 4, B))
    for row in (0, 32, 64):
        gsel[row:row + 4] = np.eye(4)[:, :, None]
    L["gsel"] = gsel.astype(bf)
    other = np.array([[0, 1], [1, 0]])
    L["own"] = np.concatenate([np.tile(np.eye(2), (1, B // 2)), np.repeat(other * NEVER, S, axis=1)],
                              axis=1).astype(bf)
    L["ones"] = np.ones((P, P), bf)
    L["wqkv"], L["wo"], L["gw1"] = I["L1_ffn_Wqkv"], I["L1_ffn_Wo"], I["L1_ffn_gate_W"]
    L["fc1"] = I["L1_ffn_fc1_w"].transpose(2, 0, 1)
    L["fc2"] = I["L1_ffn_fc2_w"].transpose(2, 0, 1).reshape(F1 // P, P, E1, D).transpose(1, 2, 0, 3)
    L["fc1b"] = I["L1_ffn_fc1_b"].reshape(E1, F1 // P, P).transpose(2, 0, 1)
    L["fc2b"] = I["L1_ffn_fc2_b"].T
    bqkv = I["L1_ffn_bqkv"].reshape(3, D)
    L["cols1"] = np.stack([I["L1_ffn_ln1_w"], I["L1_ffn_ln1_b"], I["L1_ffn_ln2_w"], I["L1_ffn_ln2_b"], bqkv[0],
                           bqkv[1], bqkv[2], bqkv[2]], axis=1)
    L["bo1"] = I["L1_ffn_bo"].reshape(1, D)
    L["headmask1"] = np.repeat(np.eye(H1, dtype=np.float32), DH1, axis=0)
    L["prio1"] = np.tile(np.arange(E1, 0, -1, dtype=np.float32), (P, 1))
    sel1 = np.zeros((3, E1, E1, P))
    sel1[:, np.arange(E1), np.arange(E1)] = 1
    L["sel1"] = np.concatenate([sel1.reshape(3 * E1, E1, P), np.zeros((P - 3 * E1, E1, P))])\
        .astype(bf)
    return L


def kernel(**inputs):
    import numpy as _np
    import concourse.bacc as _bacc
    from concourse.bass_utils import run_bass_kernel_spmd as _run

    nc = _bacc.Bacc("TRN2", target_bir_lowering=False, num_devices=1)
    arrays, args = {}, {}
    for name, a in layout({k: _np.asarray(v) for k, v in inputs.items()}).items():
        a = _np.ascontiguousarray(a)
        arrays[f"in_{name}"] = a
        args[name] = nc.dram_tensor(f"in_{name}", a.shape, mybir.dt.from_np(a.dtype), kind="ExternalInput").ap()
    out = nc.dram_tensor("out_0_dram", [P, T], F32, kind="ExternalOutput").ap()
    build(nc, args, out)
    r = _run(nc, [arrays], core_ids=[0])
    got = r.results[0]["out_0_dram"]
    return got.reshape(P, NT, D).transpose(1, 0, 2).reshape(B, S, D)
```

```python
from contextlib import ExitStack

import concourse.bass as bass
from concourse import mybir

ALU = mybir.AluOpType
ACT = mybir.ActivationFunctionType
AX = mybir.AxisListType
F32 = mybir.dt.float32
BF16 = mybir.dt.bfloat16
U32 = mybir.dt.uint32

P = 128
B, S, D = 64, 64, 128
T = B * S
NT = T // P
W = 512
NW = T // W
TW = W // P
H0, DH0 = 8, 16
E0, SF = 16, 512
H1, DH1 = 16, 8
E1, F1 = 8, 512
LN_EPS = 1e-5
NEVER = -1e30
NS0 = 48
GRP = T // 4
STAGES = 9
START = 1


class Chain:

    def __init__(self, engine, semaphore, per_turn=0):
        self.engine, self.semaphore, self.per_turn = engine, semaphore, per_turn
        self.base, self.n = 0, 0

    def turn(self, i):
        self.base, self.n = i * self.per_turn, 0

    def mark(self, instruction):
        instruction.then_inc(self.semaphore, 1)
        self.n += 1

    def wait(self):
        self.engine.wait_ge(self.semaphore, START + self.base + self.n)

    def step(self, instruction):
        self.mark(instruction)
        self.wait()

    def ended(self):
        assert self.n == self.per_turn, (self.n, self.per_turn)


def reached(n):
    return START + (max(0, n) if isinstance(n, int) else n)


def build(nc, A, out, stages=STAGES):
    ctx = ExitStack()
    with ctx:
        def sb(name, shape, dt=F32):
            return ctx.enter_context(nc.sbuf_tensor(name, shape, dt))

        semaphores = []

        def sem(name):
            semaphores.append(ctx.enter_context(nc.semaphore(name)))
            return semaphores[-1]

        def sem_from_zero(name):
            return ctx.enter_context(nc.semaphore(name))

        bank = [ctx.enter_context(nc.psum_tensor(f"bank{n}", [P, W], F32)) for n in range(8)]

        x = sb("x", [P, T])
        ctxT = sb("ctxT", [P, T])
        hT = sb("hT", [P, T])
        ident = sb("ident", [P, P])
        ident_bf = sb("ident_bf", [P, P], BF16)
        minus_half = sb("minus_half", [P, NT])
        minus_half64 = sb("minus_half64", [P, NT // 4 * H0])
        ln_stat = sb("ln_stat", [P, NT, 6])
        ln_mean = sb("ln_mean", [P, NT])
        ln_var = sb("ln_var", [P, NT])
        ln_tmp = sb("ln_tmp", [P, 3, NT])
        ln_rstd = sb("ln_rstd", [P, NT])
        ln_out = sb("ln_out", [P, 2, W])

        s_x = sem("s_x")
        s_const = sem("s_const")
        s_half = sem("s_half")
        s_lnchain = sem("s_lnchain")
        s_lnvar = sem("s_lnvar")
        s_lnrstd = sem("s_lnrstd")
        s_lnout = sem("s_lnout")
        s_lntp = sem("s_lntp")
        s_hT = sem("s_hT")
        s_out = sem("s_out")

        w0 = ExitStack()
        ctx.enter_context(w0)

        def sbw0(name, shape, dt=F32):
            return w0.enter_context(nc.sbuf_tensor(name, shape, dt))

        wr = sbw0("wr", [P, E0])
        wexp = sbw0("wexp", [P, E0 * 3 * D])
        vg = sbw0("vg", [P, SF])
        vu = sbw0("vu", [P, SF])
        vd = sbw0("vd", [P, SF // P, D])
        prio = sbw0("prio", [P, E0])
        before = sbw0("before", [P, P], BF16)
        ones0 = sbw0("ones0", [P, P], BF16)
        keep0 = sbw0("keep0", [P, E0 * NT])
        whole = sbw0("whole", [P, NT])
        count0 = sbw0("count0", [P, NS0 + 4])
        l0 = ExitStack()
        ctx.enter_context(l0)

        def sb0(name, shape, dt=F32):
            return l0.enter_context(nc.sbuf_tensor(name, shape, dt))

        gw = sb0("gw", [P, 3, 2, 32])
        gkv = sb0("gkv", [P, 2, 32])
        gb = sb0("gb", [P, 2])
        outw = sb0("outw", [P, D])
        headmask = sb0("headmask", [P, H0])
        causalT = sb0("causalT", [P, W], BF16)
        causal = sb0("causal", [P, W], BF16)
        ig = sb0("ig", [P, GRP])
        zf = sb0("zf", [P, GRP])
        nz = sb0("nz", [P, GRP])
        lf = sb0("lf", [P, GRP])
        cs = sb0("cs", [P, GRP])
        cmax = sb0("cmax", [P, GRP])
        keep = sb0("keep", [P, GRP])
        drop = sb0("drop", [P, GRP])
        gparts = sb0("gparts", [P, 3, GRP], BF16)
        cparts = sb0("cparts", [P, 3, GRP], BF16)
        rest = sb0("rest", [P, 2, GRP])
        enT = sb0("enT", [P, NT, H0])
        lhs9 = sb0("lhs9", [9, 2, 2, W], BF16)
        rhs9 = sb0("rhs9", [9, 2, 2, W // 2], BF16)
        kblk = sb0("kblk", [P, 2, 2, H0, S])
        vraw = sb0("vraw", [P, 2, 2, D])
        vblk = sb0("vblk", [P, 2, 2, H0 // 2, 2, DH0 + 1])
        dmat = sb0("dmat", [P, 2, W])
        cmat = sb0("cmat", [P, 2, W])
        num = sb0("num", [P, NT, H0, DH0 + 1])
        hsum = sb0("hsum", [P, 3, NT * H0])
        hcen = sb0("hcen", [P, 2, NT // 4 * D])

        s_g0 = sem("s_g0")
        s_gsum = sem("s_gsum")
        s_gates = sem("s_gates")
        s_gact = sem("s_gact")
        s_gdve = sem("s_gdve")
        s_gpool = sem("s_gpool")
        s_gout = sem("s_gout")
        s_entp = sem("s_entp")
        s_enT = sem("s_enT")
        s_vinit = sem("s_vinit")
        s_nine = [sem(f"s_nine{u}") for u in range(2)]
        s_vraw = [sem(f"s_vraw{u}") for u in range(2)]
        s_kblk = sem("s_kblk")
        s_vblk = sem("s_vblk")
        s_qk = sem("s_qk")
        s_dlog = sem("s_dlog")
        s_dmat = sem("s_dmat")
        s_cmat = sem("s_cmat")
        s_pv = sem("s_pv")
        s_num = sem("s_num")
        s_ctxT = sem("s_ctxT")
        s_gparts = sem("s_gparts")
        s_cparts = sem("s_cparts")
        s_mld = sem("s_mld")
        s_cmax = sem("s_cmax")
        s_en = sem("s_en")
        s_hchain = sem("s_hchain")
        s_hvar = sem("s_hvar")
        s_hrstd = sem("s_hrstd")
        s_x1 = sem("s_x1")

        gd = nc.dram_tensor("scratch_g", [3, B, H0, S], BF16).ap()
        cd = nc.dram_tensor("scratch_c", [3, B, H0, S], BF16).ap()

        l0.close()
        f0 = ExitStack()
        ctx.enter_context(f0)

        def sbf0(name, shape, dt=F32):
            return f0.enter_context(nc.sbuf_tensor(name, shape, dt))

        lgT = sbf0("lgT", [E0, 2, W])
        lg = sbf0("lg", [P, NT, E0])
        eq = sbf0("eq", [P, NT, E0])
        top = sbf0("top", [P, 4, NT])
        onehot = sbf0("onehot", [P, NT * E0], BF16)
        tot = sbf0("tot", [P, E0 * NT])
        cum = sbf0("cum", [P, E0 * NT])
        cmp0 = sbf0("cmp0", [P, (NS0 + 4) * E0])
        slot = sbf0("slot", [P, NT * E0])
        etiles = sbf0("etiles", [P, 3, E0])
        slotf = sbf0("slotf", [P, NT])
        slots = sbf0("slots", [P, NT], U32)
        wofs = sbf0("wofs", [P, 2, NS0 + 4])
        wofsi = sbf0("wofsi", [P, NS0 + 4], U32)
        scale0 = sbf0("scale0", [P, NT])
        rows = sbf0("rows", [P, NT, D])
        sortd = sbf0("sortd", [P, NS0, D])
        sortT = sbf0("sortT", [P, NS0 * P])
        wst = sbf0("wst", [P, 4, 3 * D])
        th0 = sbf0("th0", [P, 4, P])
        sg0 = sbf0("sg0", [P, 4, P])
        hb0 = sbf0("hb0", [P, 4, P])
        th = sbf0("th", [P, 2, W])
        sg = sbf0("sg", [P, W])
        prs = sbf0("prs", [P, 2, W])

        s_w0 = sem("s_w0")
        s_lgT = sem("s_lgT")
        s_lgc = sem("s_lgc")
        s_lg = sem("s_lg")
        s_route = sem("s_route")
        s_score = sem("s_score")
        s_onehot = sem("s_onehot")
        s_count = sem("s_count")
        s_place = sem("s_place")
        s_slots = sem("s_slots")
        s_zeroed = sem("s_zeroed")
        s_scat = sem_from_zero("s_scat")
        s_sorted = [sem(f"s_sorted{n}") for n in range(4)]
        s_back = [sem_from_zero(f"s_back{n}") for n in range(4)]
        s_srtp = sem("s_srtp")
        s_srT = sem("s_srT")
        s_wst = sem("s_wst")
        s_yps0 = sem("s_yps0")
        s_yo = sem("s_yo")
        s_ystored = sem("s_ystored")
        s_sgu = sem("s_sgu")
        s_th = sem("s_th")
        s_sg = sem("s_sg")
        s_pr = sem("s_pr")
        s_sdown = sem("s_sdown")
        s_x2s = sem("s_x2s")
        s_x2 = sem("s_x2")

        slots_dram = nc.dram_tensor("scratch_slots", [NS0 * P, D], F32).ap()
        outs_dram = nc.dram_tensor("scratch_outs", [NS0 * P, D], F32).ap()

        f0.close()
        w0.close()
        w1 = ExitStack()
        ctx.enter_context(w1)

        def sbw1(name, shape, dt=F32):
            return w1.enter_context(nc.sbuf_tensor(name, shape, dt))

        wqkv = sbw1("wqkv", [P, 3 * D])
        wo = sbw1("wo", [P, D])
        gw1 = sbw1("gw1", [P, E1])
        fc1 = sbw1("fc1", [P, E1, F1])
        fc2 = sbw1("fc2", [P, E1, F1 // P, D])
        fc1b = sbw1("fc1b", [P, E1, F1 // P])
        fc2b = sbw1("fc2b", [P, E1])
        cols1 = sbw1("cols1", [P, 8])
        bo1 = sbw1("bo1", [1, D])
        headmask1 = sbw1("headmask1", [P, H1])
        causal1 = sbw1("causal1", [P, W], BF16)
        prio1 = sbw1("prio1", [P, E1])
        sel1 = sbw1("sel1", [P, E1, P], BF16)
        r1 = ExitStack()
        ctx.enter_context(r1)

        def sbr1(name, shape, dt=F32):
            return r1.enter_context(nc.sbuf_tensor(name, shape, dt))

        ctx3 = sbr1("ctx3", [P, 3, NT, D], BF16)
        e3 = sbr1("e3", [P, 3, T], BF16)
        wx = sbr1("wx", [P, 3, 4 * D])
        wx3 = sbr1("wx3", [P, 3, 3, 4 * D], BF16)
        Wf = sbr1("Wf", [P, D])
        Wh = sbr1("Wh", [P, D])
        vrow = sbr1("vrow", [P, 2 * B - 2])
        b_att = sbr1("b_att", [P, 1])
        W2 = sbr1("W2", [P, 2, 4 * D])
        b1c = sbr1("b1c", [4, 2, D])
        b1r = sbr1("b1r", [4, D])
        b1p = sbr1("b1p", [P, D], BF16)
        b2c = sbr1("b2c", [P, 2, 4])
        gsel = sbr1("gsel", [P, 4, B], BF16)
        own = sbr1("own", [2, B + P], BF16)
        ones = sbr1("ones", [P, P], BF16)
        fT = sbr1("fT", [P, B, S])
        ex = ctxT[:, :].rearrange("p (b t) -> p b t", b=B)
        Hall = hT
        Call = sbr1("Call", [P, T + B])
        ctx_tok = Call[:, B:B + T].rearrange("p (n f) -> p n f", n=NT)
        state = sbr1("state", [P, B])
        st3 = sbr1("st3", [P, 3, B], BF16)
        strest = sbr1("strest", [P, B])
        unit = sbr1("unit", [P, B])
        nmx = sbr1("nmx", [B, 1])
        al = sbr1("al", [P, P])
        alpha3 = sbr1("alpha3", [P, 3, B], BF16)
        alrest = sbr1("alrest", [P, B])
        rs = sbr1("rs", [P, B])
        at = sbr1("at", [P, 3, B])
        at3 = sbr1("at3", [P, 3, B], BF16)
        tz = sbr1("tz", [P, 4, B])
        ca = sbr1("ca", [P, 2, B])
        tc = sbr1("tc", [P, B])
        t2 = e3[:, 0, :].bitcast(F32).rearrange("p (g w) -> p g w", g=4)
        c2 = e3[:, 1, :].bitcast(F32).rearrange("p (g w) -> p g w", g=4)

        s_w1 = sem("s_w1")
        s_wsc = sem("s_wsc")
        s_fps = sem("s_fps")
        s_fT = sem("s_fT")
        s_bsplit = sem("s_bsplit")
        s_split = sem("s_split")
        s_splitA = sem("s_splitA")
        s_hw = sem("s_hw")
        s_pre = sem("s_pre")
        s_ex = sem("s_ex")
        s_sc = sem("s_sc")
        s_mx = sem("s_mx")
        s_al = sem("s_al")
        s_alT = sem("s_alT")
        s_alc = sem("s_alc")
        s_asum = sem("s_asum")
        s_rs = sem("s_rs")
        s_attn = sem("s_attn")
        s_atc = sem("s_atc")
        s_z = sem("s_z")
        s_tz = sem("s_tz")
        s_cell = sem("s_cell")
        s_c = sem("s_c")
        s_tc = sem("s_tc")
        s_h = sem("s_h")
        s_st = sem("s_st")
        s_2z = sem("s_2z")
        s_2t = sem("s_2t")
        s_2d = sem("s_2d")
        s_2c = sem("s_2c")
        s_2tc = sem("s_2tc")
        s_h1 = sem("s_h1")
        s_h1T = sem("s_h1T")
        s_x3 = sem("s_x3")

        r1.close()
        a1 = ExitStack()
        ctx.enter_context(a1)

        def sba1(name, shape, dt=F32):
            return a1.enter_context(nc.sbuf_tensor(name, shape, dt))

        qT = sba1("qT", [P, T])
        kT = sba1("kT", [P, T])
        bob = sba1("bob", [P, D])
        bvx = sba1("bvx", [P, P])
        ones1 = sba1("ones1", [1, P])
        kblk1 = sba1("kblk1", [P, 2, 2, H1, S])
        qst = sba1("qst", [P, 2, 2, S])
        nst = sba1("nst", [P, 2, 2, 2, S])
        vh = sba1("vh", [P, 2, 2, H1 // 2, 2, DH1 + 1])
        smax = sba1("smax", [P, 2, H1])
        prb = sba1("prb", [P, 2, H1, S])
        prT = sba1("prT", [P, 2, H1 // 2, P])
        asum = sba1("asum", [P, 2, H1])
        att = sba1("att", [P, 2, H1, DH1])
        attT = sba1("attT", [P, 2, P])

        a1.close()
        f1 = ExitStack()
        ctx.enter_context(f1)

        def sbf1(name, shape, dt=F32):
            return f1.enter_context(nc.sbuf_tensor(name, shape, dt))

        lgT1 = sbf1("lgT1", [E1, 2, W])
        lg1 = sbf1("lg1", [P, NT, E1])
        sc1 = sbf1("sc1", [P, 3, NT, E1])
        top1 = sbf1("top1", [P, 6, NT])
        route1 = sbf1("route1", [P, NT, P], BF16)
        routeT1 = sbf1("routeT1", [P, T], BF16)
        hid = sbf1("hid", [P, 4, W])
        gbs = sbf1("gbs", [P, 2, W])
        yg = sbf1("yg", [P, 2, W])
        acc = sbf1("acc", [P, W])

        x3 = ctxT
        s_x3c = sem("s_x3c")
        s_y = sem("s_y")
        s_wl1 = sem("s_wl1")
        s_bo = sem("s_bo")
        s_bop = sem("s_bop")
        s_bob = sem("s_bob")
        s_qkp = sem("s_qkp")
        s_qkT = sem("s_qkT")
        s_a1init = sem("s_a1init")
        s_kbD = sem("s_kbD")
        s_kbP = sem("s_kbP")
        s_kq = sem("s_kq")
        s_qst = sem("s_qst")
        s_nst = sem("s_nst")
        s_vps = sem("s_vps")
        s_vh = sem("s_vh")
        s_scr = sem("s_scr")
        s_smax = sem("s_smax")
        s_ssub = sem("s_ssub")
        s_prb = sem("s_prb")
        s_prTp = sem("s_prTp")
        s_prT = sem("s_prT")
        s_pv1 = sem("s_pv1")
        s_asum1 = sem("s_asum1")
        s_att = sem("s_att")
        s_attTp = sem("s_attTp")
        s_attT = sem("s_attT")
        s_wop = sem("s_wop")
        s_x4 = sem("s_x4")
        s_lgT1 = sem("s_lgT1")
        s_lgc1 = sem("s_lgc1")
        s_lg1 = sem("s_lg1")
        s_route1 = sem("s_route1")
        s_top1 = sem("s_top1")
        s_rt1 = sem("s_rt1")
        s_rtp1 = sem("s_rtp1")
        s_routeT1 = sem("s_routeT1")
        s_gb = sem("s_gb")
        s_gbs = sem("s_gbs")
        s_hps = sem("s_hps")
        s_hid = sem("s_hid")
        s_yps = sem("s_yps")
        s_yg = sem("s_yg")
        s_acc = sem("s_acc")
        s_accT = sem("s_accT")
        s_x5 = sem("s_x5")

        block = ctx.enter_context(nc.Block())

        def tile4(buffer, i):
            return buffer[:, bass.ds(i * W, W)]

        LN_STEPS = 6

        def dve_statistics(dve, m):
            c = Chain(dve, s_lnchain)
            c.n = m * (NW + LN_STEPS) + NW
            with dve.Fori(0, NW) as i:
                for j in range(TW):
                    last = nc.vector.bn_stats(ln_stat[:, bass.ds(i * TW + j, 1), :],
                                              x[:, bass.ds(i * W + j * P, P)])
                last.then_inc(s_lnchain, 1)
            c.wait()
            mean_e, mean_o = ln_stat[:, :, 1], ln_stat[:, :, 4]
            c.mark(nc.vector.tensor_tensor(ln_tmp[:, 0, :], mean_e, mean_o, ALU.add))
            c.mark(nc.vector.tensor_tensor(ln_tmp[:, 1, :], mean_e, mean_o, ALU.subtract))
            c.step(nc.vector.tensor_tensor(ln_tmp[:, 2, :], ln_stat[:, :, 2], ln_stat[:, :, 5], ALU.add))
            c.step(nc.vector.tensor_scalar(ln_mean[:, :], ln_tmp[:, 0, :], 0.5, None, ALU.mult))
            c.step(nc.vector.tensor_tensor(ln_tmp[:, 0, :], ln_tmp[:, 1, :], ln_tmp[:, 1, :], ALU.mult))
            c.step(nc.vector.scalar_tensor_tensor(out=ln_tmp[:, 1, :], in0=ln_tmp[:, 0, :], scalar=D / 4.0,
                                                  in1=ln_tmp[:, 2, :], op0=ALU.mult, op1=ALU.add))
            nc.vector.tensor_scalar(ln_var[:, :], ln_tmp[:, 1, :], 1.0 / D, LN_EPS, ALU.mult, ALU.add)\
                .then_inc(s_lnvar, 1)
            dve.wait_ge(s_lnrstd, START + m + 1)

        def dve_layernorm(dve, k, m):
            dve_statistics(dve, m)
            with dve.Fori(0, NW // 2) as turn:
                i = 2 * turn
                dve.wait_ge(s_lntp, START + i + k * NW)
                for u in range(2):
                    for j in range(TW):
                        last = nc.vector.tensor_scalar(
                            ln_out[:, u, j * P:(j + 1) * P], x[:, bass.ds(i * W + (u * TW + j) * P, P)],
                            ln_mean[:, bass.ds(i * TW + u * TW + j, 1)],
                            ln_rstd[:, bass.ds(i * TW + u * TW + j, 1)], ALU.subtract, ALU.mult)
                    last.then_inc(s_lnout, 1)

        def pool_layernorm(pool, k):
            if k == 0:
                nc.gpsimd.memset(minus_half[:, :], -0.5)
                nc.gpsimd.memset(minus_half64[:, :], -0.5).then_inc(s_half, 1)
                pool.wait_ge(s_half, START + 1)
            pool.wait_ge(s_lnvar, START + k + 1)
            nc.gpsimd.tensor_tensor(ln_rstd[:, :], ln_var[:, :], minus_half[:, :], ALU.pow).then_inc(s_lnrstd, 1)

        def pe_layernorm(pe, k):
            with pe.Fori(0, NW // 2) as turn:
                i = 2 * turn
                pe.wait_ge(s_hT, START + i + k * NW)
                for u in range(2):
                    pe.wait_ge(s_lnout, START + i + (k * NW + u + 1))
                    for j in range(TW):
                        last = nc.tensor.transpose(bank[u][:, j * P:(j + 1) * P],
                                                   ln_out[:, u, j * P:(j + 1) * P], ident[:, :])
                    last.then_inc(s_lntp, 1)

        def act_layernorm(act, k, scale=1.0, bias=0.0, by_position=False):
            with act.Fori(0, NW // 2) as turn:
                i = 2 * turn
                for u in range(2):
                    act.wait_ge(s_lntp, START + i + (k * NW + u + 1))
                    if by_position:
                        bs = W // S
                        dst = hT[:, :].rearrange("p (t b) -> p b t", b=B)[:, bass.ds((i + u) * bs, bs), :]
                        src = bank[u][:, :].rearrange("p (b t) -> p b t", t=S)
                    else:
                        dst, src = hT[:, bass.ds((i + u) * W, W)], bank[u][:, :]
                    nc.scalar.activation(dst, src, ACT.Identity, bias=bias, scale=scale).then_inc(s_hT, 1)

        GROUPS = 4
        TAILS = 4
        TT = NT // TAILS

        def sp_mixer(sp):
            for n in range(4):
                cols = slice(n * GRP, (n + 1) * GRP)
                sp.dma_start(x[:, cols], A["x"][:, cols]).then_inc(s_x, 16)
            for dst, src in ((ident, "ident"), (ident_bf, "ident_bf")):
                sp.dma_start(dst[:, :], A[src]).then_inc(s_const, 16)
            for n in range(4):
                cols = slice(n * GRP, (n + 1) * GRP)
                sp.dma_start(ctxT[:, cols], A["ctxT"][:, cols]).then_inc(s_ctxT, 16)
            sp.dma_start(gw[:, :, :, :].rearrange("p a b c -> p (a b c)"), A["gw"]).then_inc(s_g0, 16)
            sp.dma_start(gb[:, :], A["gb"]).then_inc(s_g0, 16)
            sp.dma_start(outw[:, :], A["outw"].to_broadcast([P, D])).then_inc(s_g0, 16)
            sp.dma_start(headmask[:, :], A["headmask0"]).then_inc(s_g0, 16)
            sp.dma_start(causalT[:, :], A["causalT"]).then_inc(s_g0, 16)
            sp.dma_start(causal[:, :], A["causal"]).then_inc(s_g0, 16)
            sp.dma_start(lhs9[:, :, :, :].rearrange("p a b c -> p (a b c)"), A["lhs9"]).then_inc(s_g0, 16)
            sp.dma_start(rhs9[:, :, :, :].rearrange("p a b c -> p (a b c)"), A["rhs9"]).then_inc(s_g0, 16)
            if stages >= 2:
                sp_experts0(sp)
            sp.wait_ge(s_gparts, START + 1)
            for part in range(3):
                for j in range(GROUPS):
                    sp.dma_start(gd[part, 16 * j:16 * j + 16].rearrange("b h t -> h b t"),
                                 gparts[32 * j:32 * j + H0, part, :].rearrange("h (b t) -> h b t", t=S))\
                        .then_inc(s_gout, 16)
            sp.wait_ge(s_cparts, START + 1)
            for part in range(3):
                for j in range(GROUPS):
                    sp.dma_start(cd[part, 16 * j:16 * j + 16].rearrange("b h t -> h b t"),
                                 cparts[32 * j:32 * j + H0, part, :].rearrange("h (b t) -> h b t", t=S))\
                        .then_inc(s_gout, 16)
            sp.wait_ge(s_gout, START + 2 * 3 * GROUPS * 16)
            with sp.Fori(0, NT // 2) as turn:
                i = 2 * turn
                for u in range(2):
                    b0 = 2 * (i + u)
                    sp.wait_ge(s_dlog, START + i)
                    sp.dma_start(lhs9[0:3, u].rearrange("r b n -> r (b n)"),
                                 gd[:, bass.ds(b0, 2)].rearrange("r b h t -> r (b h t)"))\
                        .then_inc(s_nine[u], 16)
                    for h2 in range(2):
                        for b in range(2):
                            sp.dma_start(
                                rhs9[3 + 3 * h2:6 + 3 * h2, u, b, :].rearrange("r (h s) -> r h s", s=S),
                                cd[:, bass.ds(b0 + b, 1)].rearrange("r o (h two) s -> r (o h) two s", two=2)[:, :, h2, :])\
                                .then_inc(s_nine[u], 16)
                    sp.wait_ge(s_vblk, START + i)
                    for dup in range(2):
                        sp.dma_start(vraw[S * dup:S * dup + S, u, :, :],
                                     A["ctx"][bass.ds(b0, 2)].rearrange("b t f -> t b f"))\
                            .then_inc(s_vraw[u], 16)

        def pe_mixer(pe):
            pe.wait_ge(s_const, START + 32)
            pe_layernorm(pe, 0)
            pe.wait_ge(s_gsum, START + 1)
            pe.wait_ge(s_ctxT, START + 64)
            for n in range(NW):
                j, half = n // 2, n % 2
                pe.wait_ge(s_hT, START + n + 1)
                cols = slice(n * W, (n + 1) * W)
                for g in range(2):
                    dst = bank[2 + 2 * g + half][32 * j:32 * j + 32, :]
                    nc.tensor.matmul(dst, gw[:, 0, g, :], hT[:, cols], start=True, stop=False)
                    last = nc.tensor.matmul(dst, gkv[:, g, :], ctxT[:, cols], start=False, stop=True)
            last.then_inc(s_gates, 1)
            pe.wait_ge(s_en, START + 1)
            for c in range(GRP // P):
                last = nc.tensor.transpose(bank[6 + c // 4][:, (c % 4) * P:(c % 4 + 1) * P],
                                           cs[:, c * P:(c + 1) * P], ident[:, :])
            last.then_inc(s_entp, 1)
            pe.wait_ge(s_enT, START + 1)

            with pe.Fori(0, NT // 2) as turn:
                i = 2 * turn
                for u in range(2):
                    pe.wait_ge(s_kblk, START + i + (u + 1))
                    pe.wait_ge(s_cmat, START + i)
                    for b in range(2):
                        for hp in range(H0 // 2):
                            at = b * (W // 2) + hp * S
                            last = nc.tensor.matmul(
                                bank[u][:, at:at + S],
                                kblk[:, u, b, 2 * hp:2 * hp + 2, :].rearrange("p h t -> p (h t)"),
                                hT[:, bass.ds((i + u) * P + b * S, S)], start=True, stop=True)
                    last.then_inc(s_qk, 1)
                    pe.wait_ge(s_nine[u], START + i * (16 * 5 // 2) + 16 * 5)
                    pe.wait_ge(s_dmat, START + i)
                    for b in range(2):
                        for hp in range(H0 // 2):
                            at = b * (W // 2) + hp * S
                            last = nc.tensor.matmul(bank[2 + u][:, at:at + S], lhs9[:, u, b, hp * P:(hp + 1) * P],
                                                    rhs9[:, u, b, hp * S:(hp + 1) * S], start=at == 0,
                                                    stop=False, skip_group_check=True)
                    last = nc.tensor.matmul(bank[2 + u][:, :], ident_bf[:, :], causalT[:, :], start=False,
                                            stop=True, skip_group_check=True)
                    last.then_inc(s_dlog, 1)
                for u in range(2):
                    pe.wait_ge(s_cmat, START + i + (u + 1))
                    pe.wait_ge(s_vblk, START + i + (u + 1))
                    pe.wait_ge(s_num, START + i)
                    for b in range(2):
                        for hp in range(H0 // 2):
                            at = b * (W // 2) + hp * S
                            w = 2 * (DH0 + 1)
                            last = nc.tensor.matmul(
                                bank[4 + u][S * b:S * b + S, hp * w:(hp + 1) * w], cmat[:, u, at:at + S],
                                vblk[:, u, b, hp, :, :].rearrange("p h d -> p (h d)"), start=True, stop=True)
                    last.then_inc(s_pv, 1)

        def act_mixer(act):
            act_layernorm(act, 0)
            a = Chain(act, s_gact)
            act.wait_ge(s_g0, START + 8 * 16)
            act.wait_ge(s_gates, START + 1)
            for half in range(2):
                cols = slice(half * W, (half + 1) * W)
                a.mark(nc.scalar.activation(zf[:, cols], bank[4 + half][:, :], ACT.Identity, bias=gb[:, 1:2]))
            for half in range(2):
                cols = slice(half * W, (half + 1) * W)
                a.mark(nc.scalar.activation(ig[:, cols], bank[2 + half][:, :], ACT.Identity, bias=gb[:, 0:1]))
            act.wait_ge(s_gdve, START + 1)
            a.step(nc.scalar.activation(nz[:, :], nz[:, :], ACT.Exp))
            a.mark(nc.scalar.activation(nz[:, :], nz[:, :], ACT.Ln, bias=1.0))
            act.wait_ge(s_mld, START + 1)
            nc.scalar.activation(cs[:, :], cs[:, :], ACT.Exp, scale=-1.0).then_inc(s_en, 1)
            act.wait_ge(s_entp, START + 1)
            for c4 in range(2):
                src = bank[6 + c4][:, :].rearrange("p (c j h) -> p c j h", c=4, j=GROUPS)[:, :, :, 0:H0]
                dst = enT[:, :, :].rearrange("p (j c) h -> p c j h", j=GROUPS)[:, 4 * c4:4 * c4 + 4]
                last = nc.scalar.activation(dst, src, ACT.Identity)
            last.then_inc(s_enT, 1)
            with act.Fori(0, NT // 2) as turn:
                i = 2 * turn
                for u in range(2):
                    act.wait_ge(s_dlog, START + i + (u + 1))
                    act.wait_ge(s_cmat, START + i)
                    nc.scalar.activation(dmat[:, u, :], bank[2 + u][:, :], ACT.Exp).then_inc(s_dmat, 1)
                for u in range(2):
                    act.wait_ge(s_pv, START + i + (u + 1))
                    nc.scalar.activation(
                        num[:, bass.ds(i + u, 1), :, :].rearrange("p o h d -> p (o h d)"),
                        bank[4 + u][:, 0:H0 * (DH0 + 1)], ACT.Identity).then_inc(s_num, 1)

        def pool_mixer(pool):
            pool_layernorm(pool, 0)
            p = Chain(pool, s_gpool)
            pool.wait_ge(s_cmax, START + 1)
            split(nc.gpsimd, p, cmax, cparts, rest[:, 1, :], s_cparts)
            pool.wait_ge(s_g0, START + 8 * 16)
            pool.wait_ge(s_ctxT, START + 64)
            with pool.Fori(0, NT // 2) as turn:
                i = 2 * turn
                for u in range(2):
                    pool.wait_ge(s_qk, START + i)
                    for b in range(2):
                        k1 = ctxT[:, bass.ds((i + u) * P + b * S, S)]
                        last = nc.gpsimd.tensor_tensor(
                            kblk[:, u, b, :, :], k1.unsqueeze(1).to_broadcast([P, H0, S]),
                            headmask[:, :].unsqueeze(2).to_broadcast([P, H0, S]), ALU.mult)
                    last.then_inc(s_kblk, 1)
            with pool.Fori(0, TAILS) as i:
                pool.wait_ge(s_hvar, START + i + 1)
                nc.gpsimd.tensor_tensor(hsum[:, 1, 0:TT * H0], hsum[:, 2, 0:TT * H0],
                                        minus_half64[:, :], ALU.pow).then_inc(s_hrstd, 1)

        def split(engine, chain, src, parts, spare, ready):
            chain.step(engine.tensor_copy(parts[:, 0, :], src[:, :]))
            chain.step(engine.tensor_tensor(spare, src[:, :], parts[:, 0, :], ALU.subtract))
            chain.step(engine.tensor_copy(parts[:, 1, :], spare))
            engine.tensor_tensor(parts[:, 2, :], spare, parts[:, 1, :], ALU.subtract).then_inc(ready, 1)

        def dve_mixer(dve):
            d = Chain(dve, s_gdve)
            dve.wait_ge(s_g0, START + 8 * 16)
            nc.vector.tensor_tensor(gkv[:, :, :], gw[:, 1, :, :], gw[:, 2, :, :], ALU.add).then_inc(s_gsum, 1)
            dve.wait_ge(s_x, START + 64)
            dve_layernorm(dve, 0, 0)
            dve.wait_ge(s_gact, START + 2)
            d.mark(nc.vector.scalar_tensor_tensor(out=nz[:, :], in0=zf[:, :], scalar=-1.0, in1=zf[:, :],
                                                  op0=ALU.mult, op1=ALU.min))
            d.mark(nc.vector.memset(keep[:, :], 1.0))
            d.step(nc.vector.memset(drop[:, :], 0.0))
            first = lambda buffer: buffer[:, :].rearrange("p (b t) -> p b t", t=S)[:, :, 0:1]
            d.mark(nc.vector.memset(first(keep), 0.0))
            d.mark(nc.vector.memset(first(drop), NEVER))
            dve.wait_ge(s_gact, START + 6)
            d.step(nc.vector.scalar_tensor_tensor(out=lf[:, :], in0=zf[:, :], scalar=0.0, in1=nz[:, :],
                                                  op0=ALU.min, op1=ALU.subtract))
            d.step(nc.vector.tensor_tensor_scan(cs[:, :], keep[:, :], lf[:, :], 0.0, ALU.mult, ALU.add))
            d.step(nc.vector.tensor_tensor(lf[:, :], ig[:, :], cs[:, :], ALU.subtract))
            d.step(nc.vector.tensor_tensor_scan(cmax[:, :], drop[:, :], lf[:, :], 0.0, ALU.add, ALU.max))
            nc.vector.tensor_tensor(cs[:, :], cs[:, :], cmax[:, :], ALU.add).then_inc(s_mld, 1)
            dve.wait_ge(s_mld, START + 1)
            nc.vector.tensor_scalar(cmax[:, :], cmax[:, :], -1.0, None, ALU.mult).then_inc(s_cmax, 1)
            split(nc.vector, d, lf, gparts, rest[:, 0, :], s_gparts)
            nc.vector.memset(vblk[:, :, :, :, :, :].rearrange("p a b c d e -> p (a b c d e)"), 0.0)\
                .then_inc(s_vinit, 1)
            dve.wait_ge(s_vinit, START + 1)
            for h2 in range(2):
                for u in range(2):
                    last = nc.vector.memset(vblk[S * h2:S * h2 + S, u, :, :, h2, DH0:DH0 + 1], 1.0)
            last.then_inc(s_vinit, 1)
            dve.wait_ge(s_vinit, START + 2)
            with dve.Fori(0, NT // 2) as turn:
                i = 2 * turn
                for u in range(2):
                    dve.wait_ge(s_vraw[u], START + i * 16 + 32)
                    dve.wait_ge(s_pv, START + i)
                    for h2 in range(2):
                        rows = slice(S * h2, S * h2 + S)
                        src = vraw[rows, u, :, :].rearrange("p b (h two d) -> p b h two d", two=2, d=DH0)
                        last = nc.vector.tensor_copy(vblk[rows, u, :, :, h2, 0:DH0], src[:, :, :, h2, :])
                    last.then_inc(s_vblk, 1)
                for u in range(2):
                    dve.wait_ge(s_qk, START + i + (u + 1))
                    dve.wait_ge(s_dmat, START + i + (u + 1))
                    dve.wait_ge(s_pv, START + i)
                    nc.vector.tensor_tensor(cmat[:, u, :], bank[u][:, :], dmat[:, u, :], ALU.mult)\
                        .then_inc(s_cmat, 1)
            h = Chain(dve, s_hchain, per_turn=14)
            with dve.Fori(0, TAILS) as i:
                h.turn(i)
                tiles = bass.ds(i * TT, TT)
                dve.wait_ge(s_num, START + i * TT + TT)
                v = num[:, tiles, :, 0:DH0].rearrange("p n h d -> p (n h) d")
                total = num[:, tiles, :, DH0].rearrange("p n h -> p (n h)")
                en = enT[:, tiles, :].rearrange("p n h -> p (n h)")
                r, mean, var = (hsum[:, n, 0:TT * H0] for n in range(3))
                cen, sq = (hcen[:, n, :].rearrange("p (g d) -> p g d", d=DH0) for n in range(2))
                h.mark(nc.vector.tensor_reduce(mean, v, AX.X, ALU.add))
                h.step(nc.vector.scalar_tensor_tensor(out=r, in0=total, scalar=-1.0, in1=total,
                                                      op0=ALU.mult, op1=ALU.max))
                h.step(nc.vector.tensor_tensor(r, r, en, ALU.max))
                h.mark(nc.vector.tensor_scalar(mean, mean, 1.0 / DH0, None, ALU.mult))
                h.step(nc.vector.tensor_scalar(r, r, 1e-6, None, ALU.add))
                h.mark(nc.vector.tensor_tensor(cen, v, mean.unsqueeze(2).to_broadcast([P, TT * H0, DH0]), ALU.subtract))
                h.step(nc.vector.reciprocal(r, r))
                h.step(nc.vector.tensor_tensor(sq, cen, cen, ALU.mult))
                h.step(nc.vector.tensor_reduce(var, sq, AX.X, ALU.add))
                h.step(nc.vector.tensor_tensor(var, var, r, ALU.mult))
                h.step(nc.vector.tensor_tensor(var, var, r, ALU.mult))
                nc.vector.tensor_scalar(var, var, 1.0 / DH0, LN_EPS, ALU.mult, ALU.add).then_inc(s_hvar, 1)
                dve.wait_ge(s_hrstd, START + i + 1)
                h.step(nc.vector.tensor_tensor(r, r, mean, ALU.mult))
                h.step(nc.vector.tensor_tensor(cen, cen, r.unsqueeze(2).to_broadcast([P, TT * H0, DH0]), ALU.mult))
                cen = hcen[:, 0, :].rearrange("p (n f) -> p n f", f=D)
                h.step(nc.vector.tensor_tensor(cen, cen, outw[:, :].unsqueeze(1).to_broadcast([P, TT, D]), ALU.mult))
                xt = x[:, bass.ds(i * (TT * D), TT * D)]
                nc.vector.tensor_tensor(xt, xt, hcen[:, 0, :], ALU.add).then_inc(s_x1, 1)
                dve.wait_ge(s_x1, START + i + 1)
                h.ended()

        SC = SF // P
        SHARED = NW * SC
        QS0 = NS0 // 4

        def sp_experts0(sp):
            for dst, src in ((wr, "wr"), (prio, "prio"), (before, "before"), (ones0, "ones"), (keep0, "keep0"),
                             (whole, "whole"), (count0, "count0"), (vg, "vg"), (vu, "vu"), (wexp, "wexp")):
                sp.dma_start(dst[:, :], A[src]).then_inc(s_w0, 16)
            sp.dma_start(vd[:, :, :], A["vd"]).then_inc(s_w0, 16)

        W0_LOADS = 11

        def sp_slots0(sp):
            by_tile = lambda dram: dram.rearrange("(j p) f -> p j f", p=P)
            sp.wait_ge(s_half, START + 2)
            sp.dma_start(by_tile(slots_dram), sortd[:, :, :]).then_inc(s_zeroed, 16)
            sp.wait_ge(s_scat, NT * 16)
            for n in range(4):
                tiles = slice(n * QS0, (n + 1) * QS0)
                sp.dma_start(sortd[:, tiles, :], by_tile(slots_dram)[:, tiles, :]).then_inc(s_sorted[n], 16)
            for n in range(4):
                tiles = slice(n * QS0, (n + 1) * QS0)
                sp.wait_ge(s_yo, START + (n + 1) * QS0)
                sp.dma_start(by_tile(outs_dram)[:, tiles, :], sortd[:, tiles, :]).then_inc(s_ystored, 16)

        def slot_turns(engine, turn):
            for j in range(4):
                turn(j, j, lambda n: True)
            with engine.Fori(1, NS0 // 4 - 1) as t:
                for u in range(4):
                    turn(4 * t + u, u, lambda n: True)
            for u in range(4):
                turn(NS0 - 4 + u, u, lambda n: u + n < 4)

        def pe_experts0(pe):
            pe_layernorm(pe, 1)
            pe.wait_ge(s_w0, START + W0_LOADS * 16)
            for n in range(NW):
                pe.wait_ge(s_hT, START + NW + n + 1)
                if n >= 2:
                    pe.wait_ge(s_lgc, START + n - 1)
                nc.tensor.matmul(bank[2 + n % 2][0:E0, :], wr[:, :], hT[:, n * W:(n + 1) * W], start=True,
                                 stop=True).then_inc(s_lgT, 1)
                if n >= 1:
                    logits_by_token(pe, n - 1)
            logits_by_token(pe, NW - 1)
            pe.wait_ge(s_onehot, START + 1)
            nc.tensor.matmul(bank[7][:, :], before[:, :], onehot[:, :], start=True, stop=True)
            nc.tensor.matmul(bank[6][:, :], ones0[:, :], onehot[:, :], start=True, stop=True).then_inc(s_count, 1)
            pe.wait_ge(s_slots, START + 1)
            with pe.Fori(0, NW) as i:
                hcols = hT[:, bass.ds(i * W, W)]

                def gate_up(c):
                    pe.wait_ge(s_pr, START + i * SC + max(0, c - 1))
                    g = 2 * (c % 2)
                    nc.tensor.matmul(bank[2 + g][:, :], vg[:, c * P:(c + 1) * P], hcols, start=True, stop=True)
                    nc.tensor.matmul(bank[3 + g][:, :], vu[:, c * P:(c + 1) * P], hcols, start=True, stop=True)\
                        .then_inc(s_sgu, 1)

                def down(c):
                    pe.wait_ge(s_pr, START + i * SC + (c + 1))
                    if c == 0:
                        pe.wait_ge(s_x2s, START + i)
                    for j in range(TW):
                        last = nc.tensor.matmul(bank[6][:, j * P:(j + 1) * P], prs[:, c % 2, j * P:(j + 1) * P],
                                                vd[:, c, :], start=c == 0 and j == 0, stop=c == SC - 1,
                                                skip_group_check=True)
                    last.then_inc(s_sdown, 1)

                gate_up(0)
                for c in range(SC):
                    if c + 1 < SC:
                        gate_up(c + 1)
                    down(c)
            pe.wait_ge(s_x2s, START + NW)
            for n in range(NS0 // TW):
                pe.wait_ge(s_sorted[n * TW // QS0], START + 16)
                if n >= 4:
                    pe.wait_ge(s_srT, START + n - 3)
                for j in range(TW):
                    last = nc.tensor.transpose(bank[4 + n % 4][:, j * P:(j + 1) * P], sortd[:, n * TW + j, :],
                                               ident[:, :])
                last.then_inc(s_srtp, 1)
            pe.wait_ge(s_srT, START + NS0 // TW)

            def gate_up(j, u):
                pe.wait_ge(s_wst, START + j + 1)
                pe.wait_ge(s_pr, SHARED + reached(j - 3))
                cols = sortT[:, bass.ds(j * P, P)]
                for k in range(2):
                    last = nc.tensor.matmul(bank[u][:, k * P:(k + 1) * P], wst[:, u, k * D:(k + 1) * D], cols,
                                            start=True, stop=True)
                last.then_inc(s_sgu, 1)

            def turn(j, u, ahead):
                if ahead(2):
                    gate_up(j + 2, (u + 2) % 4)
                pe.wait_ge(s_pr, START + SHARED + j + 1)
                pe.wait_ge(s_yo, reached(j - 1))
                nc.tensor.matmul(bank[4 + u % 2][:, 0:D], hb0[:, u, :], wst[:, u, 2 * D:3 * D], start=True,
                                 stop=True).then_inc(s_yps0, 1)

            gate_up(0, 0)
            gate_up(1, 1)
            slot_turns(pe, turn)

        def logits_by_token(pe, n):
            pe.wait_ge(s_lgc, START + n + 1)
            for j in range(TW):
                at = (n * TW + j) * E0
                last = nc.tensor.transpose(bank[0][:, at:at + E0], lgT[:, n % 2, j * P:(j + 1) * P],
                                           ident[0:E0, 0:E0])
            last.then_inc(s_lg, 1)

        def act_experts0(act):
            act_layernorm(act, 1)
            for n in range(NW):
                act.wait_ge(s_lgT, START + n + 1)
                if n >= 2:
                    act.wait_ge(s_lg, START + n - 1)
                nc.scalar.activation(lgT[:, n % 2, :], bank[2 + n % 2][0:E0, :], ACT.Identity).then_inc(s_lgc, 1)
            act.wait_ge(s_route, START + 2)
            nc.scalar.activation(top[:, 1, :], top[:, 0, :], ACT.Tanh, scale=0.5).then_inc(s_score, 1)
            with act.Fori(0, NW) as i:
                for c in range(SC):
                    act.wait_ge(s_sgu, START + i * SC + (c + 1))
                    act.wait_ge(s_sg, START + i * SC + max(0, c - 1))
                    nc.scalar.activation(th[:, c % 2, :], bank[2 + 2 * (c % 2)][:, :], ACT.Tanh, scale=0.5)\
                        .then_inc(s_th, 1)
            for n in range(NS0 // TW):
                act.wait_ge(s_srtp, START + n + 1)
                nc.scalar.activation(sortT[:, n * W:(n + 1) * W], bank[4 + n % 4][:, :], ACT.Identity)\
                    .then_inc(s_srT, 1)

            def weights(j, u):
                act.wait_ge(s_yps0, reached(j - 3))
                offset = act.value_load(wofsi[0:1, bass.ds(j, 1)], min_val=0, max_val=(E0 - 1) * 3 * D)
                nc.scalar.activation(wst[:, u, :], wexp[:, bass.ds(offset, 3 * D)], ACT.Identity).then_inc(s_wst, 1)

            def tanh(j, u):
                act.wait_ge(s_sgu, START + SHARED + j + 1)
                act.wait_ge(s_pr, SHARED + reached(j - 3))
                nc.scalar.activation(th0[:, u, :], bank[u][:, 0:P], ACT.Tanh, scale=0.5).then_inc(s_th, 1)

            def turn(j, u, ahead):
                if ahead(3):
                    weights(j + 3, (u + 3) % 4)
                if ahead(1):
                    tanh(j + 1, (u + 1) % 4)

            act.wait_ge(s_slots, START + 1)
            for j in range(3):
                weights(j, j)
            tanh(0, 0)
            slot_turns(act, turn)

        def dve_experts0(dve):
            dve.wait_ge(s_x1, START + TAILS)
            dve_layernorm(dve, 1, 1)
            r = Chain(dve, s_route)
            dve.wait_ge(s_w0, START + W0_LOADS * 16)
            dve.wait_ge(s_lg, START + NW)
            bc = lambda a: a.unsqueeze(2).to_broadcast([P, NT, E0])
            r.step(nc.vector.tensor_copy(lg[:, :, :].rearrange("p n e -> p (n e)"), bank[0][:, :]))
            r.step(nc.vector.tensor_reduce(top[:, 0, :], lg[:, :, :], AX.X, ALU.max))
            r.step(nc.vector.tensor_tensor(eq[:, :, :], lg[:, :, :], bc(top[:, 0, :]), ALU.is_equal))
            r.step(nc.vector.tensor_tensor(eq[:, :, :], eq[:, :, :],
                                           prio[:, :].unsqueeze(1).to_broadcast([P, NT, E0]), ALU.mult))
            r.step(nc.vector.tensor_reduce(top[:, 2, :], eq[:, :, :], AX.X, ALU.max))
            by_token = lambda a: a.rearrange("p (n e) -> p n e", e=E0)
            by_expert = lambda a: a.rearrange("p (e n) -> p e n", n=NT)
            turned = lambda a: a.rearrange("p (e n) -> p n e", n=NT)
            nc.vector.tensor_tensor(by_token(onehot[:, :]), eq[:, :, :], bc(top[:, 2, :]), ALU.is_equal)\
                .then_inc(s_onehot, 1)
            q = Chain(dve, s_place)
            dve.wait_ge(s_count, START + 1)
            q.step(nc.vector.tensor_copy(by_expert(tot[:, :]), bank[6][:, :].rearrange("p (n e) -> p e n", e=E0)))
            q.step(nc.vector.tensor_tensor_scan(cum[:, :], keep0[:, :], tot[:, :], 0.0, ALU.mult, ALU.add))
            cmp_e = by_expert(cmp0[:, 0:E0 * NT])
            q.step(nc.vector.tensor_tensor(cmp_e, by_expert(cum[:, :])[:, :, NT - 1:NT].to_broadcast([P, E0, NT]),
                                           whole[:, :].unsqueeze(1).to_broadcast([P, E0, NT]), ALU.is_gt))
            q.step(nc.vector.tensor_reduce(etiles[:, 0, :], cmp_e, AX.X, ALU.add))
            q.step(nc.vector.tensor_tensor_scan(etiles[:, 1, :], keep0[:, 1:1 + E0], etiles[:, 0, :], 0.0, ALU.mult,
                                                ALU.add))
            q.mark(nc.vector.tensor_tensor(etiles[:, 2, :], etiles[:, 1, :], etiles[:, 0, :], ALU.subtract))
            cmp_j = cmp0[:, :].rearrange("p (j e) -> p j e", e=E0)
            shape = [P, NS0 + 4, E0]
            q.step(nc.vector.tensor_tensor(cmp_j, etiles[:, 1, :].unsqueeze(1).to_broadcast(shape),
                                           count0[:, :].unsqueeze(2).to_broadcast(shape), ALU.is_le))
            q.mark(nc.vector.tensor_scalar(etiles[:, 2, :], etiles[:, 2, :], float(P), None, ALU.mult))
            q.mark(nc.vector.tensor_reduce(wofs[:, 0, :], cmp_j, AX.X, ALU.add))
            q.step(nc.vector.tensor_tensor(cum[:, :], cum[:, :], tot[:, :], ALU.subtract))
            q.step(nc.vector.tensor_tensor(by_expert(cum[:, :]), by_expert(cum[:, :]),
                                           etiles[:, 2, :].unsqueeze(2).to_broadcast([P, E0, NT]), ALU.add))
            q.mark(nc.vector.tensor_scalar(wofs[:, 1, :], wofs[:, 0, :], float(E0 - 1), 3.0 * D, ALU.min, ALU.mult))
            q.step(nc.vector.tensor_tensor(by_token(slot[:, :]), by_token(bank[7][:, :]), turned(cum[:, :]), ALU.add))
            q.mark(nc.vector.tensor_copy(wofsi[:, :], wofs[:, 1, :]))
            q.step(nc.vector.tensor_tensor(slot[:, :], slot[:, :], onehot[:, :], ALU.mult))
            q.step(nc.vector.tensor_reduce(slotf[:, :], by_token(slot[:, :]), AX.X, ALU.add))
            q.mark(nc.vector.tensor_copy(slots[:, :], slotf[:, :]))
            dve.wait_ge(s_score, START + 1)
            r.step(nc.vector.tensor_scalar(top[:, 1, :], top[:, 1, :], 0.5, 0.5, ALU.mult, ALU.add))
            r.step(nc.vector.tensor_tensor(scale0[:, :], ln_rstd[:, :], top[:, 1, :], ALU.mult))
            for n in range(NT):
                last = nc.vector.tensor_scalar(rows[:, n, :], x[:, n * P:(n + 1) * P], ln_mean[:, n:n + 1],
                                               scale0[:, n:n + 1], ALU.subtract, ALU.mult)
            last.then_inc(s_slots, 1)
            with dve.Fori(0, NW) as i:
                for c in range(SC):
                    g = 2 * (c % 2)
                    dve.wait_ge(s_th, START + i * SC + (c + 1))
                    dve.wait_ge(s_pr, START + i * SC + c)
                    nc.vector.scalar_tensor_tensor(out=sg[:, :], in0=th[:, c % 2, :], scalar=1.0,
                                                   in1=bank[2 + g][:, :], op0=ALU.add, op1=ALU.mult).then_inc(s_sg, 1)
                    dve.wait_ge(s_sg, START + i * SC + (c + 1))
                    dve.wait_ge(s_sdown, START + i * SC + max(0, c - 1))
                    nc.vector.scalar_tensor_tensor(out=prs[:, c % 2, :], in0=sg[:, :], scalar=0.5,
                                                   in1=bank[3 + g][:, :], op0=ALU.mult, op1=ALU.mult)\
                        .then_inc(s_pr, 1)
                dve.wait_ge(s_sdown, START + i * SC + SC)
                nc.vector.tensor_tensor(tile4(x, i), tile4(x, i), bank[6][:, :], ALU.add).then_inc(s_x2s, 1)

            def gated(j, u):
                dve.wait_ge(s_th, START + SHARED + j + 1)
                dve.wait_ge(s_yps0, reached(j - 3))
                nc.vector.scalar_tensor_tensor(out=sg0[:, u, :], in0=th0[:, u, :], scalar=1.0, in1=bank[u][:, 0:P],
                                               op0=ALU.add, op1=ALU.mult).then_inc(s_sg, 1)
                dve.wait_ge(s_sg, START + SHARED + j + 1)
                nc.vector.scalar_tensor_tensor(out=hb0[:, u, :], in0=sg0[:, u, :], scalar=0.5,
                                               in1=bank[u][:, P:2 * P], op0=ALU.mult, op1=ALU.mult).then_inc(s_pr, 1)

            def turn(j, u, ahead):
                if ahead(1):
                    gated(j + 1, (u + 1) % 4)
                dve.wait_ge(s_yps0, START + j + 1)
                nc.vector.tensor_copy(sortd[:, bass.ds(j, 1), :].rearrange("p o f -> p (o f)"),
                                      bank[4 + u % 2][:, 0:D]).then_inc(s_yo, 1)

            dve.wait_ge(s_srT, START + NS0 // TW)
            gated(0, 0)
            slot_turns(dve, turn)
            for n in range(NW):
                dve.wait_ge(s_back[n // 2], NT // 4 * 16)
                xt = x[:, n * W:(n + 1) * W]
                nc.vector.tensor_tensor(xt, xt, rows[:, n * TW:(n + 1) * TW, :].rearrange("p n f -> p (n f)"),
                                        ALU.add).then_inc(s_x2, 1)

        def pool_experts0(pool):
            pool.wait_ge(s_x1, START + TAILS)
            nc.gpsimd.memset(sortd[:, :, :].rearrange("p j f -> p (j f)"), 0.0).then_inc(s_half, 1)
            pool_layernorm(pool, 1)
            pool.wait_ge(s_slots, START + 1)
            pool.wait_ge(s_zeroed, START + 16)
            for n in range(NT):
                pool.indirect_dma_start(slots_dram, bass.IndirectOffsetOnAxis(ap=slots[:, n:n + 1], axis=0),
                                        rows[:, n, :], None).then_inc(s_scat, 16)
            pool.wait_ge(s_scat, NT * 16)
            pool.wait_ge(s_ystored, START + 4 * 16)
            for n in range(NT):
                pool.indirect_dma_start(rows[:, n, :], None, outs_dram,
                                        bass.IndirectOffsetOnAxis(ap=slots[:, n:n + 1], axis=0))\
                    .then_inc(s_back[n // (NT // 4)], 16)

        BC = W // S
        SUMS = ((0, 2), (2, 3), (5, 4), (9, 5), (14, 6), (20, 6), (26, 6))
        PRODUCTS = ((0, 0), (0, 1), (1, 0), (1, 1), (0, 2), (2, 0))
        EMB, ATT, STA = range(3)

        def sp_recurrence(sp):
            sp.wait_ge(s_x2, START + NW)
            for name, dst in (("ctx_tok", ctx_tok[:, :, :]), ("Wf", Wf[:, :]), ("b_att", b_att[:, :]),
                              ("wx", wx[:, :, :]), ("Wh", Wh[:, :]), ("vrow", vrow[:, :]),
                              ("W2", W2[:, :, :]), ("b1c", b1c[:, :, :]), ("b2c", b2c[:, :, :]),
                              ("gsel", gsel[:, :, :]), ("own", own[:, :]), ("ones", ones[:, :])):
                sp.dma_start(dst, A[name]).then_inc(s_w1, 16)

        def pe_recurrence(pe):
            pe_layernorm(pe, 2)
            pe.wait_ge(s_w1, START + 12 * 16)
            for n in range(NW):
                pe.wait_ge(s_fT, START + max(0, n - 3))
                nc.tensor.matmul(bank[2 + n % 4][:, :], Wf[:, :], ctxT[:, n * W:(n + 1) * W], start=True,
                                 stop=True).then_inc(s_fps, 1)
            pe.wait_ge(s_wsc, START + WSC)
            pe.wait_ge(s_split, START + SPLITS * 2 + 3)
            pe.wait_ge(s_fT, START + NW)

            def keep_warm(count):
                for _ in range(count):
                    nc.tensor.matmul(bank[4][:, 0:W // 2], b1p[:, :], gsel[:, :, :].rearrange("p g b -> p (g b)"),
                                     start=True, stop=True, skip_group_check=True)

            def gates(which, parts, last_group, chosen=range(4)):
                for g in chosen:
                    for a, b in PRODUCTS:
                        last = nc.tensor.matmul(bank[3][:, g * B:(g + 1) * B],
                                                wx3[:, which, a, g * D:(g + 1) * D], parts(b), start=False,
                                                stop=last_group and (a, b) == PRODUCTS[-1], skip_group_check=True)
                return last

            with pe.Fori(0, S) as t:
                pe.wait_ge(s_tz, START + t)
                nc.tensor.matmul(bank[3][:, 0:4 * B], b1p[:, :], gsel[:, :, :].rearrange("p g b -> p (g b)"),
                                 start=True, stop=False, skip_group_check=True)
                gates(EMB, lambda b: e3[:, b, bass.ds(t * B, B)], False)
                keep_warm(4)
                nc.tensor.matmul(bank[1][0:B, 0:P], own[:, 0:B], own[:, B:B + P], start=True, stop=False)
                pe.wait_ge(s_h, START + t + 1)
                nc.tensor.matmul(bank[0][:, 0:B], Wh[:, :], state[:, :], start=True, stop=True).then_inc(s_hw, 1)
                keep_warm(8)
                for k, (n0, count) in enumerate(SUMS):
                    pe.wait_ge(s_ex, START + t * len(SUMS) + (k + 1))
                    for p in range(n0, n0 + count):
                        last = nc.tensor.matmul(bank[1][0:B, 0:P], vrow[:, B - 2 - 2 * p:2 * B - 2 - 2 * p],
                                                ex[:, 2 * p:2 * p + 2, :].rearrange("p b t -> p (b t)"),
                                                start=False, stop=p == NT - 1)
                last.then_inc(s_sc, 1)
                pe.wait_ge(s_st, START + 5 * t + 5)
                gates(STA, lambda b: st3[:, b, :], False, (0, 1))
                pe.wait_ge(s_al, START + t + 1)
                nc.tensor.transpose(bank[2][:, 0:P], al[:, :], ident[:, :]).then_inc(s_alT, 1)
                keep_warm(4)
                pe.wait_ge(s_alc, START + 4 * t + 4)
                for part in range(3):
                    last = nc.tensor.matmul(bank[7][:, 0:B], ones[:, :], alpha3[:, part, :], start=part == 0,
                                            stop=part == 2)
                last.then_inc(s_asum, 1)
                for p in range(NT):
                    for part in range(3):
                        last = nc.tensor.matmul(
                            bank[6][:, 0:3 * B].rearrange("p (c b) -> p c b", c=3)[:, 0:3 - part, 2 * p:2 * p + 2],
                            ctx3[:, part, p, :], alpha3[:, 0:3 - part, 2 * p:2 * p + 2], start=part == 0, stop=True,
                            skip_group_check=True)
                last.then_inc(s_attn, 1)
                gates(STA, lambda b: st3[:, b, :], False, (2, 3))
                keep_warm(8)
                pe.wait_ge(s_atc, START + 6 * t + 6)
                gates(ATT, lambda b: at3[:, b, :], True).then_inc(s_z, 1)
            pe.wait_ge(s_tz, START + S)
            pe.wait_ge(s_st, START + 5 * S + 1)
            pe.wait_ge(s_rs, START + S)
            pe.wait_ge(s_atc, START + 6 * S)
            with pe.Fori(0, NW) as i:
                pe.wait_ge(s_2t, START + i * 4)
                for g in range(4):
                    nc.tensor.matmul(bank[g][:, :], W2[:, 0, g * D:(g + 1) * D], Hall[:, bass.ds(i * W, W)],
                                     start=True, stop=True).then_inc(s_2z, 1)
            pe.wait_ge(s_h1, START + NW)
            for n in range(NW):
                if n >= 2:
                    pe.wait_ge(s_x3, START + n - 1)
                for j in range(TW):
                    p = n * TW + j
                    last = nc.tensor.transpose(bank[4 + n % 2][:, j * P:(j + 1) * P],
                                               fT[:, 2 * p:2 * p + 2, :].rearrange("p b t -> p (b t)"), ident[:, :])
                last.then_inc(s_h1T, 1)

        SPLITS = 2 * 4
        PIECE = T // 4
        WSC = 9

        def pieces():
            for n in range(4):
                cols = slice(n * PIECE, (n + 1) * PIECE)
                yield (Call[:, B:B + T][:, cols],
                       lambda k, cols=cols: ctx3[:, k, :, :].rearrange("p n f -> p (n f)")[:, cols])
            for n in range(4):
                cols = slice(n * PIECE, (n + 1) * PIECE)
                yield hT[:, cols], lambda k, cols=cols: e3[:, k, cols]

        def act_recurrence(act):
            act_layernorm(act, 2, by_position=True)
            act.wait_ge(s_w1, START + 12 * 16)
            for n in range(NW):
                act.wait_ge(s_fps, START + n + 1)
                nc.scalar.activation(fT[:, n * BC:(n + 1) * BC, :].rearrange("p b t -> p (b t)"),
                                     bank[2 + n % 4][:, :], ACT.Identity, bias=b_att[:, 0:1]).then_inc(s_fT, 1)
            act.wait_ge(s_hT, START + 3 * NW)
            todo = list(pieces())
            for n in range(SPLITS + 1):
                if n < SPLITS:
                    source, parts = todo[n]
                    nc.scalar.activation(parts(0), source, ACT.Identity).then_inc(s_splitA, 1)
                if n >= 1:
                    source, parts = todo[n - 1]
                    act.wait_ge(s_split, START + 2 * (n - 1) + 1)
                    nc.scalar.activation(parts(1), source, ACT.Identity).then_inc(s_splitA, 1)
            with act.Fori(0, S) as t:
                for k, (n0, count) in enumerate(SUMS):
                    act.wait_ge(s_pre, START + t * len(SUMS) + (k + 1))
                    e = ex[:, 2 * n0:2 * (n0 + count), :].rearrange("p b t -> p (b t)")
                    nc.scalar.activation(e, e, ACT.Tanh).then_inc(s_ex, 1)
                act.wait_ge(s_mx, START + t + 1)
                nc.scalar.activation(al[0:B, :], bank[1][0:B, 0:P], ACT.Exp, bias=nmx[:, 0:1]).then_inc(s_al, 1)
                act.wait_ge(s_z, START + t + 1)
                nc.scalar.activation(tz[:, :, :].rearrange("p g b -> p (g b)"), bank[3][:, 0:4 * B], ACT.Tanh)\
                    .then_inc(s_tz, 1)
                act.wait_ge(s_c, START + t + 1)
                nc.scalar.activation(tc[:, :], Call[:, bass.ds(t * B + B, B)], ACT.Tanh, scale=0.5)\
                    .then_inc(s_tc, 1)
            with act.Fori(0, NW) as i:
                act.wait_ge(s_h1, START + i)
                for g in range(4):
                    act.wait_ge(s_2z, START + i * 4 + (g + 1))
                    nc.scalar.activation(t2[:, g, :], bank[g][:, :], ACT.Tanh, bias=b2c[:, 0, g:g + 1],
                                         scale=0.25 if g < 3 else 0.5).then_inc(s_2t, 1)
                act.wait_ge(s_2c, START + i + 1)
                nc.scalar.activation(c2[:, 2, :], c2[:, 2, :], ACT.Tanh, scale=0.5).then_inc(s_2tc, 1)

        def dve_recurrence(dve):
            dve.wait_ge(s_x2, START + NW)
            dve_layernorm(dve, 2, 2)
            dve.wait_ge(s_w1, START + 12 * 16)
            sc = Chain(dve, s_wsc)
            sc.mark(nc.vector.tensor_tensor(b1r[:, :], b1c[:, 0, :], b1c[:, 1, :], ALU.add))
            sc.mark(nc.vector.tensor_tensor(b2c[:, 0, :], b2c[:, 0, :], b2c[:, 1, :], ALU.add))
            sc.mark(nc.vector.tensor_tensor(W2[:, 0, :], W2[:, 0, :], W2[:, 1, :], ALU.add))
            sc.mark(nc.vector.tensor_scalar(Wh[:, :], Wh[:, :], 0.5, None, ALU.mult))
            sc.step(nc.vector.tensor_scalar(wx[:, STA, :], wx[:, STA, :], 0.5, None, ALU.mult))
            sc.mark(nc.vector.tensor_scalar(b1r[0:3, :], b1r[0:3, :], 0.5, None, ALU.mult))
            sc.mark(nc.vector.tensor_scalar(b2c[:, 0, 0:3], b2c[:, 0, 0:3], 0.5, None, ALU.mult))
            nc.vector.memset(al[:, :], 0.0)
            nc.vector.memset(b1p[:, :].bitcast(F32), 0.0)
            nc.vector.memset(Call[:, 0:B], 0.0)
            sc.step(nc.vector.tensor_scalar(wx[:, :, 0:3 * D], wx[:, :, 0:3 * D], 0.5, None, ALU.mult))
            d = Chain(dve, s_bsplit)
            d.step(nc.vector.tensor_copy(b1p[0:4, :], b1r[:, :]))
            d.step(nc.vector.tensor_tensor(b1r[:, :], b1r[:, :], b1p[0:4, :], ALU.subtract))
            d.step(nc.vector.tensor_copy(b1p[32:36, :], b1r[:, :]))
            d.step(nc.vector.tensor_tensor(b1r[:, :], b1r[:, :], b1p[32:36, :], ALU.subtract))
            sc.mark(nc.vector.tensor_copy(b1p[64:68, :], b1r[:, :]))
            assert sc.n == WSC
            sp_ = Chain(dve, s_split)
            for n, (source, parts) in enumerate(pieces()):
                dve.wait_ge(s_splitA, START + max(1, 2 * n))
                sp_.mark(nc.vector.tensor_tensor(source, source, parts(0), ALU.subtract))
                dve.wait_ge(s_splitA, START + min(2 * n + 3, 2 * SPLITS))
                sp_.mark(nc.vector.tensor_tensor(parts(2), source, parts(1), ALU.subtract))
            sp_.step(nc.vector.tensor_copy(wx3[:, :, 0, :], wx[:, :, :]))
            sp_.step(nc.vector.tensor_tensor(wx[:, :, :], wx[:, :, :], wx3[:, :, 0, :], ALU.subtract))
            nc.vector.tensor_copy(wx3[:, :, 1, :], wx[:, :, :]).then_inc(s_bsplit, 1)
            dve.wait_ge(s_bsplit, START + 5)
            sp_.mark(nc.vector.tensor_tensor(wx3[:, :, 2, :], wx[:, :, :], wx3[:, :, 1, :], ALU.subtract))
            dve.wait_ge(s_split, START + 2 * SPLITS + 3)
            nc.vector.memset(state[:, :], 0.0).then_inc(s_h, 1)
            dve.wait_ge(s_fT, START + NW)
            cell = Chain(dve, s_cell, per_turn=2)
            alc = Chain(dve, s_alc, per_turn=4)
            atc = Chain(dve, s_atc, per_turn=6)
            with dve.Fori(0, S) as t:
                for chain in (cell, alc, atc):
                    chain.turn(t)
                dve.wait_ge(s_hw, START + t + 1)
                dve.wait_ge(s_sc, START + t)
                for n0, count in SUMS:
                    bs = slice(2 * n0, 2 * (n0 + count))
                    nc.vector.tensor_tensor(ex[:, bs, :], fT[:, bs, :],
                                            bank[0][:, bs].unsqueeze(2).to_broadcast([P, 2 * count, S]), ALU.add)\
                        .then_inc(s_pre, 1)
                dve.wait_ge(s_sc, START + t + 1)
                nc.vector.tensor_reduce(nmx[:, :], bank[1][0:B, 0:P], AX.X, ALU.max, negate=True).then_inc(s_mx, 1)
                dve.wait_ge(s_alT, START + t + 1)
                dve.wait_ge(s_attn, START + t)
                alc.step(nc.vector.tensor_copy(alpha3[:, 0, :], bank[2][:, 0:B]))
                alc.step(nc.vector.tensor_tensor(alrest[:, :], bank[2][:, 0:B], alpha3[:, 0, :], ALU.subtract))
                alc.step(nc.vector.tensor_copy(alpha3[:, 1, :], alrest[:, :]))
                alc.mark(nc.vector.tensor_tensor(alpha3[:, 2, :], alrest[:, :], alpha3[:, 1, :], ALU.subtract))
                alc.ended()
                dve.wait_ge(s_asum, START + t + 1)
                nc.vector.reciprocal(rs[:, :], bank[7][:, 0:B]).then_inc(s_rs, 1)
                dve.wait_ge(s_rs, START + t + 1)
                dve.wait_ge(s_attn, START + t + 1)
                atc.step(nc.vector.tensor_reduce(at[:, 0, :], bank[6][:, 0:3 * B].rearrange("p (c b) -> p b c", c=3),
                                                 AX.X, ALU.add))
                atc.step(nc.vector.tensor_tensor(at[:, 1, :], at[:, 0, :], rs[:, :], ALU.mult))
                atc.step(nc.vector.tensor_copy(at3[:, 0, :], at[:, 1, :]))
                atc.step(nc.vector.tensor_tensor(at[:, 2, :], at[:, 1, :], at3[:, 0, :], ALU.subtract))
                atc.step(nc.vector.tensor_copy(at3[:, 1, :], at[:, 2, :]))
                atc.mark(nc.vector.tensor_tensor(at3[:, 2, :], at[:, 2, :], at3[:, 1, :], ALU.subtract))
                atc.ended()
                dve.wait_ge(s_tz, START + t + 1)
                cell.mark(nc.vector.scalar_tensor_tensor(out=ca[:, 0, :], in0=tz[:, 1, :], scalar=1.0,
                                                         in1=Call[:, bass.ds(t * B, B)], op0=ALU.add, op1=ALU.mult))
                cell.step(nc.vector.scalar_tensor_tensor(out=ca[:, 1, :], in0=tz[:, 0, :], scalar=1.0,
                                                         in1=tz[:, 3, :], op0=ALU.add, op1=ALU.mult))
                cell.ended()
                nc.vector.scalar_tensor_tensor(out=Call[:, bass.ds(t * B + B, B)], in0=ca[:, 0, :], scalar=0.5,
                                               in1=ca[:, 1, :], op0=ALU.mult, op1=ALU.add).then_inc(s_c, 1)
                dve.wait_ge(s_tc, START + t + 1)
                dve.wait_ge(s_st, START + 5 * t + 5)
                nc.vector.scalar_tensor_tensor(out=state[:, :], in0=tz[:, 2, :], scalar=1.0,
                                               in1=tc[:, :], op0=ALU.add, op1=ALU.mult).then_inc(s_h, 1)
            d2 = Chain(dve, s_2d, per_turn=2)
            h1 = fT[:, :, :].rearrange("p b t -> p t b")
            with dve.Fori(0, NW) as i:
                d2.turn(i)
                dve.wait_ge(s_2t, START + i * 4 + 4)
                dve.wait_ge(s_h1, START + i)
                d2.mark(nc.vector.scalar_tensor_tensor(out=c2[:, 0, :], in0=t2[:, 1, :], scalar=1.0,
                                                       in1=Call[:, bass.ds(i * W + B, W)], op0=ALU.add, op1=ALU.mult))
                d2.step(nc.vector.scalar_tensor_tensor(out=c2[:, 1, :], in0=t2[:, 0, :], scalar=1.0,
                                                       in1=t2[:, 3, :], op0=ALU.add, op1=ALU.mult))
                nc.vector.scalar_tensor_tensor(out=c2[:, 2, :], in0=c2[:, 0, :], scalar=0.5,
                                               in1=c2[:, 1, :], op0=ALU.mult, op1=ALU.add).then_inc(s_2c, 1)
                dve.wait_ge(s_2tc, START + i + 1)
                tb = lambda a: a.rearrange("p (t b) -> p t b", b=B)
                nc.vector.scalar_tensor_tensor(out=h1[:, bass.ds(i * BC, BC), :], in0=tb(t2[:, 2, :]), scalar=1.0,
                                               in1=tb(c2[:, 2, :]), op0=ALU.add, op1=ALU.mult).then_inc(s_h1, 1)
            for n in range(NW):
                dve.wait_ge(s_h1T, START + n + 1)
                xt = x[:, n * W:(n + 1) * W]
                nc.vector.scalar_tensor_tensor(out=xt, in0=bank[4 + n % 2][:, :], scalar=0.5, in1=xt,
                                               op0=ALU.mult, op1=ALU.add).then_inc(s_x3, 1)

        def pool_recurrence(pool):
            pool_layernorm(pool, 2)
            st = Chain(pool, s_st, per_turn=5)

            def split_state():
                st.step(nc.gpsimd.tensor_tensor(st3[:, 0, :], state[:, :], unit[:, :], ALU.mult))
                st.step(nc.gpsimd.tensor_tensor(strest[:, :], state[:, :], st3[:, 0, :], ALU.subtract))
                st.step(nc.gpsimd.tensor_tensor(st3[:, 1, :], strest[:, :], unit[:, :], ALU.mult))
                st.step(nc.gpsimd.tensor_tensor(st3[:, 2, :], strest[:, :], st3[:, 1, :], ALU.subtract))

            pool.wait_ge(s_x2, START + NW)
            nc.gpsimd.memset(unit[:, :], 1.0).then_inc(s_half, 1)
            pool.wait_ge(s_half, START + 3)
            pool.wait_ge(s_h, START + 1)
            split_state()
            st.step(nc.gpsimd.tensor_tensor(strest[:, :], state[:, :], unit[:, :], ALU.mult))
            with pool.Fori(0, S) as t:
                st.turn(t + 1)
                pool.wait_ge(s_h, START + t + 2)
                st.step(nc.gpsimd.tensor_tensor(Hall[:, bass.ds(t * B, B)], state[:, :], unit[:, :], ALU.mult))
                pool.wait_ge(s_z, START + t + 1)
                split_state()
                st.ended()

        HP1 = H1 // 2
        VW = 2 * (DH1 + 1)

        def sp_attention1(sp):
            for name, dst in (("wqkv", wqkv[:, :]), ("wo", wo[:, :]), ("gw1", gw1[:, :]), ("fc1", fc1[:, :, :]),
                              ("fc2", fc2[:, :, :, :]), ("fc1b", fc1b[:, :, :]), ("fc2b", fc2b[:, :]),
                              ("cols1", cols1[:, :]), ("bo1", bo1[:, :]), ("headmask1", headmask1[:, :]),
                              ("causal", causal1[:, :]), ("prio1", prio1[:, :]), ("sel1", sel1[:, :, :])):
                sp.dma_start(dst, A[name]).then_inc(s_wl1, 16)

        def pe_attention1(pe):
            pe_layernorm(pe, 3)
            for n in range(NW):
                pe.wait_ge(s_hT, START + 3 * NW + n + 1)
                for g in range(2):
                    if n >= 1:
                        pe.wait_ge(s_qkT, START + 2 * n + g - 1)
                    nc.tensor.matmul(bank[2 + g][:, :], wqkv[:, g * D:(g + 1) * D], hT[:, n * W:(n + 1) * W],
                                     start=True, stop=True).then_inc(s_qkp, 1)
            pe.wait_ge(s_bo, START + 2)
            nc.tensor.matmul(bank[4][:, 0:D], bvx[:, :], wo[:, :], start=True, stop=False)
            nc.tensor.matmul(bank[4][:, 0:D], ones1[:, :], bo1[:, :], start=False, stop=True).then_inc(s_bop, 1)
            pe.wait_ge(s_bob, START + 1)

            def values(i, u):
                pe.wait_ge(s_nst, START + i + 1)
                pe.wait_ge(s_vh, reached(i))
                pe.wait_ge(s_x4, reached(i - 2))
                for b in range(2):
                    last = nc.tensor.matmul(bank[6][:, b * D:(b + 1) * D],
                                            nst[:, u, b, :, :].rearrange("p a t -> p (a t)"), wqkv[:, 2 * D:3 * D],
                                            start=True, stop=True)
                last.then_inc(s_vps, 1)

            def score_half(i, u, b, n):
                return nc.tensor.matmul(
                    bank[2 * u + n][b * S:b * S + S, :], qst[:, u, b, :],
                    kblk1[:, u, b, n * (H1 // 2):(n + 1) * (H1 // 2), :].rearrange("p h t -> p (h t)"),
                    start=True, stop=False, skip_group_check=True)

            def scores_first(i, u):
                pe.wait_ge(s_qst, START + i + 1)
                pe.wait_ge(s_kbD, START + i + 1)
                pe.wait_ge(s_ssub, reached(2 * (i - 2) + 2))
                for n in range(2):
                    score_half(i, u, 0, n)

            def scores_second(i, u, between):
                pe.wait_ge(s_kbP, START + i + 1)
                score_half(i, u, 1, 0)
                between()
                score_half(i, u, 1, 1).then_inc(s_kq, 1)
                for n in range(2):
                    last = nc.tensor.matmul(bank[2 * u + n][:, :], ident_bf[:, :], causal1[:, :], start=False,
                                            stop=True, skip_group_check=True)
                last.then_inc(s_scr, 1)

            def transposed(i, u):
                pe.wait_ge(s_prb, START + i + 1)
                pe.wait_ge(s_prT, reached(2 * i))
                for hp in range(HP1):
                    last = nc.tensor.transpose(bank[4 + hp // 4][:, (hp % 4) * P:(hp % 4 + 1) * P],
                                               prb[:, u, 2 * hp:2 * hp + 2, :].rearrange("p h t -> p (h t)"),
                                               ident[:, :])
                last.then_inc(s_prTp, 1)

            def attended(i, u):
                pe.wait_ge(s_prT, START + 2 * i + 2)
                pe.wait_ge(s_vh, START + i + 1)
                pe.wait_ge(s_att, reached(i))
                for b in range(2):
                    for hp in range(HP1):
                        last = nc.tensor.matmul(bank[7][b * S:b * S + S, hp * VW:(hp + 1) * VW],
                                                prT[:, u, hp, b * S:b * S + S],
                                                vh[:, u, b, hp, :, :].rearrange("p h d -> p (h d)"),
                                                start=True, stop=True)
                last.then_inc(s_pv1, 1)

            def heads_turned(i, u, values_read):
                pe.wait_ge(s_att, START + i + 1)
                pe.wait_ge(s_vh, START + values_read)
                nc.tensor.transpose(bank[6][:, 2 * D:2 * D + P], att[:, u, :, :].rearrange("p h d -> p (h d)"),
                                    ident[:, :]).then_inc(s_attTp, 1)

            def out_product(i, u):
                pe.wait_ge(s_attT, START + i + 1)
                nc.tensor.matmul(bank[6][:, 3 * D:4 * D], attT[:, u, :], wo[:, :], start=True, stop=True)\
                    .then_inc(s_wop, 1)

            def turn(i, u, first=False):
                values(i + 1, 1 - u)
                scores_first(i + 1, 1 - u)
                transposed(i, u)
                if not first:
                    heads_turned(i - 1, 1 - u, i + 2)
                scores_second(i + 1, 1 - u, lambda: None if first else out_product(i - 1, 1 - u))
                attended(i, u)

            values(0, 0)
            scores_first(0, 0)
            scores_second(0, 0, lambda: None)
            turn(0, 0, first=True)
            with pe.Fori(0, NT // 2 - 1) as j:
                for v in range(2):
                    turn(2 * j + (1 + v), 1 - v)
            transposed(NT - 1, 1)
            heads_turned(NT - 2, 0, NT)
            out_product(NT - 2, 0)
            attended(NT - 1, 1)
            pe.wait_ge(s_x4, START + NT - 1)
            heads_turned(NT - 1, 1, NT)
            out_product(NT - 1, 1)

        def act_attention1(act):
            act.wait_ge(s_wl1, START + 13 * 16)
            act_layernorm(act, 3, scale=cols1[:, 0:1], bias=cols1[:, 1:2])
            act.wait_ge(s_bo, START + 2)
            for n in range(NW):
                for g, dst in enumerate((qT, kT)):
                    act.wait_ge(s_qkp, START + 2 * n + g + 1)
                    nc.scalar.activation(dst[:, n * W:(n + 1) * W], bank[2 + g][:, :], ACT.Identity,
                                         bias=cols1[:, 4 + g:5 + g], scale=DH1 ** -0.5 if g == 0 else 1.0)\
                        .then_inc(s_qkT, 1)
            act.wait_ge(s_bop, START + 1)
            nc.scalar.activation(bob[:, :], bank[4][:, 0:D], ACT.Identity).then_inc(s_bob, 1)

            def operands(i, u):
                act.wait_ge(s_vps, reached(i - 1))
                act.wait_ge(s_kq, reached(i - 1))
                src = hT[:, bass.ds(i * P, P)].rearrange("p (b t) -> p b t", b=2)
                nc.scalar.activation(nst[:, u, :, :, :], src.unsqueeze(2).to_broadcast([P, 2, 2, S]), ACT.Identity)\
                    .then_inc(s_nst, 1)
                nc.scalar.activation(qst[:, u, :, :].rearrange("p b s -> p (b s)"), qT[:, bass.ds(i * P, P)],
                                     ACT.Identity).then_inc(s_qst, 1)

            def exponentials(i, u):
                act.wait_ge(s_ssub, START + 2 * i + 2)
                pr = prb[:, u, :, :].rearrange("p h t -> p (h t)")
                nc.scalar.activation(pr, pr, ACT.Exp).then_inc(s_prb, 1)

            def transposed(i, u):
                act.wait_ge(s_prTp, START + i + 1)
                act.wait_ge(s_pv1, reached(i - 1))
                for n in range(2):
                    nc.scalar.activation(prT[:, u, 4 * n:4 * n + 4, :].rearrange("p h s -> p (h s)"),
                                         bank[4 + n][:, :], ACT.Identity).then_inc(s_prT, 1)

            def heads_turned(i, u):
                act.wait_ge(s_attTp, START + i + 1)
                act.wait_ge(s_wop, reached(i - 1))
                nc.scalar.activation(attT[:, u, :], bank[6][:, 2 * D:2 * D + P], ACT.Identity).then_inc(s_attT, 1)

            operands(0, 0)
            operands(1, 1)
            exponentials(0, 0)
            operands(2, 0)
            transposed(0, 0)
            exponentials(1, 1)

            def turn(i, u, prepare=True):
                if prepare:
                    operands(i + 2, u)
                transposed(i, u)
                heads_turned(i - 1, 1 - u)
                exponentials(i + 1, 1 - u)

            with act.Fori(0, NT // 2 - 2) as j:
                for v in range(2):
                    turn(2 * j + (1 + v), 1 - v)
            turn(NT - 3, 1)
            turn(NT - 2, 0, prepare=False)
            transposed(NT - 1, 1)
            heads_turned(NT - 2, 0)
            heads_turned(NT - 1, 1)

        def dve_attention1(dve):
            dve.wait_ge(s_x3, START + NW)
            dve_statistics(dve, 3)
            dve.wait_ge(s_x3c, START + 1)
            with dve.Fori(0, NW) as i:
                for j in range(TW):
                    xt = x[:, bass.ds(i * W + j * P, P)]
                    last = nc.vector.tensor_scalar(xt, xt, ln_mean[:, bass.ds(i * TW + j, 1)],
                                                   ln_rstd[:, bass.ds(i * TW + j, 1)], ALU.subtract, ALU.mult)
                last.then_inc(s_y, 1)
            dve.wait_ge(s_y, START + NW)
            dve_layernorm(dve, 3, 4)
            dve.wait_ge(s_wl1, START + 13 * 16)
            dve.wait_ge(s_x3, START + NW)
            nc.vector.memset(ones1[:, :], 1.0)
            nc.vector.tensor_copy(bvx[:, :], cols1[:, 6:7].to_broadcast([P, P])).then_inc(s_bo, 1)
            nc.vector.tensor_scalar(cols1[:, 4:5], cols1[:, 4:5], DH1 ** -0.5, None, ALU.mult).then_inc(s_bo, 1)
            nc.vector.memset(vh[:, :, :, :, :, :].rearrange("p a b c d e -> p (a b c d e)"), 0.0)\
                .then_inc(s_a1init, 1)
            dve.wait_ge(s_a1init, START + 1)
            for h2 in range(2):
                last = nc.vector.memset(vh[S * h2:S * h2 + S, :, :, :, h2, DH1:DH1 + 1], 1.0)
            last.then_inc(s_a1init, 1)
            dve.wait_ge(s_a1init, START + 2)
            dve.wait_ge(s_bob, START + 1)
            nc.vector.tensor_tensor(x[:, :].rearrange("p (n f) -> p n f", f=D),
                                    x[:, :].rearrange("p (n f) -> p n f", f=D),
                                    bob[:, :].unsqueeze(1).to_broadcast([P, NT, D]), ALU.add).then_inc(s_a1init, 1)
            dve.wait_ge(s_a1init, START + 3)
            dve.wait_ge(s_qkT, START + 2 * NW)

            def keys(i, u):
                dve.wait_ge(s_kq, reached(i - 1))
                nc.vector.tensor_tensor(kblk1[:, u, 0, :, :],
                                        kT[:, bass.ds(i * P, S)].unsqueeze(1).to_broadcast([P, H1, S]),
                                        headmask1[:, :].unsqueeze(2).to_broadcast([P, H1, S]), ALU.mult)\
                    .then_inc(s_kbD, 1)

            def values(i, u):
                dve.wait_ge(s_vps, START + i + 1)
                dve.wait_ge(s_pv1, reached(i - 1))
                for h2 in range(2):
                    rows = slice(S * h2, S * h2 + S)
                    src = bank[6][rows, 0:2 * D].rearrange("p (b h two d) -> p b h two d", b=2, two=2, d=DH1)
                    last = nc.vector.tensor_copy(vh[rows, u, :, :, h2, 0:DH1], src[:, :, :, h2, :])
                last.then_inc(s_vh, 1)

            def scores(i, u):
                dve.wait_ge(s_scr, START + i + 1)
                dve.wait_ge(s_prTp, reached(i - 1))
                for n in range(2):
                    nc.vector.tensor_reduce(smax[:, u, n * 8:n * 8 + 8],
                                            bank[2 * u + n][:, :].rearrange("p (h t) -> p h t", t=S), AX.X, ALU.max)\
                        .then_inc(s_smax, 1)
                for n in range(2):
                    dve.wait_ge(s_smax, START + 2 * i + (n + 1))
                    nc.vector.tensor_tensor(prb[:, u, n * 8:n * 8 + 8, :],
                                            bank[2 * u + n][:, :].rearrange("p (h t) -> p h t", t=S),
                                            smax[:, u, n * 8:n * 8 + 8].unsqueeze(2).to_broadcast([P, 8, S]),
                                            ALU.subtract).then_inc(s_ssub, 1)

            def attended(i, u):
                dve.wait_ge(s_pv1, START + i + 1)
                dve.wait_ge(s_attTp, reached(i - 1))
                o = bank[7][:, 0:HP1 * VW].rearrange("p (h d) -> p h d", d=DH1 + 1)
                nc.vector.reciprocal(asum[:, u, :], o[:, :, DH1]).then_inc(s_asum1, 1)
                dve.wait_ge(s_asum1, START + i + 1)
                nc.vector.tensor_tensor(att[:, u, :, :], o[:, :, 0:DH1],
                                        asum[:, u, :].unsqueeze(2).to_broadcast([P, H1, DH1]), ALU.mult)\
                    .then_inc(s_att, 1)

            def onto_stream(i):
                dve.wait_ge(s_wop, START + i + 1)
                xt = x[:, bass.ds(i * D, D)]
                nc.vector.tensor_tensor(xt, xt, bank[6][:, 3 * D:4 * D], ALU.add).then_inc(s_x4, 1)

            keys(0, 0)
            values(0, 0)
            keys(1, 1)
            scores(0, 0)
            values(1, 1)
            keys(2, 0)
            scores(1, 1)
            attended(0, 0)

            def turn(i, u, prepare=True):
                values(i + 1, 1 - u)
                if prepare:
                    keys(i + 2, u)
                onto_stream(i - 1)
                scores(i + 1, 1 - u)
                attended(i, u)

            with dve.Fori(0, NT // 2 - 2) as j:
                for v in range(2):
                    turn(2 * j + (1 + v), 1 - v)
            turn(NT - 3, 1)
            turn(NT - 2, 0, prepare=False)
            onto_stream(NT - 2)
            attended(NT - 1, 1)
            onto_stream(NT - 1)

        def pool_attention1(pool):
            pool.wait_ge(s_x3, START + NW)
            nc.gpsimd.tensor_copy(x3[:, :], x[:, :]).then_inc(s_x3c, 1)
            pool_layernorm(pool, 3)
            pool_layernorm(pool, 4)
            pool.wait_ge(s_qkT, START + 2 * NW)

            def keys(i, u):
                pool.wait_ge(s_kq, reached(i - 1))
                nc.gpsimd.tensor_tensor(kblk1[:, u, 1, :, :],
                                        kT[:, bass.ds(i * P + S, S)].unsqueeze(1).to_broadcast([P, H1, S]),
                                        headmask1[:, :].unsqueeze(2).to_broadcast([P, H1, S]), ALU.mult)\
                    .then_inc(s_kbP, 1)

            keys(0, 0)
            keys(1, 1)
            with pool.Fori(1, NT // 2) as j:
                for u in range(2):
                    keys(2 * j + u, u)

        C1 = F1 // P
        UNITS = E1 * C1

        def pe_experts1(pe):
            pe_layernorm(pe, 4)

            def by_token(n):
                pe.wait_ge(s_lgc1, START + n + 1)
                for j in range(TW):
                    at_ = (n * TW + j) * E1
                    last = nc.tensor.transpose(bank[0][:, at_:at_ + E1], lgT1[:, n % 2, j * P:(j + 1) * P],
                                               ident[0:E1, 0:E1])
                last.then_inc(s_lg1, 1)

            for n in range(NW):
                pe.wait_ge(s_hT, START + 4 * NW + n + 1)
                if n >= 2:
                    pe.wait_ge(s_lgc1, START + n - 1)
                nc.tensor.matmul(bank[2 + n % 2][0:E1, :], gw1[:, :], hT[:, n * W:(n + 1) * W], start=True,
                                 stop=True).then_inc(s_lgT1, 1)
                if n >= 1:
                    by_token(n - 1)
            by_token(NW - 1)
            pe.wait_ge(s_rt1, START + 1)
            per = NT // 4
            for n in range(NT):
                last = nc.tensor.transpose(bank[4 + n // per][:, :].bitcast(BF16)[:, (n % per) * P:(n % per + 1) * P],
                                           route1[:, n, :], ident_bf[:, :])
                if n % per == per - 1:
                    last.then_inc(s_rtp1, 1)
            pe.wait_ge(s_routeT1, START + 4)
            with pe.Fori(0, NW) as i:
                hcols = hT[:, bass.ds(i * W, W)]
                rcols = routeT1[:, bass.ds(i * W, W)]

                def first(u):
                    e, c = u // C1, u % C1
                    pe.wait_ge(s_hid, START + i * UNITS + max(0, u - 3))
                    nc.tensor.matmul(bank[u % 4][:, :], fc1[:, e, c * P:(c + 1) * P], hcols, start=True, stop=True)\
                        .then_inc(s_hps, 1)

                def second(u):
                    e, c = u // C1, u % C1
                    if c == 0:
                        pe.wait_ge(s_gbs, START + i * E1 + e)
                        nc.tensor.matmul(bank[6][:, :], sel1[:, e, :], rcols, start=True, stop=True)\
                            .then_inc(s_gb, 1)
                        pe.wait_ge(s_yg, START + i * E1 + max(0, e - 1))
                    pe.wait_ge(s_hid, START + i * UNITS + (u + 1))
                    last = nc.tensor.matmul(bank[4 + e % 2][:, :], fc2[:, e, c, :], hid[:, u % 4, :], start=c == 0,
                                            stop=c == C1 - 1)
                    last.then_inc(s_yps, 1)

                for u in range(UNITS + 2):
                    if u < UNITS:
                        first(u)
                    if u >= 2:
                        second(u - 2)
                pe.wait_ge(s_acc, START + i * (E1 - 1) + (E1 - 1))
                pe.wait_ge(s_x5, START + i)
                for j in range(TW):
                    last = nc.tensor.transpose(bank[7][:, j * P:(j + 1) * P], acc[:, j * P:(j + 1) * P], ident[:, :])
                last.then_inc(s_accT, 1)

        def act_experts1(act):
            act_layernorm(act, 4, scale=cols1[:, 2:3], bias=cols1[:, 3:4])
            for n in range(NW):
                act.wait_ge(s_lgT1, START + n + 1)
                if n >= 2:
                    act.wait_ge(s_lg1, START + n - 1)
                nc.scalar.activation(lgT1[:, n % 2, :], bank[2 + n % 2][0:E1, :], ACT.Identity).then_inc(s_lgc1, 1)
            act.wait_ge(s_top1, START + 1)
            nc.scalar.activation(top1[:, 4, :], top1[:, 4, :], ACT.Exp).then_inc(s_score, 1)
            for n in range(4):
                act.wait_ge(s_rtp1, START + n + 1)
                nc.scalar.activation(routeT1[:, n * 2 * W:(n + 1) * 2 * W], bank[4 + n][:, :].bitcast(BF16),
                                     ACT.Identity).then_inc(s_routeT1, 1)
            with act.Fori(0, NW) as i:
                def gate(e):
                    act.wait_ge(s_gb, START + i * E1 + (e + 1))
                    act.wait_ge(s_yg, START + i * E1 + max(0, e - 1))
                    nc.scalar.activation(gbs[:, e % 2, :], bank[6][:, :], ACT.Identity).then_inc(s_gbs, 1)

                for u in range(UNITS):
                    act.wait_ge(s_hps, START + i * UNITS + (u + 1))
                    act.wait_ge(s_yps, START + i * UNITS + max(0, u - 3))
                    nc.scalar.activation(hid[:, u % 4, :], bank[u % 4][:, :], ACT.Gelu,
                                         bias=fc1b[:, u // C1, u % C1:u % C1 + 1]).then_inc(s_hid, 1)
                    if u % C1 == 2:
                        gate(u // C1)

        def dve_experts1(dve):
            dve.wait_ge(s_x4, START + NT)
            dve_layernorm(dve, 4, 5)
            r = Chain(dve, s_route1)
            dve.wait_ge(s_lg1, START + NW)
            flat = lambda a: a.rearrange("p n e -> p (n e)")
            bc = lambda a: a.unsqueeze(2).to_broadcast([P, NT, E1])
            pr = prio1[:, :].unsqueeze(1).to_broadcast([P, NT, E1])
            r.mark(nc.vector.memset(flat(route1[:, :, :]).bitcast(F32), 0.0))
            r.step(nc.vector.tensor_copy(flat(lg1[:, :, :]), bank[0][:, 0:NT * E1]))
            for k in range(2):
                chosen = sc1[:, k, :, :]
                r.step(nc.vector.tensor_reduce(top1[:, k, :], lg1[:, :, :], AX.X, ALU.max))
                r.step(nc.vector.tensor_tensor(chosen, lg1[:, :, :], bc(top1[:, k, :]), ALU.is_equal))
                r.step(nc.vector.tensor_tensor(chosen, chosen, pr, ALU.mult))
                r.step(nc.vector.tensor_reduce(top1[:, 2, :], chosen, AX.X, ALU.max))
                r.step(nc.vector.tensor_tensor(chosen, chosen, bc(top1[:, 2, :]), ALU.is_equal))
                if k == 0:
                    r.step(nc.vector.scalar_tensor_tensor(out=flat(lg1[:, :, :]), in0=flat(chosen), scalar=NEVER,
                                                          in1=flat(lg1[:, :, :]), op0=ALU.mult, op1=ALU.add))
            nc.vector.tensor_tensor(top1[:, 4, :], top1[:, 1, :], top1[:, 0, :], ALU.subtract).then_inc(s_top1, 1)
            dve.wait_ge(s_score, START + 2)
            r.step(nc.vector.tensor_scalar(top1[:, 3, :], top1[:, 4, :], 1.0, None, ALU.add))
            r.step(nc.vector.reciprocal(top1[:, 3, :], top1[:, 3, :]))
            r.step(nc.vector.tensor_tensor(top1[:, 5, :], top1[:, 3, :], top1[:, 4, :], ALU.mult))
            r.step(nc.vector.tensor_tensor(sc1[:, 0, :, :], sc1[:, 0, :, :], bc(top1[:, 3, :]), ALU.mult))
            r.step(nc.vector.tensor_tensor(sc1[:, 1, :, :], sc1[:, 1, :, :], bc(top1[:, 5, :]), ALU.mult))
            r.step(nc.vector.tensor_tensor(sc1[:, 0, :, :], sc1[:, 0, :, :], sc1[:, 1, :, :], ALU.add))
            part = lambda n: route1[:, :, n * E1:(n + 1) * E1]
            r.step(nc.vector.tensor_copy(part(0), sc1[:, 0, :, :]))
            r.step(nc.vector.tensor_tensor(sc1[:, 2, :, :], sc1[:, 0, :, :], part(0), ALU.subtract))
            r.step(nc.vector.tensor_copy(part(1), sc1[:, 2, :, :]))
            nc.vector.tensor_tensor(part(2), sc1[:, 2, :, :], part(1), ALU.subtract).then_inc(s_rt1, 1)
            dve.wait_ge(s_x3c, START + 2)
            with dve.Fori(0, NW) as i:
                for e in range(E1):
                    dve.wait_ge(s_yps, START + i * UNITS + C1 * (e + 1))
                    dve.wait_ge(s_gbs, START + i * E1 + (e + 1))
                    if e == 0:
                        dve.wait_ge(s_accT, START + i)
                    dst = acc[:, :] if e == 0 else yg[:, e % 2, :]
                    nc.vector.scalar_tensor_tensor(out=dst, in0=bank[4 + e % 2][:, :], scalar=fc2b[:, e:e + 1],
                                                   in1=gbs[:, e % 2, :], op0=ALU.add, op1=ALU.mult)\
                        .then_inc(s_yg, 1)
                    dve.wait_ge(s_yg, START + i * E1 + (e + 1))
                    if e == 0:
                        continue
                    dve.wait_ge(s_acc, START + i * (E1 - 1) + (e - 1))
                    nc.vector.tensor_tensor(acc[:, :], acc[:, :], yg[:, e % 2, :], ALU.add).then_inc(s_acc, 1)
                dve.wait_ge(s_accT, START + i + 1)
                nc.vector.tensor_tensor(tile4(x, i), tile4(x, i), bank[7][:, :], ALU.add).then_inc(s_x5, 1)

        def pool_experts1(pool):
            pool_layernorm(pool, 5)
            pool.wait_ge(s_lnout, START + 5 * NW)
            nc.gpsimd.tensor_tensor(x[:, :], x[:, :], x3[:, :], ALU.add).then_inc(s_x3c, 1)

        last_stage = [(s_x1, TAILS), (s_x2, NW), (s_x3, NW), (s_x5, NW)][:stages]
        @block.sync
        def _(sp):
            sp_mixer(sp)
            if stages >= 2:
                sp_slots0(sp)
            if stages >= 3:
                sp_recurrence(sp)
            if stages >= 4:
                sp_attention1(sp)
            sp.wait_ge(last_stage[-1][0], START + last_stage[-1][1])
            sp.dma_start(out, x[:, :]).then_inc(s_out, 16)
            sp.wait_ge(s_out, START + 16)

        @block.tensor
        def _(pe):
            pe_mixer(pe)
            if stages >= 2:
                pe_experts0(pe)
            if stages >= 3:
                pe_recurrence(pe)
            if stages >= 4:
                pe_attention1(pe)
                pe_experts1(pe)

        @block.scalar
        def _(act):
            act_mixer(act)
            if stages >= 2:
                act_experts0(act)
            if stages >= 3:
                act_recurrence(act)
            if stages >= 4:
                act_attention1(act)
                act_experts1(act)

        @block.vector
        def _(dve):
            dve_mixer(dve)
            if stages >= 2:
                dve_experts0(dve)
            if stages >= 3:
                dve_recurrence(dve)
            if stages >= 4:
                dve_attention1(dve)
                dve_experts1(dve)

        @block.gpsimd
        def _(pool):
            for semaphore in semaphores:
                pool.sem_inc(semaphore, START)
            pool_mixer(pool)
            if stages >= 2:
                pool_experts0(pool)
            if stages >= 3:
                pool_recurrence(pool)
            if stages >= 4:
                pool_attention1(pool)
                pool_experts1(pool)


def layout(I):

    import numpy as np

    bf = mybir.dt.np(BF16)

    def tokens(a):
        return np.ascontiguousarray(a.reshape(NT, P, D).transpose(1, 0, 2).reshape(P, T))

    L = {"x": tokens(I["x"]), "ctx": I["ctx_1024"]}
    L["ctxT"] = np.ascontiguousarray(I["ctx_1024"].reshape(T, D).T)
    L["ident"] = np.eye(P, dtype=np.float32)
    L["ident_bf"] = np.eye(P, dtype=bf)
    gates = [I["L0_xattn_igate_w"], I["L0_xattn_fgate_w"]]
    gw = np.zeros((P, 3, 2, 32), np.float32)
    for n, w in enumerate(gates):
        gw[:, :, n, :H0] = w.reshape(H0, 3, D).transpose(2, 1, 0)
    L["gw"] = gw.reshape(P, 192)
    gb = np.zeros((4, 32, 2), np.float32)
    gb[:, :H0, 0] = I["L0_xattn_igate_b"]
    gb[:, :H0, 1] = I["L0_xattn_fgate_b"]
    L["gb"] = gb.reshape(P, 2)
    L["outw"] = I["L0_xattn_out_w"].reshape(1, D)
    L["headmask0"] = (np.repeat(np.eye(H0), DH0, axis=0) * DH0 ** -0.5).astype(np.float32)
    later = np.where(np.arange(S)[:, None] > np.arange(S)[None, :], NEVER, 0.0)
    L["causalT"] = np.tile(later, (2, W // S)).astype(bf)
    L["causal"] = np.tile(later.T, (2, W // S)).astype(bf)
    lhs9 = np.ones((9, 2, 2, H0 // 2, 2, S))
    lhs9[3:6, :, :, :, 1] = 0
    lhs9[6:9, :, :, :, 0] = 0
    L["lhs9"] = lhs9.reshape(9, -1).astype(bf)
    L["rhs9"] = np.ones((9, 2 * W), bf)
    L["wr"] = I["L0_ffn_router_w"].T
    gate_up = I["L0_ffn_gate_up_proj"].transpose(1, 0, 2)
    L["wexp"] = np.concatenate([gate_up, I["L0_ffn_down_proj"].transpose(1, 0, 2)], axis=2).reshape(P, -1)
    L["vg"], L["vu"] = I["L0_ffn_shared_gate_w"].T, I["L0_ffn_shared_up_w"].T
    L["vd"] = I["L0_ffn_shared_down_w"].T.reshape(SF // P, P, D).transpose(1, 0, 2)
    L["prio"] = np.tile(np.arange(E0, 0, -1, dtype=np.float32), (P, 1))
    L["before"] = np.triu(np.ones((P, P)), 1).astype(bf)
    L["keep0"] = np.tile((np.arange(NT) > 0).astype(np.float32), (P, E0))
    L["whole"] = np.tile(P * np.arange(NT, dtype=np.float32), (P, 1))
    L["count0"] = np.tile(np.arange(NS0 + 4, dtype=np.float32), (P, 1))
    order = lambda w: np.concatenate([w[0:2 * D], w[3 * D:], w[2 * D:3 * D]])
    L["ctx_tok"] = I["ctx_1024"].reshape(NT, P, D).transpose(1, 0, 2)
    L["Wf"], L["Wh"] = I["L1_xattn_Wf"], I["L1_xattn_Wh"]
    L["b_att"] = I["L1_xattn_b_att"].reshape(D, 1)
    L["vrow"] = np.zeros((P, 2 * B - 2), np.float32)
    L["vrow"][:, B - 2:B] = I["L1_xattn_v"][:, None]
    w_in = order(I["L1_xattn_W_ih0"]).T
    L["wx"] = np.stack([w_in[:D], w_in[D:], order(I["L1_xattn_W_hh0"]).T], axis=1)
    L["W2"] = np.stack([order(I["L1_xattn_W_ih1"]).T, order(I["L1_xattn_W_hh1"]).T], axis=1)
    L["b1c"] = np.stack([order(I[f"L1_xattn_b_{k}0"]).reshape(4, D) for k in ("ih", "hh")], axis=1)
    L["b2c"] = np.stack([order(I[f"L1_xattn_b_{k}1"]).reshape(4, D).T for k in ("ih", "hh")], axis=1)
    gsel = np.zeros((P, 4, B))
    for row in (0, 32, 64):
        gsel[row:row + 4] = np.eye(4)[:, :, None]
    L["gsel"] = gsel.astype(bf)
    other = np.array([[0, 1], [1, 0]])
    L["own"] = np.concatenate([np.tile(np.eye(2), (1, B // 2)), np.repeat(other * NEVER, S, axis=1)],
                              axis=1).astype(bf)
    L["ones"] = np.ones((P, P), bf)
    L["wqkv"], L["wo"], L["gw1"] = I["L1_ffn_Wqkv"], I["L1_ffn_Wo"], I["L1_ffn_gate_W"]
    L["fc1"] = I["L1_ffn_fc1_w"].transpose(2, 0, 1)
    L["fc2"] = I["L1_ffn_fc2_w"].transpose(2, 0, 1).reshape(F1 // P, P, E1, D).transpose(1, 2, 0, 3)
    L["fc1b"] = I["L1_ffn_fc1_b"].reshape(E1, F1 // P, P).transpose(2, 0, 1)
    L["fc2b"] = I["L1_ffn_fc2_b"].T
    bqkv = I["L1_ffn_bqkv"].reshape(3, D)
    L["cols1"] = np.stack([I["L1_ffn_ln1_w"], I["L1_ffn_ln1_b"], I["L1_ffn_ln2_w"], I["L1_ffn_ln2_b"], bqkv[0],
                           bqkv[1], bqkv[2], bqkv[2]], axis=1)
    L["bo1"] = I["L1_ffn_bo"].reshape(1, D)
    L["headmask1"] = np.repeat(np.eye(H1, dtype=np.float32), DH1, axis=0)
    L["prio1"] = np.tile(np.arange(E1, 0, -1, dtype=np.float32), (P, 1))
    sel1 = np.zeros((3, E1, E1, P))
    sel1[:, np.arange(E1), np.arange(E1)] = 1
    L["sel1"] = np.concatenate([sel1.reshape(3 * E1, E1, P), np.zeros((P - 3 * E1, E1, P))])\
        .astype(bf)
    return L


def kernel(**inputs):
    import numpy as _np
    import concourse.bacc as _bacc
    from concourse.bass_utils import run_bass_kernel_spmd as _run

    nc = _bacc.Bacc("TRN2", target_bir_lowering=False, num_devices=1)
    arrays, args = {}, {}
    for name, a in layout({k: _np.asarray(v) for k, v in inputs.items()}).items():
        a = _np.ascontiguousarray(a)
        arrays[f"in_{name}"] = a
        args[name] = nc.dram_tensor(f"in_{name}", a.shape, mybir.dt.from_np(a.dtype), kind="ExternalInput").ap()
    out = nc.dram_tensor("out_0_dram", [P, T], F32, kind="ExternalOutput").ap()
    build(nc, args, out)
    r = _run(nc, [arrays], core_ids=[0])
    got = r.results[0]["out_0_dram"]
    return got.reshape(P, NT, D).transpose(1, 0, 2).reshape(B, S, D)
```
